# Optimizing a Trainium2 kernel written in Bass

```python
import numpy as np
import jax
import jax.numpy as jnp

def _softmax(x, axis=-1):
    return jax.nn.softmax(x, axis=axis)

def _gelu(x):
    return jax.nn.gelu(x, approximate=True)

def _silu(x):
    return jax.nn.silu(x)

def _sigmoid(x):
    return jax.nn.sigmoid(x)

def _layernorm(x, axis=-1, eps=1e-05):
    m = jnp.mean(x, axis=axis, keepdims=True)
    v = jnp.var(x, axis=axis, keepdims=True)
    return (x - m) / jnp.sqrt(v + eps)

def _scatter_add(tgt, idx, src, axis=0):
    return tgt.at[idx].add(src)

def _segment_sum(src, seg, n):
    return jax.ops.segment_sum(src, seg, n)
kernel_name = 'mk_xattn_ffn_d1_seqx_r4_72ed70'

def setup_inputs(seed: int=0):
    np.random.seed(seed)
    _w = jnp.asarray

    def _rec_inputs():
        import jax
        import jax.numpy as jnp
        _rk = jax.random.key(seed)
        x = -0.0002928 + 1 * jax.random.normal(jax.random.fold_in(_rk, 1), (2, 1024, 256), jnp.float32)
        _lenS = 1024 - jax.random.randint(jax.random.fold_in(_rk, 7), (2,), 0, max(1, 1024 // 4) + 1, jnp.int32)
        _lenS2 = 154 - jax.random.randint(jax.random.fold_in(_rk, 8), (2,), 0, max(1, 154 // 4) + 1, jnp.int32)
        _ctx_1024P = jax.random.normal(jax.random.fold_in(_rk, 11), (2, 16, 256), jnp.float32)
        _ctx_1024c = jax.random.dirichlet(jax.random.fold_in(_rk, 511), 0.3 * jnp.ones((16,), jnp.float32), (2, 154))
        _ctx_1024t = jnp.einsum('bsk,bkd->bsd', _ctx_1024c, _ctx_1024P)
        _ctx_1024t = _ctx_1024t * jax.lax.rsqrt(jnp.mean(jnp.square(_ctx_1024t)) + 1e-12) * 0.953939
        ctx_1024 = -1.39393e-06 + 0.999914 * (_ctx_1024t + 0.3 * jax.random.normal(jax.random.fold_in(_rk, 611), (2, 154, 256), jnp.float32))
        return (x, ctx_1024)
    x, ctx_1024 = _rec_inputs()

    def _L0_xattn_setup():
        import jax, jax.numpy as jnp
        import numpy as np
        import math
        EMBED = 256
        HEADS = 16
        HEAD_DIM = EMBED // HEADS

        def alibi_slopes(heads: int) -> jnp.ndarray:
            return jnp.asarray([2.0 ** (-8.0 * (h + 1) / heads) for h in range(heads)], dtype=jnp.float32)
        key = jax.random.key(seed)
        ks = jax.random.split(key, 8)
        B, Nq, Nk = (2, 512, 512)
        s = 0.02
        return {'query': jax.random.normal(ks[0], (B, Nq, EMBED), jnp.float32), 'kv': jax.random.normal(ks[1], (B, Nk, EMBED), jnp.float32), 'Wq': jax.random.normal(ks[2], (EMBED, EMBED), jnp.float32) * s, 'bq': jnp.zeros((EMBED,), jnp.float32), 'Wkv': jax.random.normal(ks[3], (EMBED, 2 * EMBED), jnp.float32) * s, 'bkv': jnp.zeros((2 * EMBED,), jnp.float32), 'Wo': jax.random.normal(ks[4], (EMBED, EMBED), jnp.float32) * s, 'bo': jnp.zeros((EMBED,), jnp.float32)}
    _L0_xattn_all = _L0_xattn_setup()
    _L0_xattn_in = {k: v for k, v in _L0_xattn_all.items() if k in ('Wq', 'bq', 'Wkv', 'bkv', 'Wo', 'bo')}
    del _L0_xattn_all

    def _L0_ffn_setup():
        import jax, jax.numpy as jnp
        import numpy as np
        N_EMBED = 256
        FFN_HIDDEN = 1024
        NUM_EXPERTS = 8
        TOP_K = 2
        key = jax.random.key(seed)
        ks = jax.random.split(key, 8)
        d, f, E = (N_EMBED, FFN_HIDDEN, NUM_EXPERTS)
        s_d = 1.0 / np.sqrt(d)
        s_f = 1.0 / np.sqrt(f)
        return {'x': jax.random.normal(ks[0], (2, 512, d), dtype=jnp.float32), 'Wg': jax.random.uniform(ks[1], (d, E), jnp.float32, -s_d, s_d), 'bg': jax.random.uniform(ks[2], (E,), jnp.float32, -s_d, s_d), 'W1': jax.random.uniform(ks[3], (E, d, f), jnp.float32, -s_d, s_d), 'b1': jax.random.uniform(ks[4], (E, f), jnp.float32, -s_d, s_d), 'W2': jax.random.uniform(ks[5], (E, f, d), jnp.float32, -s_f, s_f), 'b2': jax.random.uniform(ks[6], (E, d), jnp.float32, -s_f, s_f)}
    _L0_ffn_all = _L0_ffn_setup()
    _L0_ffn_in = {k: v for k, v in _L0_ffn_all.items() if k in ('Wg', 'bg', 'W1', 'b1', 'W2', 'b2')}
    del _L0_ffn_all
    return {'x': x, 'ctx_1024': ctx_1024, 'L0_xattn_Wq': _L0_xattn_in['Wq'], 'L0_xattn_bq': _L0_xattn_in['bq'], 'L0_xattn_Wkv': _L0_xattn_in['Wkv'], 'L0_xattn_bkv': _L0_xattn_in['bkv'], 'L0_xattn_Wo': _L0_xattn_in['Wo'], 'L0_xattn_bo': _L0_xattn_in['bo'], 'L0_ffn_Wg': _L0_ffn_in['Wg'], 'L0_ffn_bg': _L0_ffn_in['bg'], 'L0_ffn_W1': _L0_ffn_in['W1'], 'L0_ffn_b1': _L0_ffn_in['b1'], 'L0_ffn_W2': _L0_ffn_in['W2'], 'L0_ffn_b2': _L0_ffn_in['b2']}

def reference(x, ctx_1024, L0_xattn_Wq, L0_xattn_bq, L0_xattn_Wkv, L0_xattn_bkv, L0_xattn_Wo, L0_xattn_bo, L0_ffn_Wg, L0_ffn_bg, L0_ffn_W1, L0_ffn_b1, L0_ffn_W2, L0_ffn_b2):
    import jax
    import jax.numpy as jnp

    def _L0_xattn_ref(query, kv, Wq, bq, Wkv, bkv, Wo, bo):
        import jax, jax.numpy as jnp
        import numpy as np
        import math
        EMBED = 256
        HEADS = 16
        HEAD_DIM = EMBED // HEADS

        def alibi_slopes(heads: int) -> jnp.ndarray:
            return jnp.asarray([2.0 ** (-8.0 * (h + 1) / heads) for h in range(heads)], dtype=jnp.float32)
        B, Nq, E = query.shape
        Nk = kv.shape[1]
        H, D = (HEADS, HEAD_DIM)
        q = query @ Wq + bq
        kvp = kv @ Wkv + bkv
        k, v = jnp.split(kvp, 2, axis=-1)
        q = q.reshape(B, Nq, H, D).transpose(0, 2, 1, 3)
        k = k.reshape(B, Nk, H, D).transpose(0, 2, 1, 3)
        v = v.reshape(B, Nk, H, D).transpose(0, 2, 1, 3)
        slopes = alibi_slopes(H)
        rel = jnp.abs(jnp.arange(Nk)[None, :] - jnp.arange(Nq)[:, None] - (Nk - Nq))
        bias = -slopes[:, None, None] * rel.astype(jnp.float32)
        scale = 1.0 / math.sqrt(D)
        scores = jnp.einsum('bhqd,bhkd->bhqk', q, k) * scale + bias[None]
        attn = jax.nn.softmax(scores, axis=-1)
        out = jnp.einsum('bhqk,bhkd->bhqd', attn, v)
        out = out.transpose(0, 2, 1, 3).reshape(B, Nq, E)
        return out @ Wo + bo

    def _L0_ffn_ref(x, Wg, bg, W1, b1, W2, b2):
        import jax, jax.numpy as jnp
        import numpy as np
        N_EMBED = 256
        FFN_HIDDEN = 1024
        NUM_EXPERTS = 8
        TOP_K = 2
        gate_scores = jax.nn.softmax(x @ Wg + bg, axis=-1)
        topk_scores, topk_idx = jax.lax.top_k(gate_scores, TOP_K)
        topk_scores = topk_scores / (jnp.sum(topk_scores, axis=-1, keepdims=True) + 1e-08)
        onehot = jax.nn.one_hot(topk_idx, NUM_EXPERTS, dtype=x.dtype)
        combine_w = jnp.einsum('bsk,bske->bse', topk_scores, onehot)
        output = jnp.zeros_like(x)
        for e in range(NUM_EXPERTS):
            h = jax.nn.gelu(x @ W1[e] + b1[e])
            y = h @ W2[e] + b2[e]
            output = output + y * combine_w[..., e:e + 1]
        return output
    x = x + _L0_xattn_ref(_layernorm(x, axis=-1), ctx_1024, L0_xattn_Wq, L0_xattn_bq, L0_xattn_Wkv, L0_xattn_bkv, L0_xattn_Wo, L0_xattn_bo)
    x = x + _L0_ffn_ref(_layernorm(x, axis=-1), L0_ffn_Wg, L0_ffn_bg, L0_ffn_W1, L0_ffn_b1, L0_ffn_W2, L0_ffn_b2)
    return x

_drawn_inputs = setup_inputs


def setup_inputs(seed=0):
    import zlib

    import numpy as np

    out = dict(_drawn_inputs(seed))
    spreads = {'L0_xattn_bq': (0.0, 0.8), 'L0_xattn_bkv': (0.0, 0.1), 'L0_xattn_bo': (0.0, 0.1)}
    factors = {'L0_xattn_Wq': 8.0, 'L0_ffn_b1': 6.217, 'L0_ffn_b2': 4.362}
    for name, (base, spread) in spreads.items():
        noise = np.random.default_rng([zlib.crc32(name.encode()), seed]).standard_normal(out[name].shape)
        drawn = base * np.exp(spread * noise) if base else spread * noise
        out[name] = jnp.asarray(drawn.astype(out[name].dtype))
    for name, factor in factors.items():
        out[name] = (out[name] * factor).astype(out[name].dtype)
    return out
```

```python
import math
from contextlib import ExitStack

import numpy as np

import concourse.bass as bass
from concourse import mybir

P = 128
B, NQ, NK, D = 2, 1024, 154, 256
H, DH = 16, 16
E, F = 8, 1024
NT = B * NQ // P
DC = D // P
HG = 4
G = H // HG
GK = HG * NK
PAIR = 2 * NK
FLAT = H * NK
NC = -(-FLAT // P)
NU = NC // 4
DV = DH + 1
FC = F // P
LIST = B * NQ + P
NBLK = (2 * B * NQ - E) // P + E
SPARE = NBLK - 2 * B * NQ // P
XROWS = E * LIST + SPARE * P
ROW = 2 * D + 8
BIASES = 2 + HG + 4
UNITS = E * 4
EPS = 1e-5
KINK = NQ - NK

SX, SW = 2.0**8, 2.0**8
SCALE = 1 / math.sqrt(DH)
SQ, SK = 2.0**6 * SCALE, 2.0**8
SCTX = 2.0**6
S_SCORE = 2.0**14
S_ROW = 2.0**6
S_P, S_V, S_H = 2.0**8, 2.0**8, 2.0**6
SLOPES = [2.0 ** (-8.0 * (h + 1) / H) for h in range(H)]

C_ID, C_KINK, C_MASK = 0, P, P + 2 * NK
C_SLOPE = C_MASK + 2 * NC
C_IOTA = C_SLOPE + G
C_BLK = C_IOTA + E
C_HALF = C_BLK + NBLK
C_MINUS = C_HALF + 1
C_SW = C_MINUS + 1
C_ROW = C_SW + 1
C_KPOS = C_ROW + HG
C_END = C_KPOS + NK
H_ID, H_TRI, H_ONE = 0, P, 2 * P
H_ROW, H_BV, H_BASE, H_END = 3 * P, 4 * P, 5 * P, 5 * P + E


def group_of_unit(v):
    return (min(4 * P * (v + 1), FLAT) - 1) // GK


def constants():
    c = np.zeros((P, C_END), np.float32)
    c[:, C_ID:C_ID + P] = np.eye(P)
    k = np.arange(NK)
    for n in range(2):
        u = np.maximum((NQ // P - 2 + n) * P + np.arange(P) - KINK, 0)
        c[:, C_KINK + n * NK:C_KINK + (n + 1) * NK] = np.minimum(k[None, :], u[:, None])
    for ch in range(NC):
        f = ch * P + np.arange(P)
        h = f // NK
        first = ch * P // NK
        c[:, C_MASK + 2 * ch] = (h == first) & (f < FLAT)
        c[:, C_MASK + 2 * ch + 1] = (h == first + 1) & (f < FLAT)
    for j in range(HG):
        for g in range(G):
            c[32 * j + DH, C_SLOPE + g] = -SLOPES[HG * g + j] * S_ROW
        c[32 * j + DH, C_ROW + j] = 1.0
    c[:, C_KPOS:C_KPOS + NK] = k
    c[:, C_IOTA:C_IOTA + E] = np.arange(E)
    c[:, C_BLK:C_BLK + NBLK] = np.arange(NBLK)
    c[:, C_HALF] = -0.5
    c[:, C_MINUS] = -1.0
    c[:, C_SW] = SW
    h = np.zeros((P, H_END), np.float16)
    h[:, H_ID:H_ID + P] = np.eye(P)
    h[:, H_TRI:H_TRI + P] = np.triu(np.ones((P, P)), 1)
    h[:, H_ONE:H_ONE + P] = 1.0
    h[0, H_BV:H_BV + P] = 2.0**7
    h[0, H_BASE:H_BASE + E] = np.arange(E) * LIST
    for j in range(HG):
        h[0, H_ROW + 32 * j + DH] = S_SCORE / S_ROW * (SX * SW / SQ) / 2.0**7
    ids = np.zeros((P, NT + 1), np.int32)
    for i in range(NT):
        ids[:, i] = (i % B) * NQ + (i // B) * P + np.arange(P)
    ids[:, NT] = 2 * B * NQ + np.arange(P)
    return c, h, ids


def program(nc, x, ctx_in, wq, bq, wkv, bkv, wo, bo, wg, bg, w1, b1, w2, b2, c32_in, c16_in, ids_in, out):
    f32, f16, i32, u32 = mybir.dt.float32, mybir.dt.float16, mybir.dt.int32, mybir.dt.uint32
    ALU = mybir.AluOpType
    ACT = mybir.ActivationFunctionType
    AX = mybir.AxisListType
    ds = bass.ds
    xlist = nc.dram_tensor("xlist", [XROWS, ROW // 2], i32, kind="Internal").ap()
    out_rows = out.rearrange("b n d -> (b n) d")
    x_rows = x.rearrange("b n d -> (b n) d")

    with ExitStack() as ctx:
        def sb(name, shape, dt):
            return ctx.enter_context(nc.sbuf_tensor(name, shape, dt))

        def sem(name):
            return ctx.enter_context(nc.semaphore(name))

        c32 = sb("c32", [P, C_END], f32)
        c16 = sb("c16", [P, H_END], f16)
        ids = sb("ids", [P, NT + 1], i32)
        wts = sb("wts", [P, E, 4, 2048], f16)
        stage = sb("stage", [P, 2, 1024], f32)
        b1T = sb("b1T", [P, E * FC], f32)
        pad_rows = sb("pad_rows", [P, ROW], f16)
        sched_f = sb("sched_f", [P, 3, NBLK + 1], f32)
        sched_i = sb("sched_i", [1, 2, NBLK + 1], i32)
        cnt_f = sb("cnt_f", [P, 6, E], f32)
        cnt_i = sb("cnt_i", [P, 3, E], i32)
        ident = c32[:, C_ID:C_ID + P]
        ident16 = c16[:, H_ID:H_ID + P]
        tri16 = c16[:, H_TRI:H_TRI + P]
        one16 = c16[:, H_ONE:H_ONE + P]

        kbd = sb("kbd", [P, 2, B, G, GK], f16)
        after_k = kbd[:].rearrange("p a b g k -> p (a b g k)").bitcast(f32)
        b2bc = after_k[:, 0:E * D]
        block_rows = [after_k[:, E * D + n * ROW // 2:E * D + (n + 1) * ROW // 2] for n in range(4)]
        xt = [b.bitcast(f16)[:, 0:2 * D] for b in block_rows]
        pay = [b[:, D:ROW // 2] for b in block_rows]
        probs = sb("probs", [P, NC * P], f32)
        h32 = [probs[:, n * F:(n + 1) * F] for n in range(2)]
        pt = sb("pt", [P, NU, 2, 512], f16)
        hh = [pt[:].rearrange("p u s k -> p (u s k)")[:, n * 2 * F:(n + 1) * 2 * F].rearrange("p (s k) -> p s k", s=2)
              for n in range(2)]
        qs = sb("qs", [P, 2, 2, G * P], f16)
        xa = sb("xa", [P, 2, D], f32)
        xb = sb("xb", [P, 2, D], f32)
        wos = sb("wos", [P, 2, DC, D], f16)
        wgs = sb("wgs", [P, 2, DC, E], f16)
        kbias = sb("kbias", [P, G], f32)
        fold = sb("fold", [P, G], f32)
        bo_bc = sb("bo_bc", [P, D], f32)
        bg_bc = sb("bg_bc", [P, E], f32)
        o32 = sb("o32", [P, D], f32)
        xn2 = sb("xn2", [P, D], f32)
        rows = sb("rows", [P, 2, ROW], f16)
        oT = sb("oT", [P, 2, D], f16)
        x2T = sb("x2T", [P, 4 * P], f16)
        small = sb("small", [P, 8], f32)
        mx = sb("mx", [P, G, HG], f32)
        nb = sb("nb", [P, G, HG], f32)
        rec = sb("rec", [P, H], f32)
        lg = sb("lg", [P, E], f32)
        m8 = sb("m8", [P, E], f32)
        e8 = sb("e8", [P, E], f32)
        mi = sb("mi", [P, E], u32)
        oh = sb("oh", [P, 2, E], f32)
        ohr = sb("ohr", [P, 2, E], f32)
        pos = sb("pos", [P, 2, 2], i32)
        sel = sb("sel", [P, E], f16)
        cum = sb("cum", [P, 2, E], f16)
        st1, mv1, rs1 = sb("st1", [P, 6], f32), sb("mv1", [P, 2], f32), sb("rs1", [P, 2], f32)
        st2, mv2, rs2 = sb("st2", [P, 6], f32), sb("mv2", [P, 2], f32), sb("rs2", [P, 2], f32)
        xT = [qs[:, n, 0, :] for n in range(2)]
        ysb = [o32, xn2]
        wsel = sb("wsel", [P, 2, 2], f32)

        at = [0, 0]

        def borrow(e, words16):
            n = e - (E - 2)
            at[n] += words16
            assert at[n] <= 8192
            return wts[:, e, :, :].rearrange("p a k -> p (a k)")[:, at[n] - words16:at[n]]

        def scratch(words16):
            return borrow(E - 2, words16)

        def late(words16):
            return borrow(E - 1, words16)

        wqa = late(2 * DC * H * 32).rearrange("p (s c h d) -> p s c h d", s=2, c=DC, h=H)
        xn = late(2 * D).bitcast(f32)
        xnT = late(2 * D).rearrange("p (s d) -> p s d", s=2)
        late(1024)
        vs = late(2 * B * NC * 2 * DV).rearrange("p (s b c h d) -> p s b c h d", s=2, b=B, c=NC, h=2)

        wka = scratch(2 * DC * 512).rearrange("p (s c h d) -> p s c h d", s=2, c=DC, h=H)
        wva = scratch(2 * DC * D).rearrange("p (s c d) -> p s c d", s=2, c=DC)
        ctxT = scratch(2 * DC * B * PAIR).rearrange("p (s c b k) -> p s c b k", s=2, c=DC, b=B)
        v32 = scratch(NC * 32 * 2).bitcast(f32)
        bvr = scratch(2 * D)
        bvf = scratch(2 * D).bitcast(f32)
        raw = pt[:].rearrange("p u s k -> p (u s k)").bitcast(f32)
        wq_raw = raw[:, 0:512].rearrange("p (c n) -> p c n", c=DC)
        wkv_raw = raw[:, 512:1536].rearrange("p (c n) -> p c n", c=DC)
        wo_raw = raw[:, 1536:2048].rearrange("p (c n) -> p c n", c=DC)
        wg_raw = raw[:, 2048:2064].rearrange("p (c n) -> p c n", c=DC)
        ctx_main = probs[:, 0:512].rearrange("p (b d) -> p b d", b=B)
        ctx_tail = probs[0:NK - P, 512:1024].rearrange("p (b d) -> p b d", b=B)
        b1_raw = probs[0:E * FC, 1024:1024 + P]
        bk_bc, bq_bc, prod = (probs[:, 1152 + n * D:1152 + (n + 1) * D] for n in range(3))
        k32 = [probs[:, 1920 + n * NK:1920 + (n + 1) * NK] for n in range(2)]

        ps = ctx.enter_context(nc.psum_tensor("ps", [P, 8, 512], f32))
        score_ps = [ps[:, 2 * n:2 * n + 2, :] for n in range(2)]
        pt_ps, o_ps, misc = [ps[:, 4, :], ps[:, 7, :]], ps[:, 5, :], ps[:, 6, :]
        k_bank = [misc, ps[:, 7, :]]
        misc16 = ps[:, 6, :].bitcast(f16)
        h_ps = [[ps[:, 2 * n + m, :] for m in range(2)] for n in range(2)]
        y_ps = [ps[:, 4, 0:D], ps[:, 5, 0:D]]
        xT_ps = [ps[:, 6, :].bitcast(f16)[:, 0:512], ps[:, 7, :].bitcast(f16)[:, 0:512]]

        S = {n: sem(n) for n in """c_in ctx_in w_in bias_in z_bias z_pad z_cum z_kbd z_set padid x_in0 x_in1 xb_in0 xb_in1 list_init
            ctxT_ps k_ps k_aff k_hi k_lo k_row k_fold v_ps v_mask v_hi v_done b1T_ps b1T_done wsplit_hi wsplit
            w_stage0 w_stage1 w_scaled w_hi w_lo0 w_lo1 apart
            st1_d mv1_d ve1_d rstd1 xn_done xnT_ps xnT_hi xnT_lo q_ps q_hi q_lo
            s_ps kink mx_d nb_d p_done t_ps pt_hi pt_lo m_done rec_d o_norm oT_ps oT_hi oT_lo pr_ps xb_bo x2_done x2_out0 x2_out1
            st2_d mv2_d ve2_d rstd2 xn2_done xs_hi xs_lo x2T_ps x2T_done lg_ps lg_d m8_d mi_d nm_d e8_d oh_d sel_d
            cum_d rk_ps ohr_d pos_d gates tail_d scat0 scat1
            cnt_ps sched sched_done n_done pads b2_in
            xt_in0 xt_in1 xt_in2 xt_in3 xT_ps_d xT_done h_ps_d h_done hh_hi hh_lo y_ps_d yb_d wa_d wb_d y_done added""".split()}
        s = type("Sems", (), S)

        def wait(eng, semaphore, value):
            if not isinstance(value, int) or value > 0:
                eng.wait_ge(semaphore, value)

        def wait_alone(eng, semaphore, value):
            if not isinstance(value, int):
                eng.wait_ge(semaphore, value).then_inc(s.apart, 1)
            elif value > 0:
                eng.wait_ge(semaphore, value)

        def per_tile(i, par, each):
            return each * (i // 2) if isinstance(i, int) else each // 2 * (i - par)

        def turns(turn, loop):
            for i in range(-3, 5):
                turn(i, i % 2)
            with loop(5, 11, 2) as i:
                turn(i, 1)
                turn(i + 1, 0)
            for i in range(11, NT + 3):
                turn(i, i % 2)

        def tile(t):
            return t if not isinstance(t, int) or 0 <= t < NT else None

        def stages(i):
            return [tile(i + n) for n in (3, 2, 1, 0, -1, -2, -3)]

        def upto(t):
            return min(max(t + 1, 0), NT) if isinstance(t, int) else t + 1

        def first_row(i, par):
            return (i % B) * NQ + (i // B) * P if isinstance(i, int) else par * NQ + (i - par) * (P // B)

        def weight_units(i):
            if not isinstance(i, int):
                return []
            return {-3: range(0, 4), -2: range(4, 8), -1: range(8, 12), 14: range(28, 30), 16: range(30, 32)}.get(
                i, range(12 + 2 * i, 14 + 2 * i) if 0 <= i < 5 else range(2 * i, 2 * i + 2) if 11 <= i < 14 else [])

        def units_at(i, slot):
            units = list(weight_units(i))
            return units[slot:slot + 1] if len(units) > 2 else units[slot // 2:slot // 2 + 1] if slot in (1, 3) else []

        def by_pool(u):
            return u >= 12 and u % 2 == 1

        def unit_place(u, lo):
            return wts[:, u // 4, (u % 4) // 2 * 2 + lo, (u % 2) * 1024:(u % 2 + 1) * 1024]

        def per_block(t, slot):
            return 16 * (t // 4) if isinstance(t, int) else 4 * (t - slot)

        def blocks(step, loop, first):
            for t in range(first, 3):
                step(t, t % 4)
            with loop(3, NBLK - 7, 4) as t:
                for n in range(4):
                    step(t + n, (3 + n) % 4)
            for t in range(NBLK - 4, NBLK):
                step(t, t % 4)

        block = ctx.enter_context(nc.Block())

        @block.sync
        def _(sp):
            sp.dma_start(c32[:], c32_in).then_inc(s.c_in, 16)
            sp.dma_start(ctx_main, ctx_in[:, 0:P, :].rearrange("b k d -> k b d")).then_inc(s.ctx_in, 16)
            sp.dma_start(ctx_tail, ctx_in[:, P:NK, :].rearrange("b k d -> k b d")).then_inc(s.ctx_in, 16)
            sp.dma_start(c16[:], c16_in).then_inc(s.c_in, 16)
            sp.dma_start(ids[:], ids_in).then_inc(s.c_in, 16)
            sp.dma_start(wkv_raw, wkv.rearrange("(c p) n -> p c n", p=P)).then_inc(s.w_in, 16)
            sp.dma_start(wq_raw, wq.rearrange("(c p) n -> p c n", p=P)).then_inc(s.w_in, 16)
            sp.dma_start(wo_raw, wo.rearrange("(c p) n -> p c n", p=P)).then_inc(s.w_in, 16)
            sp.dma_start(wg_raw, wg.rearrange("(c p) n -> p c n", p=P)).then_inc(s.w_in, 16)
            sp.dma_start(bvf[0:1, :], bkv[D:2 * D].rearrange("(o n) -> o n", o=1)).then_inc(s.bias_in, 16)
            sp.dma_start(b1_raw, b1.rearrange("e (c p) -> (e c) p", p=P)).then_inc(s.bias_in, 16)
            sp.wait_ge(s.z_bias, 1)
            with nc.allow_non_contiguous_dma(reason="bias columns"):
                for j in range(HG):
                    part = slice(32 * j, 32 * j + DH)
                    sp.dma_start(kbias[part, :], bkv[0:D].rearrange("(g j d) -> j d g", j=HG, d=DH)[j]).then_inc(s.bias_in, 16)
            sp.dma_start(bq_bc, bq.rearrange("(o n) -> o n", o=1).to_broadcast([P, D])).then_inc(s.bias_in, 16)
            sp.dma_start(bk_bc, bkv[0:D].rearrange("(o n) -> o n", o=1).to_broadcast([P, D])).then_inc(s.bias_in, 16)
            sp.dma_start(bo_bc[:], bo.rearrange("(o n) -> o n", o=1).to_broadcast([P, D])).then_inc(s.bias_in, 16)
            sp.dma_start(bg_bc[:], bg.rearrange("(o n) -> o n", o=1).to_broadcast([P, E])).then_inc(s.bias_in, 16)

            def load_a(i, par):
                wait_alone(sp, s.xn_done, i - 1)
                sp.dma_start(xa[:, par, :], x_rows[ds(first_row(i, par), P), :]).then_inc(S[f"x_in{par}"], 16)

            def store(i, par):
                wait_alone(sp, s.x2_done, i + 1)
                sp.dma_start(out_rows[ds(first_row(i, par), P), :], xb[:, par, :]).then_inc(S[f"x2_out{par}"], 16)

            def load_b(i, par):
                wait_alone(sp, s.xn2_done, i - 1)
                wait_alone(sp, S[f"x2_out{par}"], per_tile(i, par, 16))
                sp.dma_start(xb[:, par, :], x_rows[ds(first_row(i, par), P), :]).then_inc(S[f"xb_in{par}"], 16)

            def load_w(u):
                e, n = u // 4, u % 2
                wait(sp, S[f"w_lo{n}"], u // 2)
                if u % 4 < 2:
                    sp.dma_start(stage[:, n, :], w1[e, n * P:(n + 1) * P, :]).then_inc(S[f"w_stage{n}"], 16)
                else:
                    sp.dma_start(stage[:, n, :].rearrange("p (c d) -> p c d", c=4),
                                 w2[e].rearrange("(c p) d -> p c d", p=P)[:, 4 * n:4 * n + 4, :]).then_inc(S[f"w_stage{n}"], 16)

            load_a(0, 0)
            load_w(0)
            load_w(1)
            sp.wait_ge(s.padid, 1)
            for n in range(SPARE):
                sp.dma_start(xlist[E * LIST + n * P:E * LIST + (n + 1) * P, :], pad_rows[:].bitcast(i32)).then_inc(s.list_init, 16)

            def turn(i, par):
                f1, f2, sc, mt, b1, b2, b3 = stages(i)
                if isinstance(i, int) and i == 11:
                    for u in weight_units(i):
                        load_w(u)
                if tile(i + 4) is not None:
                    load_a(i + 4, par)
                if b2 is not None:
                    store(b2, par)
                if mt is not None:
                    load_b(mt, par)
                if isinstance(i, int):
                    for u in ([2, 3] if i == -3 else []) + list(weight_units(i + 1) if i != 10 else []):
                        load_w(u)

            turns(turn, sp.Fori)
            sp.wait_ge(s.scat0, 16 * NT)
            sp.wait_ge(s.scat1, 16 * NT)
            sp.wait_ge(s.list_init, 16 * SPARE)
            sp.wait_ge(s.n_done, 1)
            for e in range(E):
                n = sp.value_load(cnt_i[0:1, 0, e:e + 1], min_val=0, max_val=B * NQ)
                sp.dma_start(xlist[ds(n + e * LIST, P), :], pad_rows[:].bitcast(i32)).then_inc(s.pads, 16)
            sp.wait_ge(s.pads, 16 * E)
            sp.wait_ge(s.sched_done, 1)

            def load_block(t, slot):
                r = sp.value_load(sched_i[0:1, 0, ds(t, 1)], min_val=0, max_val=XROWS - P)
                wait_alone(sp, s.added, 16 * (t - 3))
                sp.dma_start(block_rows[slot].bitcast(i32), xlist[ds(r, P), :]).then_inc(S[f"xt_in{slot}"], 16)

            blocks(lambda t, slot: load_block(t + 4, slot) if not isinstance(t, int) or t + 4 < NBLK else None, sp.Fori, -4)
            sp.wait_ge(s.added, 16 * NBLK)

        @block.gpsimd
        def _(pool):
            pool.memset(kbias[:], 0.0).then_inc(s.z_bias, 1)
            pool.memset(pad_rows[:], 0.0).then_inc(s.z_pad, 1)
            pool.memset(cum[:], 0.0).then_inc(s.z_cum, 1)
            pool.wait_ge(s.c_in, 48)
            pool.wait_ge(s.z_pad, 1)
            pool.tensor_copy(pad_rows[:, 2 * D:2 * D + 2].bitcast(i32), ids[:, NT:NT + 1]).then_inc(s.padid, 1)

            def rstd(i, rs, done, ve_sem):
                pool.wait_ge(ve_sem, i + 1)
                pool.tensor_tensor(rs[:, 1:2], rs[:, 0:1], c32[:, C_HALF:C_HALF + 1], ALU.pow).then_inc(done, 1)

            def scale_w(u):
                pool.wait_ge(s.w_stage1, 16 * (u // 2 + 1))
                pool.tensor_tensor(stage[:, 1, :], stage[:, 1, :], c32[:, C_SW:C_SW + 1].to_broadcast([P, 1024]), ALU.mult).then_inc(s.w_scaled, 1)

            def split_w_lo(u):
                pool.wait_ge(s.w_hi, u + 1)
                pool.tensor_tensor(unit_place(u, 1), stage[:, 1, :], unit_place(u, 0), ALU.subtract).then_inc(s.w_lo1, 1)

            def weights_of(i, q):
                words = rows[:, q, 2 * D:ROW]
                z, zsum = e8[:, 1:2], small[:, 1:2]
                wait_alone(pool, s.e8_d, i + 1)
                pool.tensor_scalar(small[:, 2:3], zsum, 1e-8, 1.0, ALU.mult, ALU.add).then_inc(s.gates, 1)
                pool.wait_ge(s.gates, 4 * i + 1)
                pool.tensor_tensor(small[:, 3:4], small[:, 2:3], z, ALU.add).then_inc(s.gates, 1)
                pool.wait_ge(s.gates, 4 * i + 2)
                pool.tensor_tensor(small[:, 4:5], small[:, 3:4], c32[:, C_MINUS:C_MINUS + 1], ALU.pow).then_inc(s.gates, 1)
                pool.wait_ge(s.gates, 4 * i + 3)
                pool.tensor_tensor(words[:, 6:8].bitcast(f32), small[:, 4:5], z, ALU.mult).then_inc(s.gates, 1)
                pool.tensor_copy(words[:, 2:4].bitcast(f32), mi[:, 0:1]).then_inc(s.tail_d, 1)
                pool.tensor_copy(words[:, 0:2].bitcast(i32), ids[:, ds(i, 1)]).then_inc(s.tail_d, 1)
                pool.wait_ge(s.gates, 4 * i + 4)
                pool.tensor_tensor(words[:, 4:6].bitcast(f32), small[:, 4:5], words[:, 6:8].bitcast(f32), ALU.subtract).then_inc(s.tail_d, 1)

            def dispatch(i, q):
                wait_alone(pool, s.xs_lo, i + 1)
                wait_alone(pool, s.tail_d, 3 * (i + 1))
                wait_alone(pool, s.pos_d, i + 1)
                for c in range(2):
                    pool.indirect_dma_start(
                        out=xlist, out_offset=bass.IndirectOffsetOnAxis(ap=pos[:, q, c:c + 1], axis=0),
                        in_=rows[:, q, :].bitcast(i32), in_offset=None).then_inc(S[f"scat{q}"], 16)

            def turn(i, par):
                f1, f2, sc, mt, b1, b2, b3 = stages(i)
                units = [u for u in weight_units(i) if by_pool(u)]
                if b2 is not None:
                    rstd(b2, rs2, s.rstd2, s.ve2_d)
                if b1 is not None:
                    pool.wait_ge(S[f"xb_in{1 - par}"], per_tile(b1, 1 - par, 16) + 16)
                    pool.tensor_tensor(xb[:, 1 - par, :], xb[:, 1 - par, :], bo_bc[:], ALU.add).then_inc(s.xb_bo, 1)
                for u in units:
                    scale_w(u)
                if b3 is not None:
                    weights_of(b3, 1 - par)
                if f1 is not None:
                    rstd(f1, rs1, s.rstd1, s.ve1_d)
                if b2 is not None:
                    pool.wait_ge(s.xs_hi, b2 + 1)
                    pool.tensor_tensor(rows[:, par, D:2 * D], xn2[:], rows[:, par, 0:D], ALU.subtract).then_inc(s.xs_lo, 1)
                for u in units:
                    split_w_lo(u)
                if b3 is not None:
                    dispatch(b3, 1 - par)

            pool.wait_ge(s.bias_in, 16 * BIASES)
            turns(turn, pool.Fori)
            pool.wait_ge(s.s_ps, G * NT)
            for e in range(E):
                pool.dma_start(b2bc[:, e * D:(e + 1) * D], b2[e:e + 1, :].to_broadcast([P, D])).then_inc(s.b2_in, 16)
            pool.wait_ge(s.x2_out0, 8 * NT)
            pool.wait_ge(s.x2_out1, 8 * NT)

            def add_block(t, slot):
                wait_alone(pool, s.y_done, t + 1)
                wait_alone(pool, s.added, 16 * t)
                pool.indirect_dma_start(
                    out=out_rows, out_offset=bass.IndirectOffsetOnAxis(ap=pay[slot][:, 0:1].bitcast(i32), axis=0),
                    in_=ysb[slot % 2][:], in_offset=None, bounds_check=B * NQ - 1, oob_is_err=False,
                    compute_op=ALU.add).then_inc(s.added, 16)

            blocks(add_block, pool.Fori, 0)
            pool.wait_ge(s.added, 16 * NBLK)

        @block.scalar
        def _(act):
            act.wait_ge(s.z_kbd, 1)
            for b in range(B):
                for g in range(G):
                    n = b * G + g
                    act.wait_ge(s.k_row, n + 1)
                    for j in range(HG):
                        part = slice(32 * j, 32 * j + 32)
                        last = nc.scalar.copy(kbd[part, 0, b, g, j * NK:(j + 1) * NK], k32[n % 2][part, :])
                    last.then_inc(s.k_hi, 1)

            def split_w_hi(u):
                if by_pool(u):
                    act.wait_ge(s.w_scaled, (u - 12) // 2 + 1)
                else:
                    act.wait_ge(S[f"w_stage{u % 2}"], 16 * (u // 2 + 1))
                if u == UNITS - 4:
                    act.wait_ge(s.q_ps, NT)
                if u == UNITS - 2:
                    act.wait_ge(s.m_done, NU * NT)
                nc.scalar.activation(unit_place(u, 0), stage[:, u % 2, :], ACT.Copy, scale=1.0 if by_pool(u) else SW).then_inc(s.w_hi, 1)

            def pt_hi(i, v, par):
                act.wait_ge(s.t_ps, i * NU + v + 1)
                wait(act, s.m_done, (i - 1) * NU + v + 1)
                nc.scalar.copy(pt[:, v, 0, :], pt_ps[(v + par) % 2]).then_inc(s.pt_hi, 1)

            def exps(i, g):
                act.wait_ge(s.nb_d, i * G + g + 1)
                wait(act, s.t_ps, (i - 1) * NU + min((g + 1) * GK - 1, FLAT - 1) // 512 + 1)
                for j in range(HG):
                    last = nc.scalar.activation(probs[:, (g * HG + j) * NK:(g * HG + j + 1) * NK],
                                                score_ps[g % 2][:, j // 2, (j % 2) * NK:(j % 2 + 1) * NK],
                                                ACT.Exp, bias=nb[:, g, j:j + 1], scale=1.0 / S_SCORE)
                last.then_inc(s.p_done, 1)

            def turn(i, par):
                f1, f2, sc, mt, b1, b2, b3 = stages(i)
                if b3 is not None:
                    act.wait_ge(s.x2T_ps, b3 + 1)
                    act.wait_ge(s.x2_done, upto(i - 2))
                    nc.scalar.copy(x2T[:], misc16[:, 2 * D:4 * D]).then_inc(s.x2T_done, 1)
                for slot in range(5):
                    for u in units_at(i, slot):
                        split_w_hi(u)
                    if f2 is not None and slot == 4:
                        act.wait_ge(s.q_ps, f2 + 1)
                        nc.scalar.activation(qs[:, par, 0, :], misc, ACT.Copy, scale=SQ / (SX * SW)).then_inc(s.q_hi, 1)
                    if mt is not None:
                        pt_hi(mt, slot, par)
                    if sc is not None and slot > 0:
                        exps(sc, slot - 1)
                    if b1 is not None and slot == 2:
                        act.wait_ge(s.oT_ps, b1 + 1)
                        wait(act, s.pr_ps, b1)
                        nc.scalar.copy(oT[:, 0, :], misc[:, 0:D]).then_inc(s.oT_hi, 1)
                    if b3 is not None and slot == 2:
                        act.wait_ge(s.nm_d, b3 + 1)
                        wait(act, s.tail_d, 3 * b3)
                        nc.scalar.activation(e8[:], m8[:], ACT.Exp, bias=small[:, 0:1], accum_out=small[:, 1:2]).then_inc(s.e8_d, 1)
                    if f2 is not None and slot == 3:
                        act.wait_ge(s.xnT_ps, f2 + 1)
                        wait(act, s.q_ps, f2)
                        nc.scalar.copy(xnT[:, 0, :], misc[:, 0:D]).then_inc(s.xnT_hi, 1)
                    if b2 is not None and slot == 3:
                        act.wait_ge(s.xn2_done, b2 + 1)
                        wait(act, S[f"scat{par}"], per_tile(b2, par, 32))
                        nc.scalar.copy(rows[:, par, 0:D], xn2[:]).then_inc(s.xs_hi, 1)

            turns(turn, act.Fori)

            act.wait_ge(s.sched_done, 1)
            act.wait_ge(s.b1T_done, 1)
            act.wait_ge(s.o_norm, NT)

            def copy_rows(t, par):
                act.wait_ge(s.xT_ps_d, t + 1)
                wait(act, s.h_ps_d, 2 * (t - 1))
                nc.scalar.copy(xT[par], xT_ps[par]).then_inc(s.xT_done, 1)

            def gelu_block(t, par):
                e = act.value_load(sched_i[0:1, 1, ds(t, 1)], min_val=0, max_val=E - 1)
                for m in range(2):
                    act.wait_ge(s.h_ps_d, 2 * t + m + 1)
                    wait(act, s.hh_lo, 2 * (t - 1))
                    for f in range(4):
                        c = 4 * m + f
                        last = nc.scalar.activation(h32[par][:, c * P:(c + 1) * P], h_ps[par][m][:, f * P:(f + 1) * P],
                                                    ACT.Gelu_apprx_tanh, bias=b1T[:, ds(e * FC + c, 1)], scale=1.0 / (SX * SW))
                    last.then_inc(s.h_done, 1)

            def step(t, slot):
                if not isinstance(t, int) or t + 2 < NBLK:
                    copy_rows(t + 2, slot % 2)
                if not isinstance(t, int) or 0 <= t + 1 < NBLK:
                    gelu_block(t + 1, 1 - slot % 2)

            blocks(step, act.Fori, -2)

        @block.vector
        def _(dve):
            def split(dst, src, scale, inc=None):
                dve.tensor_scalar(dst(0), src, scale, None, ALU.mult).then_inc(s.wsplit_hi, 1)
                count[0] += 1
                dve.wait_ge(s.wsplit_hi, count[0])
                dve.scalar_tensor_tensor(out=dst(1), in0=src, scalar=scale, in1=dst(0), op0=ALU.mult,
                                         op1=ALU.subtract).then_inc(s.wsplit, 1)

            count = [0]
            dve.memset(kbd[:].bitcast(u32), 0).then_inc(s.z_kbd, 1)
            dve.memset(wka.bitcast(u32), 0).then_inc(s.z_set, 1)
            dve.memset(wqa.bitcast(u32), 0).then_inc(s.z_set, 1)
            dve.memset(probs[:, FLAT:NC * P], 0.0).then_inc(s.z_set, 1)
            dve.wait_ge(s.z_set, 3)
            dve.wait_ge(s.w_in, 64)
            for c in range(DC):
                split(lambda w: wka[:, w, c, :, 0:DH], wkv_raw[:, c, 0:D].rearrange("p (h d) -> p h d", h=H), SW)
            for c in range(DC):
                split(lambda w: wva[:, w, c, :], wkv_raw[:, c, D:2 * D], SW)
            dve.wait_ge(s.ctxT_ps, 1)
            for c in range(DC):
                for b in range(B):
                    src = ps[:, 2 * c + b, 0:NK].unsqueeze(1).to_broadcast([P, 2, NK])
                    split(lambda w: ctxT[:, w, c, b, :].rearrange("p (r k) -> p r k", r=2), src, SCTX)
            dve.wait_ge(s.bias_in, 16 * BIASES)
            for n in range(DC + 1):
                src = wkv_raw[:, n, 0:D] if n < DC else bk_bc
                dve.tensor_tensor(prod, src, bq_bc, ALU.mult).then_inc(s.k_fold, 1)
                dve.wait_ge(s.k_fold, 2 * n + 1)
                dve.tensor_reduce(rec[:], prod.rearrange("p (h d) -> p h d", h=H), AX.X, ALU.add).then_inc(s.k_fold, 1)
                dve.wait_ge(s.k_fold, 2 * n + 2)
                if n < DC:
                    split(lambda w: wka[:, w, n, :, DH], rec[:], S_ROW * SCALE * SW / SK)
                    dve.wait_ge(s.wsplit, count[0])
            dve.tensor_tensor(prod[:, 0:H].rearrange("p (g j) -> p g j", g=G), rec[:].rearrange("p (g j) -> p g j", g=G),
                              c32[:, C_ROW:C_ROW + HG].unsqueeze(1).to_broadcast([P, G, HG]), ALU.mult).then_inc(s.k_fold, 1)
            dve.wait_ge(s.k_fold, 2 * DC + 3)
            dve.tensor_reduce(fold[:], prod[:, 0:H].rearrange("p (g j) -> p g j", g=G), AX.X, ALU.add).then_inc(s.k_fold, 1)
            dve.wait_ge(s.z_bias, 1)
            dve.tensor_scalar(kbias[:], kbias[:], SK, None, ALU.mult).then_inc(s.k_fold, 1)
            dve.wait_ge(s.k_fold, 2 * DC + 5)
            dve.scalar_tensor_tensor(out=kbias[:], in0=fold[:], scalar=S_ROW * SCALE, in1=kbias[:], op0=ALU.mult,
                                     op1=ALU.add).then_inc(s.k_fold, 1)
            split(lambda w: bvr[0:1, w * D:(w + 1) * D], bvf[0:1, :], 2.0**7)
            for c in range(DC):
                split(lambda w: wqa[:, w, c, :, 0:DH], wq_raw[:, c, :].rearrange("p (h d) -> p h d", h=H), SW)
            split(lambda w: wos[:, w, :, :], wo_raw, SW)
            split(lambda w: wgs[:, w, :, :], wg_raw, SW)
            dve.wait_ge(s.b1T_ps, 1)
            dve.tensor_copy(b1T[:], o_ps[:, 0:E * FC]).then_inc(s.b1T_done, 1)

            dve.wait_ge(s.k_fold, 2 * DC + 6)

            def k_affine(n):
                b, g = n // G, n % G
                dve.wait_ge(s.k_ps, n + 1)
                wait(dve, s.k_lo, n - 1)
                wait(dve, s.k_hi, n - 1)
                dve.tensor_scalar(k32[n % 2], k_bank[n % 2][:, 0:NK], SK / (SCTX * SW), kbias[:, g:g + 1], ALU.mult, ALU.add).then_inc(s.k_aff, 1)
                dve.wait_ge(s.k_aff, n + 1)
                dve.scalar_tensor_tensor(out=k32[n % 2], in0=c32[:, C_KPOS:C_KPOS + NK], scalar=c32[:, C_SLOPE + g:C_SLOPE + g + 1],
                                         in1=k32[n % 2], op0=ALU.mult, op1=ALU.add).then_inc(s.k_row, 1)

            def k_low(n):
                b, g = n // G, n % G
                dve.wait_ge(s.k_hi, n + 1)
                for j in range(HG):
                    part, cols = slice(32 * j, 32 * j + 32), slice(j * NK, (j + 1) * NK)
                    last = dve.tensor_tensor(kbd[part, 1, b, g, cols], k32[n % 2][part, :], kbd[part, 0, b, g, cols], ALU.subtract)
                last.then_inc(s.k_lo, 1)

            for n in range(B * G + 1):
                if n < B * G:
                    k_affine(n)
                if n > 0:
                    k_low(n - 1)
            mask = c32[:, C_MASK:C_MASK + 2 * NC].rearrange("p (c m) -> p c m", m=2)
            dve.tensor_copy(vs[:, 0, :, :, :, DH], mask.unsqueeze(1).to_broadcast([P, B, NC, 2]))
            dve.memset(vs[:, 1, :, :, :, DH], 0.0)
            for b in range(B):
                dve.wait_ge(s.v_ps, b + 1)
                for m in range(2):
                    half = ps[:, 2 * m, 0:(NC // 2) * 32].rearrange("p (c h d) -> p c h d", h=2, d=DH)
                    chunks = slice(m * (NC // 2), (m + 1) * (NC // 2))
                    vm = v32.rearrange("p (c h d) -> p c h d", h=2, d=DH)[:, chunks]
                    n = 2 * b + m
                    dve.tensor_scalar(vm, half, S_V / (SCTX * SW), None, ALU.mult).then_inc(s.v_mask, 1)
                    dve.wait_ge(s.v_mask, 2 * n + 1)
                    dve.tensor_tensor(vm, vm, mask[:, chunks].unsqueeze(3).to_broadcast([P, NC // 2, 2, DH]), ALU.mult).then_inc(s.v_mask, 1)
                    dve.wait_ge(s.v_mask, 2 * n + 2)
                    dve.tensor_copy(vs[:, 0, b, chunks, :, 0:DH], vm).then_inc(s.v_hi, 1)
                    dve.wait_ge(s.v_hi, n + 1)
                    dve.tensor_tensor(vs[:, 1, b, chunks, :, 0:DH], vm, vs[:, 0, b, chunks, :, 0:DH], ALU.subtract).then_inc(s.v_done, 1)

            def pt_lo(i, v, par):
                dve.wait_ge(s.pt_hi, i * NU + v + 1)
                dve.tensor_tensor(pt[:, v, 1, :], pt_ps[(v + par) % 2], pt[:, v, 0, :], ALU.subtract).then_inc(s.pt_lo, 1)

            def split_w_lo(i, slot):
                for u in units_at(i, slot):
                    if not by_pool(u):
                        dve.wait_ge(s.w_hi, u + 1)
                        dve.scalar_tensor_tensor(out=unit_place(u, 1), in0=stage[:, u % 2, :], scalar=SW, in1=unit_place(u, 0),
                                                 op0=ALU.mult, op1=ALU.subtract).then_inc(S[f"w_lo{u % 2}"], 1)

            def maxima(i, g):
                two_banks = score_ps[g % 2]
                dve.wait_ge(s.s_ps, i * G + g + 1)
                if isinstance(i, int) and i >= NT - 4:
                    tail = i // 2 - (NT // 2 - 2)
                    for j in range(HG):
                        cols = two_banks[:, j // 2, (j % 2) * NK:(j % 2 + 1) * NK]
                        dve.scalar_tensor_tensor(out=cols, in0=c32[:, C_KINK + tail * NK:C_KINK + (tail + 1) * NK],
                                                 scalar=2.0 * SLOPES[g * HG + j] * S_SCORE, in1=cols,
                                                 op0=ALU.mult, op1=ALU.add).then_inc(s.kink, 1)
                    dve.wait_ge(s.kink, ((i - (NT - 4)) * G + g + 1) * HG)
                dve.tensor_reduce(mx[:, g, :], two_banks[:, :, 0:PAIR].rearrange("p a (j k) -> p a j k", j=2), AX.X, ALU.max).then_inc(s.mx_d, 1)

            def exp_bias(i, g):
                dve.wait_ge(s.mx_d, i * G + g + 1)
                dve.tensor_scalar(nb[:, g, :], mx[:, g, :], -1.0 / S_SCORE, math.log(S_P), ALU.mult, ALU.add).then_inc(s.nb_d, 1)

            def turn(i, par):
                f1, f2, sc, mt, b1, b2, b3 = stages(i)
                p1, p2 = 1 - par, par
                if b2 is not None:
                    dve.wait_ge(s.pr_ps, b2 + 1)
                    dve.wait_ge(s.xb_bo, b2 + 1)
                    dve.scalar_tensor_tensor(out=xb[:, p2, :], in0=misc[:, 0:D], scalar=1.0 / (S_V * SW), in1=xb[:, p2, :],
                                             op0=ALU.mult, op1=ALU.add).then_inc(s.x2_done, 1)
                if mt is not None:
                    pt_lo(mt, 0, par)
                if b2 is not None:
                    dve.wait_ge(s.x2_done, b2 + 1)
                    dve.bn_stats(st2[:], xb[:, p2, :]).then_inc(s.st2_d, 1)
                if sc is not None:
                    maxima(sc, 0)
                if b2 is not None:
                    wait_alone(dve, s.st2_d, b2 + 1)
                    dve.bn_aggr(mv2[:], st2[:]).then_inc(s.mv2_d, 1)
                if sc is not None:
                    exp_bias(sc, 0)
                if b2 is not None:
                    dve.wait_ge(s.mv2_d, b2 + 1)
                    dve.tensor_scalar(rs2[:, 0:1], mv2[:, 1:2], EPS, 1.0 / (SX * SX), ALU.add, ALU.mult).then_inc(s.ve2_d, 1)
                if b3 is not None:
                    dve.wait_ge(s.lg_ps, b3 + 1)
                    dve.scalar_tensor_tensor(out=lg[:], in0=misc[:, 0:E], scalar=1.0 / (SX * SW), in1=bg_bc[:], op0=ALU.mult,
                                             op1=ALU.add).then_inc(s.lg_d, 1)
                if b1 is not None:
                    dve.wait_ge(s.m_done, NU * (b1 + 1))
                    ov = o_ps[:, 0:H * DV].rearrange("p (h d) -> p h d", h=H)
                    dve.reciprocal(rec[:], ov[:, :, DH]).then_inc(s.rec_d, 1)
                if b3 is not None:
                    wait_alone(dve, s.lg_d, b3 + 1)
                    wait_alone(dve, s.e8_d, b3)
                    dve.max(m8[:], lg[:]).then_inc(s.m8_d, 1)
                if b1 is not None:
                    dve.wait_ge(s.rec_d, b1 + 1)
                    wait(dve, s.oT_ps, b1)
                    dve.tensor_tensor(o32[:].rearrange("p (h d) -> p h d", h=H), ov[:, :, 0:DH],
                                      rec[:].unsqueeze(2).to_broadcast([P, H, DH]), ALU.mult).then_inc(s.o_norm, 1)
                split_w_lo(i, 0)
                if b3 is not None:
                    wait_alone(dve, s.m8_d, b3 + 1)
                    wait_alone(dve, s.tail_d, 3 * b3)
                    dve.max_index(mi[:], m8[:], lg[:]).then_inc(s.mi_d, 1)
                    dve.tensor_scalar(small[:, 0:1], m8[:, 0:1], -1.0, None, ALU.mult).then_inc(s.nm_d, 1)
                if mt is not None:
                    pt_lo(mt, 1, par)
                if b3 is not None:
                    dve.wait_ge(s.mi_d, b3 + 1)
                    dve.tensor_tensor(oh[:], c32[:, C_IOTA:C_IOTA + E].unsqueeze(1).to_broadcast([P, 2, E]),
                                      mi[:, 0:2].unsqueeze(2).to_broadcast([P, 2, E]), ALU.is_equal).then_inc(s.oh_d, 1)
                if sc is not None:
                    maxima(sc, 1)
                if b3 is not None:
                    dve.wait_ge(s.oh_d, b3 + 1)
                    wait(dve, s.rk_ps, b3)
                    dve.tensor_tensor(sel[:], oh[:, 0, :], oh[:, 1, :], ALU.add).then_inc(s.sel_d, 1)
                if sc is not None:
                    exp_bias(sc, 1)
                if b3 is not None:
                    dve.wait_ge(s.sel_d, b3 + 1)
                    dve.tensor_tensor(cum[:, p2, :], cum[:, p1, :], sel[:], ALU.add).then_inc(s.cum_d, 1)
                split_w_lo(i, 1)
                if b1 is not None:
                    dve.wait_ge(s.oT_hi, b1 + 1)
                    dve.tensor_tensor(oT[:, 1, :], misc[:, 0:D], oT[:, 0, :], ALU.subtract).then_inc(s.oT_lo, 1)
                if b2 is not None:
                    dve.wait_ge(s.rstd2, b2 + 1)
                    wait(dve, s.xs_lo, b2)
                    dve.tensor_scalar(xn2[:], xb[:, p2, :], mv2[:, 0:1], rs2[:, 1:2], ALU.subtract, ALU.mult).then_inc(s.xn2_done, 1)
                if mt is not None:
                    pt_lo(mt, 2, par)
                if f1 is not None:
                    dve.wait_ge(S[f"x_in{p1}"], per_tile(f1, p1, 16) + 16)
                    dve.bn_stats(st1[:], xa[:, p1, :]).then_inc(s.st1_d, 1)
                if sc is not None:
                    maxima(sc, 2)
                if f1 is not None:
                    wait_alone(dve, s.st1_d, f1 + 1)
                    dve.bn_aggr(mv1[:], st1[:]).then_inc(s.mv1_d, 1)
                if sc is not None:
                    exp_bias(sc, 2)
                split_w_lo(i, 2)
                if f1 is not None:
                    dve.wait_ge(s.mv1_d, f1 + 1)
                    dve.tensor_scalar(rs1[:, 0:1], mv1[:, 1:2], EPS, 1.0 / (SX * SX), ALU.add, ALU.mult).then_inc(s.ve1_d, 1)
                if f2 is not None:
                    dve.wait_ge(s.xnT_hi, f2 + 1)
                    dve.tensor_tensor(xnT[:, 1, :], misc[:, 0:D], xnT[:, 0, :], ALU.subtract).then_inc(s.xnT_lo, 1)
                if b3 is not None:
                    dve.wait_ge(s.rk_ps, b3 + 1)
                    dve.wait_ge(s.xnT_hi, upto(i + 2))
                    dve.tensor_tensor(ohr[:], oh[:], misc[:, D:D + E].unsqueeze(1).to_broadcast([P, 2, E]), ALU.mult).then_inc(s.ohr_d, 1)
                if mt is not None:
                    pt_lo(mt, 3, par)
                if b3 is not None:
                    dve.wait_ge(s.ohr_d, b3 + 1)
                    wait(dve, S[f"scat{p1}"], per_tile(b3, p1, 32))
                    with nc.allow_low_precision(reason="whole numbers below 2^24"):
                        dve.tensor_reduce(pos[:, p1, :], ohr[:], AX.X, ALU.add).then_inc(s.pos_d, 1)
                if sc is not None:
                    maxima(sc, 3)
                if f1 is not None:
                    dve.wait_ge(s.rstd1, f1 + 1)
                    wait(dve, s.xnT_ps, f1)
                    dve.tensor_scalar(xn, xa[:, p1, :], mv1[:, 0:1], rs1[:, 1:2], ALU.subtract, ALU.mult).then_inc(s.xn_done, 1)
                if sc is not None:
                    exp_bias(sc, 3)
                split_w_lo(i, 3)
                if f2 is not None:
                    dve.wait_ge(s.q_hi, f2 + 1)
                    dve.scalar_tensor_tensor(out=qs[:, par, 1, :], in0=misc, scalar=SQ / (SX * SW), in1=qs[:, par, 0, :],
                                             op0=ALU.mult, op1=ALU.subtract).then_inc(s.q_lo, 1)
                if mt is not None:
                    pt_lo(mt, 4, par)

            dve.wait_ge(s.z_cum, 1)
            turns(turn, dve.Fori)

            n_sched = [0]

            def then(ins):
                n_sched[0] += 1
                ins.then_inc(s.sched, 1)
                dve.wait_ge(s.sched, n_sched[0])

            dve.wait_ge(s.cnt_ps, 1)
            then(dve.tensor_copy(cnt_i[:, 0, :], misc[:, 0:E]))
            dve.tensor_scalar(cnt_f[:, 0, :], misc[:, 0:E], float(P - 1), None, ALU.add).then_inc(s.n_done, 1)
            dve.wait_ge(s.n_done, 1)
            then(dve.tensor_copy(cnt_i[:, 1, :], cnt_f[:, 0, :]))
            then(dve.tensor_single_scalar(cnt_i[:, 2, :], cnt_i[:, 1, :], 7, ALU.arith_shift_right))
            then(dve.tensor_copy(cnt_f[:, 1, :], cnt_i[:, 2, :]))
            src = 1
            for n, step in enumerate((1, 2, 4)):
                then(dve.tensor_copy(cnt_f[:, 2 + n, 0:step], cnt_f[:, src, 0:step]))
                then(dve.tensor_tensor(cnt_f[:, 2 + n, step:E], cnt_f[:, src, step:E], cnt_f[:, src, 0:E - step], ALU.add))
                src = 2 + n
            blk = c32[:, C_BLK:C_BLK + NBLK]
            before, expert, start = (sched_f[:, n, 0:NBLK] for n in range(3))
            for e in range(E):
                if e == 0:
                    then(dve.tensor_scalar(expert, blk, cnt_f[:, 4, e:e + 1], None, ALU.is_ge))
                    then(dve.tensor_scalar(start, expert, cnt_f[:, 1, e:e + 1], None, ALU.mult))
                else:
                    then(dve.tensor_scalar(before, blk, cnt_f[:, 4, e:e + 1], None, ALU.is_ge))
                    then(dve.tensor_tensor(expert, expert, before, ALU.add))
                    then(dve.scalar_tensor_tensor(out=start, in0=before, scalar=cnt_f[:, 1, e:e + 1], in1=start, op0=ALU.mult, op1=ALU.add))
            then(dve.tensor_tensor(before, blk, start, ALU.subtract))
            then(dve.tensor_scalar(before, before, float(P), None, ALU.mult))
            then(dve.scalar_tensor_tensor(out=start, in0=expert, scalar=float(LIST), in1=before, op0=ALU.mult, op1=ALU.add))
            then(dve.tensor_scalar(before, expert, float(E - 1), None, ALU.min))
            then(dve.tensor_copy(sched_i[0:1, 0, 0:NBLK], start[0:1, :]))
            dve.tensor_copy(sched_i[0:1, 1, 0:NBLK], before[0:1, :]).then_inc(s.sched_done, 1)
            dve.wait_ge(s.b2_in, 16 * E)

            def split_h(t, par):
                for m in range(2):
                    cols = slice(m * 512, (m + 1) * 512)
                    dve.wait_ge(s.h_done, 2 * t + m + 1)
                    wait(dve, s.y_ps_d, t - 1)
                    dve.tensor_scalar(hh[par][:, 0, cols], h32[par][:, cols], S_H, None, ALU.mult).then_inc(s.hh_hi, 1)
                    dve.wait_ge(s.hh_hi, 2 * t + m + 1)
                    dve.scalar_tensor_tensor(out=hh[par][:, 1, cols], in0=h32[par][:, cols], scalar=S_H, in1=hh[par][:, 0, cols],
                                             op0=ALU.mult, op1=ALU.subtract).then_inc(s.hh_lo, 1)

            def weigh(t, slot):
                e = dve.value_load(sched_i[0:1, 1, ds(t, 1)], min_val=0, max_val=E - 1)
                par = slot % 2
                dve.wait_ge(S[f"xt_in{slot}"], per_block(t, slot) + 16)
                wait(dve, s.y_done, t)
                dve.scalar_tensor_tensor(out=wsel[:, par, 0:1], in0=pay[slot][:, 1:2], scalar=sched_f[:, 1, ds(t, 1)],
                                         in1=pay[slot][:, 2:3], op0=ALU.is_equal, op1=ALU.mult).then_inc(s.wa_d, 1)
                dve.wait_ge(s.wa_d, t + 1)
                dve.tensor_tensor(wsel[:, par, 1:2], wsel[:, par, 0:1], pay[slot][:, 3:4], ALU.add).then_inc(s.wb_d, 1)
                dve.wait_ge(s.y_ps_d, t + 1)
                wait(dve, s.added, 16 * (t - 1))
                dve.scalar_tensor_tensor(out=ysb[par][:], in0=y_ps[par], scalar=1.0 / (S_H * SW), in1=b2bc[:, ds(e * D, D)],
                                         op0=ALU.mult, op1=ALU.add).then_inc(s.yb_d, 1)
                dve.wait_ge(s.yb_d, t + 1)
                dve.wait_ge(s.wb_d, t + 1)
                dve.tensor_scalar(ysb[par][:], ysb[par][:], wsel[:, par, 1:2], None, ALU.mult).then_inc(s.y_done, 1)

            def step(t, slot):
                if not isinstance(t, int) or 0 <= t + 1 < NBLK:
                    split_h(t + 1, 1 - slot % 2)
                if not isinstance(t, int) or t >= 0:
                    weigh(t, slot)

            blocks(step, dve.Fori, -1)

        @block.tensor
        def _(pe):
            def mm(out_, lhsT, rhs, start, stop, skip=False):
                return nc.tensor.matmul(out_, lhsT, rhs, start=start, stop=stop, skip_group_check=skip)

            THREE = ((0, 0), (0, 1), (1, 0))
            pe.wait_ge(s.c_in, 48)
            pe.wait_ge(s.ctx_in, 32)
            for c in range(DC):
                for b in range(B):
                    cols = slice(c * P, (c + 1) * P)
                    nc.tensor.transpose(ps[:, 2 * c + b, 0:P], ctx_main[:, b, cols], ident)
                    last = nc.tensor.transpose(ps[:, 2 * c + b, P:NK], ctx_tail[:, b, cols], ident[0:NK - P, 0:NK - P])
            last.then_inc(s.ctxT_ps, 1)
            pe.wait_ge(s.bias_in, 16 * BIASES)
            nc.tensor.transpose(o_ps[:, 0:E * FC], b1_raw, ident[0:E * FC, 0:E * FC]).then_inc(s.b1T_ps, 1)
            pe.wait_ge(s.wsplit, 10)
            for b in range(B):
                for g in range(G):
                    n = b * G + g
                    dst = k_bank[n % 2]
                    wait(pe, s.k_aff, n - 1)
                    for c in range(DC):
                        for a, z in THREE:
                            last = mm(dst[:, 0:NK], wka[:, a, c, g * HG:(g + 1) * HG, :].rearrange("p h d -> p (h d)"),
                                      ctxT[:, z, c, b, 0:NK], c == 0 and (a, z) == (0, 0), c == 1 and (a, z) == (1, 0))
                    last.then_inc(s.k_ps, 1)
            pe.wait_ge(s.wsplit, 11)
            for b in range(B):
                wait(pe, s.v_done, 2 * b)
                for ch in range(NC):
                    k0, h0 = ch * P % NK, ch * P // NK
                    o = (ch % (NC // 2)) * 32
                    bank = ps[:, 2 * (ch // (NC // 2)), :]
                    for o, w in ((o, 32),) if h0 + 1 < H else ((o, DH), (o + DH, DH)):
                        for c in range(DC):
                            for a, z in THREE:
                                mm(bank[:, o:o + w], ctxT[:, a, c, b, k0:k0 + P], wva[:, z, c, h0 * DH:h0 * DH + w],
                                   c == 0 and (a, z) == (0, 0), False)
                        for z in range(2):
                            last = mm(bank[:, o:o + w], c16[0:1, H_BV:H_BV + P],
                                      bvr[0:1, z * D + h0 * DH:z * D + h0 * DH + w], False, z == 1)
                last.then_inc(s.v_ps, 1)

            def transposes(i, v, par):
                pe.wait_ge(s.p_done, i * G + group_of_unit(v) + 1)
                wait(pe, s.pt_lo, i * NU + v - 1)
                for n in range(4):
                    c = 4 * v + n
                    last = nc.tensor.transpose(pt_ps[(v + par) % 2][:, n * P:(n + 1) * P], probs[:, c * P:(c + 1) * P], ident)
                last.then_inc(s.t_ps, 1)

            def scores(i, g, par):
                pe.wait_ge(s.q_lo, i + 1)
                wait(pe, s.p_done, i * G + g - 1)
                for n in range(2):
                    for a, z in THREE:
                        last = mm(score_ps[g % 2][:, n, 0:PAIR], qs[:, par, a, g * P:(g + 1) * P],
                                  kbd[:, z, par, g, n * PAIR:(n + 1) * PAIR], (a, z) == (0, 0), (a, z) == (1, 0))
                last.then_inc(s.s_ps, 1)

            def mix(i, v, par):
                pe.wait_ge(s.pt_lo, i * NU + v + 1)
                if v == 0:
                    wait(pe, s.o_norm, i)
                for n in range(4):
                    c = 4 * v + n
                    h0 = c * P // NK
                    two = (c * P + P - 1) // NK > h0 and h0 + 1 < H
                    w = 2 * DV if two else DV
                    for a, z in THREE:
                        last = mm(o_ps[:, h0 * DV:h0 * DV + w], pt[:, v, a, n * P:(n + 1) * P],
                                  vs[:, z, par, c, :, :].rearrange("p h d -> p (h d)")[:, 0:w],
                                  c == 0 and (a, z) == (0, 0), c == NC - 1 and (a, z) == (1, 0), True)
                last.then_inc(s.m_done, 1)

            def turn(i, par):
                f1, f2, sc, mt, b1, b2, b3 = stages(i)
                q = 1 - par
                if mt is not None:
                    transposes(mt, 0, par)
                if sc is not None:
                    scores(sc, 0, q)
                if b1 is not None:
                    mix(b1, NU - 1, q)
                wait(pe, s.x2_done, upto(i - 2))
                if isinstance(i, int):
                    wait(pe, s.q_lo, min(i + 2, NT))
                if b3 is not None:
                    pe.wait_ge(s.x2T_done, b3 + 1)
                    for c in range(DC):
                        for a, z in THREE:
                            last = mm(misc[:, 0:E], x2T[:, (2 * a + c) * P:(2 * a + c + 1) * P], wgs[:, z, c, :],
                                      c == 0 and (a, z) == (0, 0), c == 1 and (a, z) == (1, 0))
                    last.then_inc(s.lg_ps, 1)
                if mt is not None:
                    transposes(mt, 1, par)
                if sc is not None:
                    scores(sc, 1, q)
                if b1 is not None:
                    pe.wait_ge(s.o_norm, b1 + 1)
                    wait(pe, s.lg_d, b3 + 1 if b3 is not None else 0)
                    for c in range(DC):
                        last = nc.tensor.transpose(misc[:, c * P:(c + 1) * P], o32[:, c * P:(c + 1) * P], ident)
                    last.then_inc(s.oT_ps, 1)
                if mt is not None:
                    mix(mt, 0, par)
                if mt is not None:
                    transposes(mt, 2, par)
                if sc is not None:
                    scores(sc, 2, q)
                if b3 is not None:
                    pe.wait_ge(s.sel_d, b3 + 1)
                    wait(pe, s.cum_d, b3)
                    wait(pe, s.lg_d, b3 + 1)
                if b1 is not None:
                    pe.wait_ge(s.oT_lo, b1 + 1)
                if b3 is not None:
                    mm(misc[:, D:D + E], tri16, sel[:], True, False)
                    mm(misc[:, D:D + E], one16, cum[:, q, :], False, False)
                    mm(misc[:, D:D + E], one16[0:1, :], c16[0:1, H_BASE:H_BASE + E], False, True).then_inc(s.rk_ps, 1)
                if f2 is not None:
                    pe.wait_ge(s.xn_done, f2 + 1)
                    for c in range(DC):
                        last = nc.tensor.transpose(misc[:, c * P:(c + 1) * P], xn[:, c * P:(c + 1) * P], ident)
                    last.then_inc(s.xnT_ps, 1)
                if mt is not None:
                    mix(mt, 1, par)
                if mt is not None:
                    transposes(mt, 3, par)
                if sc is not None:
                    scores(sc, 3, q)
                if f2 is not None:
                    pe.wait_ge(s.xnT_lo, f2 + 1)
                    if b3 is not None:
                        pe.wait_ge(s.ohr_d, b3 + 1)
                    for g in range(G):
                        for c in range(DC):
                            for a, z in THREE:
                                mm(misc[:, g * P:(g + 1) * P],
                                   wqa[:, a, c, g * HG:(g + 1) * HG, :].rearrange("p h d -> p (h d)"),
                                   xnT[:, z, c * P:(c + 1) * P], c == 0 and (a, z) == (0, 0), False)
                        last = mm(misc[:, g * P:(g + 1) * P], c16[0:1, H_ROW:H_ROW + P], c16[0:1, H_BV:H_BV + P], False, True)
                    last.then_inc(s.q_ps, 1)
                if mt is not None:
                    mix(mt, 2, par)
                if mt is not None:
                    transposes(mt, 4, par)
                    mix(mt, 3, par)
                if b3 is not None:
                    wait(pe, s.ohr_d, b3 + 1)
                if b1 is not None or b2 is not None:
                    wait(pe, s.q_lo, upto(i + 2))
                if b2 is not None:
                    pe.wait_ge(s.xs_lo, b2 + 1)
                    for n in range(4):
                        last = nc.tensor.transpose(misc16[:, 2 * D + n * P:2 * D + (n + 1) * P], rows[:, par, n * P:(n + 1) * P], ident16)
                    last.then_inc(s.x2T_ps, 1)
                if b1 is not None:
                    pe.wait_ge(s.oT_lo, b1 + 1)
                    for c in range(DC):
                        for a, z in THREE:
                            last = mm(misc[:, 0:D], oT[:, a, c * P:(c + 1) * P], wos[:, z, c, :],
                                      c == 0 and (a, z) == (0, 0), c == 1 and (a, z) == (1, 0))
                    last.then_inc(s.pr_ps, 1)

            pe.wait_ge(s.wsplit, 15)
            pe.wait_ge(s.k_lo, B * G)
            pe.wait_ge(s.v_done, 2 * B)
            pe.wait_ge(s.b1T_done, 1)
            pe.wait_ge(s.z_cum, 1)
            turns(turn, pe.Fori)
            pe.wait_ge(s.cum_d, NT)
            mm(misc[:, 0:E], one16, cum[:, 0, :], True, True).then_inc(s.cnt_ps, 1)

            pe.wait_ge(s.sched_done, 1)

            def turn_rows(t, slot):
                pe.wait_ge(S[f"xt_in{slot}"], per_block(t, slot) + 16)
                wait(pe, s.xT_done, t - 1)
                for n in range(4):
                    last = nc.tensor.transpose(xT_ps[slot % 2][:, n * P:(n + 1) * P], xt[slot][:, n * P:(n + 1) * P], ident16)
                last.then_inc(s.xT_ps_d, 1)

            def up(t, par):
                e = pe.value_load(sched_i[0:1, 1, ds(t, 1)], min_val=0, max_val=E - 1)
                pe.wait_ge(s.xT_done, t + 1)
                wait(pe, s.h_done, 2 * (t - 1))
                w1v = wts[:].rearrange("p e a k -> p (e a k)")
                for m in range(2):
                    for f in range(4):
                        for c in range(DC):
                            for a, z in THREE:
                                off = a * 2048 + c * F + (4 * m + f) * P
                                last = mm(h_ps[par][m][:, f * P:(f + 1) * P], w1v[:, ds(e * 8192 + off, P)],
                                          xT[par][:, (2 * z + c) * P:(2 * z + c + 1) * P],
                                          c == 0 and (a, z) == (0, 0), c == 1 and (a, z) == (1, 0))
                    last.then_inc(s.h_ps_d, 1)

            def down(t, par):
                e = pe.value_load(sched_i[0:1, 1, ds(t, 1)], min_val=0, max_val=E - 1)
                wait(pe, s.yb_d, t - 1)
                w2v = wts[:].rearrange("p e a k -> p (e a k)")
                for c in range(FC):
                    if c % 4 == 0:
                        pe.wait_ge(s.hh_lo, 2 * t + c // 4 + 1)
                    for a, z in THREE:
                        last = mm(y_ps[par], hh[par][:, a, c * P:(c + 1) * P], w2v[:, ds(e * 8192 + (2 + z) * 2048 + c * D, D)],
                                  c == 0 and (a, z) == (0, 0), c == FC - 1 and (a, z) == (1, 0))
                last.then_inc(s.y_ps_d, 1)

            pe.wait_ge(s.w_lo0, UNITS // 2)
            pe.wait_ge(s.w_lo1, UNITS // 2)
            def step(t, slot):
                if not isinstance(t, int) or t + 2 < NBLK:
                    turn_rows(t + 2, (slot + 2) % 4)
                if not isinstance(t, int) or 0 <= t + 1 < NBLK:
                    up(t + 1, 1 - slot % 2)
                if not isinstance(t, int) or t >= 0:
                    down(t, slot % 2)

            blocks(step, pe.Fori, -2)


_NAMES = ["x", "ctx_1024", "L0_xattn_Wq", "L0_xattn_bq", "L0_xattn_Wkv", "L0_xattn_bkv", "L0_xattn_Wo", "L0_xattn_bo",
          "L0_ffn_Wg", "L0_ffn_bg", "L0_ffn_W1", "L0_ffn_b1", "L0_ffn_W2", "L0_ffn_b2"]


def kernel(**inputs):
    import concourse.bacc as bacc
    from concourse.bass_utils import run_bass_kernel_spmd

    nc = bacc.Bacc("TRN2", target_bir_lowering=False, num_devices=1)
    arrays, args = {}, []
    c32, c16, ids = constants()
    for name, a in [(n, np.ascontiguousarray(inputs[n])) for n in _NAMES] + [("c32", c32), ("c16", c16), ("ids", ids)]:
        arrays[f"in_{name}"] = a
        args.append(nc.dram_tensor(f"in_{name}", a.shape, mybir.dt.from_np(a.dtype), kind="ExternalInput").ap())
    args.append(nc.dram_tensor("out_0", (B, NQ, D), mybir.dt.float32, kind="ExternalOutput").ap())
    program(nc, *args)
    result = run_bass_kernel_spmd(nc, [arrays], core_ids=[0])
    return result.results[0]["out_0"]
```

```python
import math
from contextlib import ExitStack

import numpy as np

import concourse.bass as bass
from concourse import mybir

P = 128
B, NQ, NK, D = 2, 1024, 154, 256
H, DH = 16, 16
E, F = 8, 1024
NT = B * NQ // P
DC = D // P
HG = 4
G = H // HG
GK = HG * NK
PAIR = 2 * NK
FLAT = H * NK
NC = -(-FLAT // P)
NU = NC // 4
DV = DH + 1
FC = F // P
LIST = B * NQ + P
NBLK = (2 * B * NQ - E) // P + E
SPARE = NBLK - 2 * B * NQ // P
XROWS = E * LIST + SPARE * P
ROW = 2 * D + 8
BIASES = 2 + HG + 4
EARLY = 4
UNITS = E * 4
EPS = 1e-5
KINK = NQ - NK

SX, SW = 2.0**8, 2.0**8
SCALE = 1 / math.sqrt(DH)
SQ, SK = 2.0**6 * SCALE, 2.0**8
SCTX = 2.0**6
S_SCORE = 2.0**14
S_ROW = 2.0**6
S_P, S_V, S_H = 2.0**8, 2.0**8, 2.0**6
SLOPES = [2.0 ** (-8.0 * (h + 1) / H) for h in range(H)]

C_ID, C_KINK, C_MASK = 0, P, P + 2 * NK
C_SLOPE = C_MASK + 2 * NC
C_IOTA = C_SLOPE + G
C_BLK = C_IOTA + E
C_HALF = C_BLK + NBLK
C_MINUS = C_HALF + 1
C_SW = C_MINUS + 1
C_ROW = C_SW + 1
C_KPOS = C_ROW + HG
C_END = C_KPOS + NK
H_ID, H_TRI, H_ONE = 0, P, 2 * P
H_ROW, H_BV, H_BASE, H_END = 3 * P, 4 * P, 5 * P, 5 * P + E


def group_of_unit(v):
    return (min(4 * P * (v + 1), FLAT) - 1) // GK


def constants():
    c = np.zeros((P, C_END), np.float32)
    c[:, C_ID:C_ID + P] = np.eye(P)
    k = np.arange(NK)
    for n in range(2):
        u = np.maximum((NQ // P - 2 + n) * P + np.arange(P) - KINK, 0)
        c[:, C_KINK + n * NK:C_KINK + (n + 1) * NK] = np.minimum(k[None, :], u[:, None])
    for ch in range(NC):
        f = ch * P + np.arange(P)
        h = f // NK
        first = ch * P // NK
        c[:, C_MASK + 2 * ch] = (h == first) & (f < FLAT)
        c[:, C_MASK + 2 * ch + 1] = (h == first + 1) & (f < FLAT)
    for j in range(HG):
        for g in range(G):
            c[32 * j + DH, C_SLOPE + g] = -SLOPES[HG * g + j] * S_ROW
        c[32 * j + DH, C_ROW + j] = 1.0
    c[:, C_KPOS:C_KPOS + NK] = k
    c[:, C_IOTA:C_IOTA + E] = np.arange(E)
    c[:, C_BLK:C_BLK + NBLK] = np.arange(NBLK)
    c[:, C_HALF] = -0.5
    c[:, C_MINUS] = -1.0
    c[:, C_SW] = SW
    h = np.zeros((P, H_END), np.float16)
    h[:, H_ID:H_ID + P] = np.eye(P)
    h[:, H_TRI:H_TRI + P] = np.triu(np.ones((P, P)), 1)
    h[:, H_ONE:H_ONE + P] = 1.0
    h[0, H_BV:H_BV + P] = 2.0**7
    h[0, H_BASE:H_BASE + E] = np.arange(E) * LIST
    for j in range(HG):
        h[0, H_ROW + 32 * j + DH] = S_SCORE / S_ROW * (SX * SW / SQ) / 2.0**7
    ids = np.zeros((P, NT + 1), np.int32)
    for i in range(NT):
        ids[:, i] = (i % B) * NQ + (i // B) * P + np.arange(P)
    ids[:, NT] = 2 * B * NQ + np.arange(P)
    return c, h, ids


def program(nc, x, ctx_in, wq, bq, wkv, bkv, wo, bo, wg, bg, w1, b1, w2, b2, c32_in, c16_in, ids_in, out):
    f32, f16, i32, u32 = mybir.dt.float32, mybir.dt.float16, mybir.dt.int32, mybir.dt.uint32
    ALU = mybir.AluOpType
    ACT = mybir.ActivationFunctionType
    AX = mybir.AxisListType
    ds = bass.ds
    xlist = nc.dram_tensor("xlist", [XROWS, ROW // 2], i32, kind="Internal").ap()
    out_rows = out.rearrange("b n d -> (b n) d")
    x_rows = x.rearrange("b n d -> (b n) d")

    with ExitStack() as ctx:
        def sb(name, shape, dt):
            return ctx.enter_context(nc.sbuf_tensor(name, shape, dt))

        def sem(name):
            return ctx.enter_context(nc.semaphore(name))

        c32 = sb("c32", [P, C_END], f32)
        c16 = sb("c16", [P, H_END], f16)
        ids = sb("ids", [P, NT + 1], i32)
        wts = sb("wts", [P, E, 4, 2048], f16)
        stage = sb("stage", [P, 2, 1024], f32)
        b1T = sb("b1T", [P, E * FC], f32)
        pad_rows = sb("pad_rows", [P, ROW], f16)
        sched_f = sb("sched_f", [P, 3, NBLK + 1], f32)
        sched_i = sb("sched_i", [1, 2, NBLK + 1], i32)
        cnt_f = sb("cnt_f", [P, 6, E], f32)
        cnt_i = sb("cnt_i", [P, 3, E], i32)
        ident = c32[:, C_ID:C_ID + P]
        ident16 = c16[:, H_ID:H_ID + P]
        tri16 = c16[:, H_TRI:H_TRI + P]
        one16 = c16[:, H_ONE:H_ONE + P]

        kbd = sb("kbd", [P, 2, B, G, GK], f16)
        after_k = kbd[:].rearrange("p a b g k -> p (a b g k)").bitcast(f32)
        b2bc = after_k[:, 0:E * D]
        block_rows = [after_k[:, E * D + n * ROW // 2:E * D + (n + 1) * ROW // 2] for n in range(4)]
        xt = [b.bitcast(f16)[:, 0:2 * D] for b in block_rows]
        pay = [b[:, D:ROW // 2] for b in block_rows]
        probs = sb("probs", [P, NC * P], f32)
        h32 = [probs[:, n * F:(n + 1) * F] for n in range(2)]
        pt = sb("pt", [P, NU, 2, 512], f16)
        hh = [pt[:].rearrange("p u s k -> p (u s k)")[:, n * 2 * F:(n + 1) * 2 * F].rearrange("p (s k) -> p s k", s=2)
              for n in range(2)]
        qs = sb("qs", [P, 2, 2, G * P], f16)
        xa = sb("xa", [P, 2, D], f32)
        xb = sb("xb", [P, 2, D], f32)
        wos = sb("wos", [P, 2, DC, D], f16)
        wgs = sb("wgs", [P, 2, DC, E], f16)
        kbias = sb("kbias", [P, G], f32)
        fold = sb("fold", [P, G], f32)
        bo_bc = sb("bo_bc", [P, D], f32)
        bg_bc = sb("bg_bc", [P, E], f32)
        o32 = sb("o32", [P, D], f32)
        xn2 = sb("xn2", [P, D], f32)
        rows = sb("rows", [P, 2, ROW], f16)
        oT = sb("oT", [P, 2, D], f16)
        x2T = sb("x2T", [P, 4 * P], f16)
        small = sb("small", [P, 8], f32)
        mx = sb("mx", [P, G, HG], f32)
        nb = sb("nb", [P, G, HG], f32)
        rec = sb("rec", [P, H], f32)
        lg = sb("lg", [P, E], f32)
        m8 = sb("m8", [P, E], f32)
        e8 = sb("e8", [P, E], f32)
        mi = sb("mi", [P, E], u32)
        oh = sb("oh", [P, 2, E], f32)
        ohr = sb("ohr", [P, 2, E], f32)
        pos = sb("pos", [P, 2, 2], i32)
        sel = sb("sel", [P, E], f16)
        cum = sb("cum", [P, 2, E], f16)
        st1, mv1, rs1 = sb("st1", [P, 6], f32), sb("mv1", [P, 2], f32), sb("rs1", [P, 2], f32)
        st2, mv2, rs2 = sb("st2", [P, 6], f32), sb("mv2", [P, 2], f32), sb("rs2", [P, 2], f32)
        xT = [qs[:, n, 0, :] for n in range(2)]
        ysb = [o32, xn2]
        wsel = sb("wsel", [P, 4, 2], f32)
        row_id = sb("row_id", [P, 4], i32)

        at = [0, 0]

        def borrow(e, words16):
            n = e - (E - 2)
            at[n] += words16
            assert at[n] <= 8192
            return wts[:, e, :, :].rearrange("p a k -> p (a k)")[:, at[n] - words16:at[n]]

        def scratch(words16):
            return borrow(E - 2, words16)

        def late(words16):
            return borrow(E - 1, words16)

        wqa = late(2 * DC * H * 32).rearrange("p (s c h d) -> p s c h d", s=2, c=DC, h=H)
        xn = late(2 * D).bitcast(f32)
        xnT = late(2 * D).rearrange("p (s d) -> p s d", s=2)
        late(1024)
        vs = late(2 * B * NC * 2 * DV).rearrange("p (s b c h d) -> p s b c h d", s=2, b=B, c=NC, h=2)

        wka = scratch(2 * DC * 512).rearrange("p (s c h d) -> p s c h d", s=2, c=DC, h=H)
        wva = scratch(2 * DC * D).rearrange("p (s c d) -> p s c d", s=2, c=DC)
        ctxT = scratch(2 * DC * B * PAIR).rearrange("p (s c b k) -> p s c b k", s=2, c=DC, b=B)
        v32 = scratch(NC * 32 * 2).bitcast(f32)
        bvr = scratch(2 * D)
        bvf = scratch(2 * D).bitcast(f32)
        raw = pt[:].rearrange("p u s k -> p (u s k)").bitcast(f32)
        wq_raw = raw[:, 0:512].rearrange("p (c n) -> p c n", c=DC)
        wkv_raw = raw[:, 512:1536].rearrange("p (c n) -> p c n", c=DC)
        wo_raw = raw[:, 1536:2048].rearrange("p (c n) -> p c n", c=DC)
        wg_raw = raw[:, 2048:2064].rearrange("p (c n) -> p c n", c=DC)
        ctx_main = probs[:, 0:512].rearrange("p (b d) -> p b d", b=B)
        ctx_tail = probs[0:NK - P, 512:1024].rearrange("p (b d) -> p b d", b=B)
        b1_raw = probs[0:E * FC, 1024:1024 + P]
        bk_bc, bq_bc, prod = (probs[:, 1152 + n * D:1152 + (n + 1) * D] for n in range(3))
        k32 = [probs[:, 1920 + n * NK:1920 + (n + 1) * NK] for n in range(2)]

        ps = ctx.enter_context(nc.psum_tensor("ps", [P, 8, 512], f32))
        score_ps = [ps[:, 2 * n:2 * n + 2, :] for n in range(2)]
        pt_ps, o_ps, misc = [ps[:, 4, :], ps[:, 7, :]], ps[:, 5, :], ps[:, 6, :]
        k_bank = [misc, ps[:, 7, :]]
        misc16 = ps[:, 6, :].bitcast(f16)
        h_ps = [[ps[:, 2 * n + m, :] for m in range(2)] for n in range(2)]
        y_ps = [ps[:, 4, :], ps[:, 5, :]]
        xT_ps = [ps[:, 6, :].bitcast(f16)[:, 0:512], ps[:, 7, :].bitcast(f16)[:, 0:512]]

        S = {n: sem(n) for n in """c_in ctx_in w_in bias_in z_bias z_pad z_cum z_kbd z_set padid x_in0 x_in1 xb_in0 xb_in1 list_init
            ctxT_ps k_ps k_aff k_hi k_lo k_row k_fold v_ps v_mask v_hi v_done b1T_ps b1T_done wsplit_hi wsplit
            w_stage0 w_stage1 w_scaled w_hi w_lo0 w_lo1 apart
            st1_d mv1_d ve1_d rstd1 xn_done xnT_ps xnT_hi xnT_lo q_ps q_hi q_lo
            s_ps kink mx_d nb_d p_done t_ps pt_hi pt_lo m_done rec_d o_norm oT_ps oT_hi oT_lo pr_ps xb_bo x2_done x2_out0 x2_out1
            st2_d mv2_d ve2_d rstd2 xn2_done xs_hi xs_lo x2T_ps x2T_done lg_ps lg_d m8_d mi_d nm_d e8_d oh_d sel_d
            cum_d rk_ps ohr_d pos_d gates tail_d scat0 scat1
            cnt_ps sched sched_done n_done pads b2_in
            xt_in0 xt_in1 xt_in2 xt_in3 xT_ps_d xT_done h_ps_d h_done hh_hi hh_lo y_ps_d yb_d wa_d wb_d ex_d y_done added""".split()}
        s = type("Sems", (), S)

        def wait(eng, semaphore, value):
            if not isinstance(value, int) or value > 0:
                eng.wait_ge(semaphore, value)

        def wait_alone(eng, semaphore, value):
            if not isinstance(value, int):
                eng.wait_ge(semaphore, value).then_inc(s.apart, 1)
            elif value > 0:
                eng.wait_ge(semaphore, value)

        def per_tile(i, par, each):
            return each * (i // 2) if isinstance(i, int) else each // 2 * (i - par)

        def turns(turn, loop):
            for i in range(-3, 5):
                turn(i, i % 2)
            with loop(5, 11, 2) as i:
                turn(i, 1)
                turn(i + 1, 0)
            for i in range(11, NT + 3):
                turn(i, i % 2)

        def tile(t):
            return t if not isinstance(t, int) or 0 <= t < NT else None

        def stages(i):
            return [tile(i + n) for n in (3, 2, 1, 0, -1, -2, -3)]

        def upto(t):
            return min(max(t + 1, 0), NT) if isinstance(t, int) else t + 1

        def first_row(i, par):
            return (i % B) * NQ + (i // B) * P if isinstance(i, int) else par * NQ + (i - par) * (P // B)

        def weight_units(i, par):
            if not isinstance(i, int):
                return [(EARLY + 2 * i + n, i + 2 - par, par, n, EARLY // 2 + i) for n in range(2)]
            u = EARLY + 2 * i if 0 <= i < 11 else UNITS - 6 + 2 * (i - 15) if 15 <= i < 18 else None
            return [] if u is None else [numbered(u), numbered(u + 1)]

        def numbered(u):
            return u, u // 4 * 2, u % 4 // 2, u % 2, u // 2

        def units_at(i, par, slot):
            return weight_units(i, par)[slot - 3:slot - 2] if slot in (3, 4) else []

        def scaled_before(unit):
            u, before = unit[0], unit[4]
            return u if isinstance(u, int) and u < EARLY else before + EARLY // 2

        def by_pool(unit):
            u, n = unit[0], unit[3]
            return n == 1 and u < UNITS - 6 or u < EARLY if isinstance(u, int) else n == 1

        def unit_place(unit, lo):
            twice, second, n = unit[1:4]
            flat = wts[:].rearrange("p e a k -> p (e a k)")
            if second:
                return flat[:, ds(twice * 4096 + 4096 + n * 2048, 2048)].rearrange("p (c s d) -> p c s d", c=4, s=2)[:, :, lo, :]
            return flat[:, ds(twice * 4096 + lo * 2048 + n * 1024, 1024)].rearrange("p (c k) -> p c k", c=4)

        def staged(unit):
            return stage[:, unit[3], :].rearrange("p (c k) -> p c k", c=4)

        def v_bank(b, half):
            return 2 * half + b

        def v_parts(n):
            chunks = slice((n % 2) * (NC // 2), (n % 2 + 1) * (NC // 2))
            return (v32.rearrange("p (n c h d) -> p n c h d", n=2, h=2, d=DH)[:, n % 2],
                    lambda w: vs[:, w, n // 2, chunks, :, 0:DH])

        def per_block(t, slot):
            return 16 * (t // 4) if isinstance(t, int) else 4 * (t - slot)

        def experts(eng, t, n):
            first = max(t, 0) if isinstance(t, int) else t
            n = min(t + n, NBLK) - first if isinstance(t, int) else n
            _, values = nc.values_load_multi_w_load_instructions(sched_i[0:1, 1, ds(first, n)], engines=[eng.engine],
                                                                 min_val=0, max_val=E - 1)
            return [None] * (first - t if isinstance(t, int) else 0) + list(values)

        def blocks(step, eng, first, ahead=None):
            def group(t, n, slot):
                known = None if ahead is None else experts(eng, t, n + ahead)
                for k in range(n):
                    step(t + k, (slot + k) % 4, *([] if ahead is None else [known[k:]]))

            group(first, 3 - first, first % 4)
            with eng.Fori(3, NBLK - 7, 4) as t:
                group(t, 4, 3)
            group(NBLK - 4, 4, 3)

        block = ctx.enter_context(nc.Block())

        @block.sync
        def _(sp):
            sp.dma_start(c32[:], c32_in).then_inc(s.c_in, 16)
            sp.dma_start(ctx_main, ctx_in[:, 0:P, :].rearrange("b k d -> k b d")).then_inc(s.ctx_in, 16)
            sp.dma_start(ctx_tail, ctx_in[:, P:NK, :].rearrange("b k d -> k b d")).then_inc(s.ctx_in, 16)
            sp.dma_start(c16[:], c16_in).then_inc(s.c_in, 16)
            sp.dma_start(ids[:], ids_in).then_inc(s.c_in, 16)
            sp.dma_start(wkv_raw, wkv.rearrange("(c p) n -> p c n", p=P)).then_inc(s.w_in, 16)
            sp.dma_start(wq_raw, wq.rearrange("(c p) n -> p c n", p=P)).then_inc(s.w_in, 16)
            sp.dma_start(wo_raw, wo.rearrange("(c p) n -> p c n", p=P)).then_inc(s.w_in, 16)
            sp.dma_start(wg_raw, wg.rearrange("(c p) n -> p c n", p=P)).then_inc(s.w_in, 16)
            sp.dma_start(bvf[0:1, :], bkv[D:2 * D].rearrange("(o n) -> o n", o=1)).then_inc(s.bias_in, 16)
            sp.dma_start(b1_raw, b1.rearrange("e (c p) -> (e c) p", p=P)).then_inc(s.bias_in, 16)
            sp.wait_ge(s.z_bias, 1)
            with nc.allow_non_contiguous_dma(reason="bias columns"):
                for j in range(HG):
                    part = slice(32 * j, 32 * j + DH)
                    sp.dma_start(kbias[part, :], bkv[0:D].rearrange("(g j d) -> j d g", j=HG, d=DH)[j]).then_inc(s.bias_in, 16)
            sp.dma_start(bq_bc, bq.rearrange("(o n) -> o n", o=1).to_broadcast([P, D])).then_inc(s.bias_in, 16)
            sp.dma_start(bk_bc, bkv[0:D].rearrange("(o n) -> o n", o=1).to_broadcast([P, D])).then_inc(s.bias_in, 16)
            sp.dma_start(bo_bc[:], bo.rearrange("(o n) -> o n", o=1).to_broadcast([P, D])).then_inc(s.bias_in, 16)
            sp.dma_start(bg_bc[:], bg.rearrange("(o n) -> o n", o=1).to_broadcast([P, E])).then_inc(s.bias_in, 16)

            def load_a(i, par):
                wait_alone(sp, s.xn_done, i - 1)
                sp.dma_start(xa[:, par, :], x_rows[ds(first_row(i, par), P), :]).then_inc(S[f"x_in{par}"], 16)

            def store(i, par):
                wait_alone(sp, s.x2_done, i + 1)
                sp.dma_start(out_rows[ds(first_row(i, par), P), :], xb[:, par, :]).then_inc(S[f"x2_out{par}"], 16)

            def load_b(i, par):
                wait_alone(sp, s.xn2_done, i - 1)
                wait_alone(sp, S[f"x2_out{par}"], per_tile(i, par, 16))
                sp.dma_start(xb[:, par, :], x_rows[ds(first_row(i, par), P), :]).then_inc(S[f"xb_in{par}"], 16)

            def load_second_biases():
                sp.wait_ge(s.s_ps, G * NT)
                sp.dma_start(b2bc, b2.rearrange("(o e) d -> o (e d)", o=1).to_broadcast([P, E * D])).then_inc(s.b2_in, 16)

            def load_w(unit):
                u, twice, second, n, before = unit
                wait_alone(sp, S[f"w_lo{n}"], before)
                if second:
                    src = w2.rearrange("e f d -> (e f) d")[ds(twice * 512 + n * 512, 512), :].rearrange("(c p) d -> p c d", p=P)
                    sp.dma_start(staged(unit), src).then_inc(S[f"w_stage{n}"], 16)
                else:
                    src = w1.rearrange("e d f -> (e d) f")[ds(twice * P + n * P, P), :]
                    sp.dma_start(stage[:, n, :], src).then_inc(S[f"w_stage{n}"], 16)

            load_a(0, 0)
            load_a(1, 1)
            for u in range(2):
                load_w(numbered(u))
            sp.wait_ge(s.padid, 1)
            for n in range(SPARE):
                sp.dma_start(xlist[E * LIST + n * P:E * LIST + (n + 1) * P, :], pad_rows[:].bitcast(i32)).then_inc(s.list_init, 16)

            def turn(i, par):
                f1, f2, sc, mt, b1, b2, b3 = stages(i)
                for u in weight_units(i, par):
                    load_w(u)
                if tile(i + 4) is not None and not (isinstance(i, int) and i == -3):
                    load_a(i + 4, par)
                if b2 is not None:
                    store(b2, par)
                if mt is not None:
                    load_b(mt, par)
                if isinstance(i, int) and i == 15:
                    load_second_biases()

            for u in range(2, EARLY):
                load_w(numbered(u))
            turns(turn, sp.Fori)
            sp.wait_ge(s.scat0, 16 * NT)
            sp.wait_ge(s.scat1, 16 * NT)
            sp.wait_ge(s.list_init, 16 * SPARE)
            sp.wait_ge(s.n_done, 1)
            _, lengths = nc.values_load_multi_w_load_instructions(cnt_i[0:1, 0, :], engines=[sp.engine], min_val=0, max_val=B * NQ)
            for e in range(E):
                sp.dma_start(xlist[ds(lengths[e] + e * LIST, P), :], pad_rows[:].bitcast(i32)).then_inc(s.pads, 16)
            sp.wait_ge(s.pads, 16 * E)
            sp.wait_ge(s.sched_done, 1)

            def load_block(t, slot):
                r = sp.value_load(sched_i[0:1, 0, ds(t, 1)], min_val=0, max_val=XROWS - P)
                wait_alone(sp, s.xT_ps_d, t - 3)
                wait_alone(sp, s.ex_d, t - 3)
                sp.dma_start(block_rows[slot].bitcast(i32), xlist[ds(r, P), :]).then_inc(S[f"xt_in{slot}"], 16)

            blocks(lambda t, slot: load_block(t + 4, slot) if not isinstance(t, int) or t + 4 < NBLK else None, sp, -4)
            sp.wait_ge(s.added, 16 * NBLK)

        @block.gpsimd
        def _(pool):
            pool.memset(kbias[:], 0.0).then_inc(s.z_bias, 1)
            pool.memset(pad_rows[:], 0.0).then_inc(s.z_pad, 1)
            pool.memset(kbd[:].bitcast(u32), 0).then_inc(s.z_kbd, 1)
            pool.memset(cum[:], 0.0).then_inc(s.z_cum, 1)
            pool.wait_ge(s.c_in, 48)
            pool.wait_ge(s.z_pad, 1)
            pool.tensor_copy(pad_rows[:, 2 * D:2 * D + 2].bitcast(i32), ids[:, NT:NT + 1]).then_inc(s.padid, 1)

            def rstd(i, rs, done, ve_sem):
                pool.wait_ge(ve_sem, i + 1)
                pool.tensor_tensor(rs[:, 1:2], rs[:, 0:1], c32[:, C_HALF:C_HALF + 1], ALU.pow).then_inc(done, 1)

            def scale_w(u):
                pool.wait_ge(S[f"w_stage{u[3]}"], 16 * (u[4] + 1))
                pool.tensor_tensor(stage[:, u[3], :], stage[:, u[3], :], c32[:, C_SW:C_SW + 1].to_broadcast([P, 1024]), ALU.mult).then_inc(s.w_scaled, 1)

            def split_w_lo(u):
                wait_alone(pool, s.w_hi, u[0] + 1)
                pool.tensor_tensor(unit_place(u, 1), staged(u), unit_place(u, 0), ALU.subtract).then_inc(S[f"w_lo{u[3]}"], 1)

            def weights_of(i, q):
                words = rows[:, q, 2 * D:ROW]
                z, zsum = e8[:, 1:2], small[:, 1:2]
                wait_alone(pool, s.e8_d, i + 1)
                pool.tensor_scalar(small[:, 2:3], zsum, 1e-8, 1.0, ALU.mult, ALU.add).then_inc(s.gates, 1)
                pool.wait_ge(s.gates, 4 * i + 1)
                pool.tensor_tensor(small[:, 3:4], small[:, 2:3], z, ALU.add).then_inc(s.gates, 1)
                pool.wait_ge(s.gates, 4 * i + 2)
                pool.tensor_tensor(small[:, 4:5], small[:, 3:4], c32[:, C_MINUS:C_MINUS + 1], ALU.pow).then_inc(s.gates, 1)
                pool.wait_ge(s.gates, 4 * i + 3)
                pool.tensor_tensor(words[:, 6:8].bitcast(f32), small[:, 4:5], z, ALU.mult).then_inc(s.gates, 1)
                pool.tensor_copy(words[:, 2:4].bitcast(f32), mi[:, 0:1]).then_inc(s.tail_d, 1)
                pool.tensor_copy(words[:, 0:2].bitcast(i32), ids[:, ds(i, 1)]).then_inc(s.tail_d, 1)
                pool.wait_ge(s.gates, 4 * i + 4)
                pool.tensor_tensor(words[:, 4:6].bitcast(f32), small[:, 4:5], words[:, 6:8].bitcast(f32), ALU.subtract).then_inc(s.tail_d, 1)

            def dispatch(i, q):
                wait_alone(pool, s.xs_lo, i + 1)
                wait_alone(pool, s.tail_d, 3 * (i + 1))
                wait_alone(pool, s.pos_d, i + 1)
                for c in range(2):
                    pool.indirect_dma_start(
                        out=xlist, out_offset=bass.IndirectOffsetOnAxis(ap=pos[:, q, c:c + 1], axis=0),
                        in_=rows[:, q, :].bitcast(i32), in_offset=None).then_inc(S[f"scat{q}"], 16)

            def turn(i, par):
                f1, f2, sc, mt, b1, b2, b3 = stages(i)
                units = [u for u in weight_units(i, par) if by_pool(u)]
                if b2 is not None:
                    rstd(b2, rs2, s.rstd2, s.ve2_d)
                if b1 is not None:
                    pool.wait_ge(S[f"xb_in{1 - par}"], per_tile(b1, 1 - par, 16) + 16)
                    pool.tensor_tensor(xb[:, 1 - par, :], xb[:, 1 - par, :], bo_bc[:], ALU.add).then_inc(s.xb_bo, 1)
                for u in units:
                    scale_w(u)
                if b3 is not None:
                    weights_of(b3, 1 - par)
                if f1 is not None:
                    rstd(f1, rs1, s.rstd1, s.ve1_d)
                if b2 is not None:
                    pool.wait_ge(s.xs_hi, b2 + 1)
                    pool.tensor_tensor(rows[:, par, D:2 * D], xn2[:], rows[:, par, 0:D], ALU.subtract).then_inc(s.xs_lo, 1)
                if b3 is not None:
                    dispatch(b3, 1 - par)
                for u in units:
                    split_w_lo(u)

            scale_w(numbered(0))
            for u in range(1, EARLY):
                scale_w(numbered(u))
                split_w_lo(numbered(u - 1))
            split_w_lo(numbered(EARLY - 1))
            pool.wait_ge(s.bias_in, 16 * BIASES)
            turns(turn, pool.Fori)
            pool.wait_ge(s.x2_out0, 8 * NT)
            pool.wait_ge(s.x2_out1, 8 * NT)

            def add_block(t, slot):
                wait_alone(pool, s.y_done, t + 1)
                wait_alone(pool, s.added, 16 * t)
                pool.indirect_dma_start(
                    out=out_rows, out_offset=bass.IndirectOffsetOnAxis(ap=row_id[:, slot:slot + 1], axis=0),
                    in_=ysb[slot % 2][:], in_offset=None, bounds_check=B * NQ - 1, oob_is_err=False,
                    compute_op=ALU.add).then_inc(s.added, 16)

            blocks(add_block, pool, 0)
            pool.wait_ge(s.added, 16 * NBLK)

        @block.scalar
        def _(act):
            def split_w_hi(u):
                if by_pool(u):
                    act.wait_ge(s.w_scaled, scaled_before(u) + 1)
                else:
                    act.wait_ge(S[f"w_stage{u[3]}"], 16 * (u[4] + 1))
                if isinstance(u[0], int) and u[0] == UNITS - 4:
                    act.wait_ge(s.q_ps, NT)
                if isinstance(u[0], int) and u[0] == UNITS - 2:
                    act.wait_ge(s.m_done, NU * NT)
                nc.scalar.activation(unit_place(u, 0), staged(u), ACT.Copy, scale=1.0 if by_pool(u) else SW).then_inc(s.w_hi, 1)

            for u in range(2):
                split_w_hi(numbered(u))
            act.wait_ge(s.z_kbd, 1)
            for b in range(B):
                for g in range(G):
                    n = b * G + g
                    act.wait_ge(s.k_row, n + 1)
                    for j in range(HG):
                        part = slice(32 * j, 32 * j + 32)
                        last = nc.scalar.copy(kbd[part, 0, b, g, j * NK:(j + 1) * NK], k32[n % 2][part, :])
                    last.then_inc(s.k_hi, 1)
                    if n % G == G - 1:
                        split_w_hi(numbered(2 + b))
            for n in range(2 * B):
                act.wait_ge(s.v_mask, n + 1)
                vm, vh = v_parts(n)
                nc.scalar.copy(vh(0), vm).then_inc(s.v_hi, 1)

            def pt_hi(i, v, par):
                act.wait_ge(s.t_ps, i * NU + v + 1)
                wait(act, s.m_done, (i - 1) * NU + v + 1)
                nc.scalar.copy(pt[:, v, 0, :], pt_ps[(v + par) % 2]).then_inc(s.pt_hi, 1)

            def exps(i, g):
                act.wait_ge(s.nb_d, i * G + g + 1)
                wait(act, s.t_ps, (i - 1) * NU + min((g + 1) * GK - 1, FLAT - 1) // 512 + 1)
                for j in range(HG):
                    last = nc.scalar.activation(probs[:, (g * HG + j) * NK:(g * HG + j + 1) * NK],
                                                score_ps[g % 2][:, j // 2, (j % 2) * NK:(j % 2 + 1) * NK],
                                                ACT.Exp, bias=nb[:, g, j:j + 1], scale=1.0 / S_SCORE)
                last.then_inc(s.p_done, 1)

            def turn(i, par):
                f1, f2, sc, mt, b1, b2, b3 = stages(i)
                for slot in range(5):
                    if mt is not None:
                        pt_hi(mt, slot, par)
                    if b3 is not None and slot == 0:
                        act.wait_ge(s.x2T_ps, b3 + 1)
                        act.wait_ge(s.x2_done, upto(i - 2))
                        nc.scalar.copy(x2T[:], misc16[:, 2 * D:4 * D]).then_inc(s.x2T_done, 1)
                    if b1 is not None and slot == 2:
                        act.wait_ge(s.oT_ps, b1 + 1)
                        wait(act, s.pr_ps, b1)
                        nc.scalar.copy(oT[:, 0, :], misc[:, 0:D]).then_inc(s.oT_hi, 1)
                    if f2 is not None and slot == 3:
                        act.wait_ge(s.xnT_ps, f2 + 1)
                        wait(act, s.q_ps, f2)
                        nc.scalar.copy(xnT[:, 0, :], misc[:, 0:D]).then_inc(s.xnT_hi, 1)
                    if f2 is not None and slot == 4:
                        act.wait_ge(s.q_ps, f2 + 1)
                        nc.scalar.activation(qs[:, par, 0, :], misc, ACT.Copy, scale=SQ / (SX * SW)).then_inc(s.q_hi, 1)
                    if sc is not None and slot > 0:
                        exps(sc, slot - 1)
                    if b3 is not None and slot == 2:
                        act.wait_ge(s.nm_d, b3 + 1)
                        wait(act, s.tail_d, 3 * b3)
                        nc.scalar.activation(e8[:], m8[:], ACT.Exp, bias=small[:, 0:1], accum_out=small[:, 1:2]).then_inc(s.e8_d, 1)
                    if b2 is not None and slot == 3:
                        act.wait_ge(s.xn2_done, b2 + 1)
                        wait(act, S[f"scat{par}"], per_tile(b2, par, 32))
                        nc.scalar.copy(rows[:, par, 0:D], xn2[:]).then_inc(s.xs_hi, 1)
                    for u in units_at(i, par, slot):
                        split_w_hi(u)

            turns(turn, act.Fori)

            act.wait_ge(s.sched_done, 1)
            act.wait_ge(s.b1T_done, 1)
            act.wait_ge(s.o_norm, NT)

            def copy_rows(t, par):
                act.wait_ge(s.xT_ps_d, t + 1)
                wait(act, s.h_ps_d, 2 * (t - 1))
                nc.scalar.copy(xT[par], xT_ps[par]).then_inc(s.xT_done, 1)

            def gelu_block(t, e, par):
                for m in range(2):
                    act.wait_ge(s.h_ps_d, 2 * t + m + 1)
                    wait(act, s.hh_lo, 2 * (t - 1))
                    for f in range(4):
                        c = 4 * m + f
                        last = nc.scalar.activation(h32[par][:, c * P:(c + 1) * P], h_ps[par][m][:, f * P:(f + 1) * P],
                                                    ACT.Gelu_apprx_tanh, bias=b1T[:, ds(e * FC + c, 1)], scale=1.0 / (SX * SW))
                    last.then_inc(s.h_done, 1)

            def step(t, slot, e):
                if not isinstance(t, int) or t + 2 < NBLK:
                    copy_rows(t + 2, slot % 2)
                if not isinstance(t, int) or 0 <= t + 1 < NBLK:
                    gelu_block(t + 1, e[1], 1 - slot % 2)

            blocks(step, act, -2, 1)

        @block.vector
        def _(dve):
            def split(dst, src, scale, inc=None):
                dve.tensor_scalar(dst(0), src, scale, None, ALU.mult).then_inc(s.wsplit_hi, 1)
                count[0] += 1
                dve.wait_ge(s.wsplit_hi, count[0])
                dve.scalar_tensor_tensor(out=dst(1), in0=src, scalar=scale, in1=dst(0), op0=ALU.mult,
                                         op1=ALU.subtract).then_inc(s.wsplit, 1)

            count = [0]
            dve.memset(wka.bitcast(u32), 0).then_inc(s.z_set, 1)
            dve.memset(wqa.bitcast(u32), 0).then_inc(s.z_set, 1)
            dve.memset(probs[:, FLAT:NC * P], 0.0).then_inc(s.z_set, 1)
            dve.wait_ge(s.z_set, 3)
            dve.wait_ge(s.w_in, 64)
            for c in range(DC):
                split(lambda w: wka[:, w, c, :, 0:DH], wkv_raw[:, c, 0:D].rearrange("p (h d) -> p h d", h=H), SW)
            for c in range(DC):
                split(lambda w: wva[:, w, c, :], wkv_raw[:, c, D:2 * D], SW)
            dve.wait_ge(s.ctxT_ps, 1)
            for c in range(DC):
                for b in range(B):
                    src = ps[:, 2 * c + b, 0:NK].unsqueeze(1).to_broadcast([P, 2, NK])
                    split(lambda w: ctxT[:, w, c, b, :].rearrange("p (r k) -> p r k", r=2), src, SCTX)
            dve.wait_ge(s.bias_in, 16 * BIASES)
            for n in range(DC + 1):
                src = wkv_raw[:, n, 0:D] if n < DC else bk_bc
                dve.tensor_tensor(prod, src, bq_bc, ALU.mult).then_inc(s.k_fold, 1)
                dve.wait_ge(s.k_fold, 2 * n + 1)
                dve.tensor_reduce(rec[:], prod.rearrange("p (h d) -> p h d", h=H), AX.X, ALU.add).then_inc(s.k_fold, 1)
                dve.wait_ge(s.k_fold, 2 * n + 2)
                if n < DC:
                    split(lambda w: wka[:, w, n, :, DH], rec[:], S_ROW * SCALE * SW / SK)
                    dve.wait_ge(s.wsplit, count[0])
            dve.tensor_tensor(prod[:, 0:H].rearrange("p (g j) -> p g j", g=G), rec[:].rearrange("p (g j) -> p g j", g=G),
                              c32[:, C_ROW:C_ROW + HG].unsqueeze(1).to_broadcast([P, G, HG]), ALU.mult).then_inc(s.k_fold, 1)
            dve.wait_ge(s.k_fold, 2 * DC + 3)
            dve.tensor_reduce(fold[:], prod[:, 0:H].rearrange("p (g j) -> p g j", g=G), AX.X, ALU.add).then_inc(s.k_fold, 1)
            dve.wait_ge(s.z_bias, 1)
            dve.tensor_scalar(kbias[:], kbias[:], SK, None, ALU.mult).then_inc(s.k_fold, 1)
            dve.wait_ge(s.k_fold, 2 * DC + 5)
            dve.scalar_tensor_tensor(out=kbias[:], in0=fold[:], scalar=S_ROW * SCALE, in1=kbias[:], op0=ALU.mult,
                                     op1=ALU.add).then_inc(s.k_fold, 1)
            split(lambda w: bvr[0:1, w * D:(w + 1) * D], bvf[0:1, :], 2.0**7)
            for c in range(DC):
                split(lambda w: wqa[:, w, c, :, 0:DH], wq_raw[:, c, :].rearrange("p (h d) -> p h d", h=H), SW)
            split(lambda w: wos[:, w, :, :], wo_raw, SW)
            split(lambda w: wgs[:, w, :, :], wg_raw, SW)
            dve.wait_ge(s.b1T_ps, 1)
            dve.tensor_copy(b1T[:], o_ps[:, 0:E * FC]).then_inc(s.b1T_done, 1)

            dve.wait_ge(s.k_fold, 2 * DC + 6)

            def k_affine(n):
                b, g = n // G, n % G
                dve.wait_ge(s.k_ps, n + 1)
                wait(dve, s.k_lo, n - 1)
                wait(dve, s.k_hi, n - 1)
                dve.tensor_scalar(k32[n % 2], k_bank[n % 2][:, 0:NK], SK / (SCTX * SW), kbias[:, g:g + 1], ALU.mult, ALU.add).then_inc(s.k_aff, 1)
                dve.wait_ge(s.k_aff, n + 1)
                dve.scalar_tensor_tensor(out=k32[n % 2], in0=c32[:, C_KPOS:C_KPOS + NK], scalar=c32[:, C_SLOPE + g:C_SLOPE + g + 1],
                                         in1=k32[n % 2], op0=ALU.mult, op1=ALU.add).then_inc(s.k_row, 1)

            def k_low(n):
                b, g = n // G, n % G
                dve.wait_ge(s.k_hi, n + 1)
                for j in range(HG):
                    part, cols = slice(32 * j, 32 * j + 32), slice(j * NK, (j + 1) * NK)
                    last = dve.tensor_tensor(kbd[part, 1, b, g, cols], k32[n % 2][part, :], kbd[part, 0, b, g, cols], ALU.subtract)
                last.then_inc(s.k_lo, 1)

            for n in range(B * G + 1):
                if n < B * G:
                    k_affine(n)
                if n > 0:
                    k_low(n - 1)
            mask = c32[:, C_MASK:C_MASK + 2 * NC].rearrange("p (c m) -> p c m", m=2)
            dve.tensor_copy(vs[:, 0, :, :, :, DH], mask.unsqueeze(1).to_broadcast([P, B, NC, 2]))
            dve.memset(vs[:, 1, :, :, :, DH], 0.0)
            def v_low(n):
                vm, place = v_parts(n)
                dve.wait_ge(s.v_hi, n + 1)
                dve.tensor_tensor(place(1), vm, place(0), ALU.subtract).then_inc(s.v_done, 1)

            for n in range(2 * B):
                chunks = slice((n % 2) * (NC // 2) * 2, (n % 2 + 1) * (NC // 2) * 2)
                flat = lambda v: v.rearrange("p (k d) -> p k d", d=DH)
                dve.wait_ge(s.v_ps, n // 2 + 1)
                wait(dve, s.v_done, n - 1)
                dve.scalar_tensor_tensor(out=flat(v32)[:, chunks], in0=flat(ps[:, v_bank(n // 2, n % 2), 0:(NC // 2) * 32]),
                                         scalar=S_V / (SCTX * SW),
                                         in1=c32[:, C_MASK:C_MASK + 2 * NC][:, chunks].unsqueeze(2).to_broadcast([P, NC, DH]),
                                         op0=ALU.mult, op1=ALU.mult).then_inc(s.v_mask, 1)
                if n > 0:
                    v_low(n - 1)
            v_low(2 * B - 1)

            def pt_lo(i, v, par):
                dve.wait_ge(s.pt_hi, i * NU + v + 1)
                dve.tensor_tensor(pt[:, v, 1, :], pt_ps[(v + par) % 2], pt[:, v, 0, :], ALU.subtract).then_inc(s.pt_lo, 1)

            def split_w_lo(i, par, slot):
                for u in units_at(i, par, slot):
                    if not by_pool(u):
                        dve.wait_ge(s.w_hi, u[0] + 1)
                        dve.scalar_tensor_tensor(out=unit_place(u, 1), in0=staged(u), scalar=SW, in1=unit_place(u, 0),
                                                 op0=ALU.mult, op1=ALU.subtract).then_inc(S[f"w_lo{u[3]}"], 1)

            def maxima(i, g):
                two_banks = score_ps[g % 2]
                dve.wait_ge(s.s_ps, i * G + g + 1)
                if isinstance(i, int) and i >= NT - 4:
                    tail = i // 2 - (NT // 2 - 2)
                    for j in range(HG):
                        cols = two_banks[:, j // 2, (j % 2) * NK:(j % 2 + 1) * NK]
                        dve.scalar_tensor_tensor(out=cols, in0=c32[:, C_KINK + tail * NK:C_KINK + (tail + 1) * NK],
                                                 scalar=2.0 * SLOPES[g * HG + j] * S_SCORE, in1=cols,
                                                 op0=ALU.mult, op1=ALU.add).then_inc(s.kink, 1)
                    dve.wait_ge(s.kink, ((i - (NT - 4)) * G + g + 1) * HG)
                dve.tensor_reduce(mx[:, g, :], two_banks[:, :, 0:PAIR].rearrange("p a (j k) -> p a j k", j=2), AX.X, ALU.max).then_inc(s.mx_d, 1)

            def exp_bias(i, g):
                dve.wait_ge(s.mx_d, i * G + g + 1)
                dve.tensor_scalar(nb[:, g, :], mx[:, g, :], -1.0 / S_SCORE, math.log(S_P), ALU.mult, ALU.add).then_inc(s.nb_d, 1)

            def turn(i, par):
                f1, f2, sc, mt, b1, b2, b3 = stages(i)
                p1, p2 = 1 - par, par
                if b2 is not None:
                    dve.wait_ge(s.pr_ps, b2 + 1)
                    dve.wait_ge(s.xb_bo, b2 + 1)
                    dve.scalar_tensor_tensor(out=xb[:, p2, :], in0=misc[:, 0:D], scalar=1.0 / (S_V * SW), in1=xb[:, p2, :],
                                             op0=ALU.mult, op1=ALU.add).then_inc(s.x2_done, 1)
                if mt is not None:
                    pt_lo(mt, 0, par)
                if sc is not None:
                    maxima(sc, 0)
                if b1 is not None:
                    dve.wait_ge(s.m_done, NU * (b1 + 1))
                    ov = o_ps[:, 0:H * DV].rearrange("p (h d) -> p h d", h=H)
                    dve.reciprocal(rec[:], ov[:, :, DH]).then_inc(s.rec_d, 1)
                if sc is not None:
                    exp_bias(sc, 0)
                if b3 is not None:
                    dve.wait_ge(s.lg_ps, b3 + 1)
                    dve.scalar_tensor_tensor(out=lg[:], in0=misc[:, 0:E], scalar=1.0 / (SX * SW), in1=bg_bc[:], op0=ALU.mult,
                                             op1=ALU.add).then_inc(s.lg_d, 1)
                if b1 is not None:
                    dve.wait_ge(s.rec_d, b1 + 1)
                    wait(dve, s.oT_ps, b1)
                    dve.tensor_tensor(o32[:].rearrange("p (h d) -> p h d", h=H), ov[:, :, 0:DH],
                                      rec[:].unsqueeze(2).to_broadcast([P, H, DH]), ALU.mult).then_inc(s.o_norm, 1)
                if b3 is not None:
                    wait_alone(dve, s.lg_d, b3 + 1)
                    wait_alone(dve, s.e8_d, b3)
                    dve.max(m8[:], lg[:]).then_inc(s.m8_d, 1)
                if b2 is not None:
                    dve.wait_ge(s.x2_done, b2 + 1)
                    dve.bn_stats(st2[:], xb[:, p2, :]).then_inc(s.st2_d, 1)
                if b3 is not None:
                    wait_alone(dve, s.m8_d, b3 + 1)
                    wait_alone(dve, s.tail_d, 3 * b3)
                    dve.max_index(mi[:], m8[:], lg[:]).then_inc(s.mi_d, 1)
                    dve.tensor_scalar(small[:, 0:1], m8[:, 0:1], -1.0, None, ALU.mult).then_inc(s.nm_d, 1)
                if mt is not None:
                    pt_lo(mt, 1, par)
                if b2 is not None:
                    wait_alone(dve, s.st2_d, b2 + 1)
                    dve.bn_aggr(mv2[:], st2[:]).then_inc(s.mv2_d, 1)
                if sc is not None:
                    maxima(sc, 1)
                if b3 is not None:
                    dve.wait_ge(s.mi_d, b3 + 1)
                    dve.tensor_tensor(oh[:], c32[:, C_IOTA:C_IOTA + E].unsqueeze(1).to_broadcast([P, 2, E]),
                                      mi[:, 0:2].unsqueeze(2).to_broadcast([P, 2, E]), ALU.is_equal).then_inc(s.oh_d, 1)
                if sc is not None:
                    exp_bias(sc, 1)
                if b2 is not None:
                    dve.wait_ge(s.mv2_d, b2 + 1)
                    dve.tensor_scalar(rs2[:, 0:1], mv2[:, 1:2], EPS, 1.0 / (SX * SX), ALU.add, ALU.mult).then_inc(s.ve2_d, 1)
                if b3 is not None:
                    dve.wait_ge(s.oh_d, b3 + 1)
                    wait(dve, s.rk_ps, b3)
                    dve.tensor_tensor(sel[:], oh[:, 0, :], oh[:, 1, :], ALU.add).then_inc(s.sel_d, 1)
                if b1 is not None:
                    dve.wait_ge(s.oT_hi, b1 + 1)
                    dve.tensor_tensor(oT[:, 1, :], misc[:, 0:D], oT[:, 0, :], ALU.subtract).then_inc(s.oT_lo, 1)
                if mt is not None:
                    pt_lo(mt, 2, par)
                if b3 is not None:
                    dve.wait_ge(s.sel_d, b3 + 1)
                    dve.tensor_tensor(cum[:, p2, :], cum[:, p1, :], sel[:], ALU.add).then_inc(s.cum_d, 1)
                if sc is not None:
                    maxima(sc, 2)
                if f1 is not None:
                    dve.wait_ge(S[f"x_in{p1}"], per_tile(f1, p1, 16) + 16)
                    dve.bn_stats(st1[:], xa[:, p1, :]).then_inc(s.st1_d, 1)
                if sc is not None:
                    exp_bias(sc, 2)
                if b2 is not None:
                    dve.wait_ge(s.rstd2, b2 + 1)
                    wait(dve, s.xs_lo, b2)
                    dve.tensor_scalar(xn2[:], xb[:, p2, :], mv2[:, 0:1], rs2[:, 1:2], ALU.subtract, ALU.mult).then_inc(s.xn2_done, 1)
                if f1 is not None:
                    wait_alone(dve, s.st1_d, f1 + 1)
                    dve.bn_aggr(mv1[:], st1[:]).then_inc(s.mv1_d, 1)
                if f1 is not None:
                    dve.wait_ge(s.mv1_d, f1 + 1)
                    dve.tensor_scalar(rs1[:, 0:1], mv1[:, 1:2], EPS, 1.0 / (SX * SX), ALU.add, ALU.mult).then_inc(s.ve1_d, 1)
                if f2 is not None:
                    dve.wait_ge(s.xnT_hi, f2 + 1)
                    dve.tensor_tensor(xnT[:, 1, :], misc[:, 0:D], xnT[:, 0, :], ALU.subtract).then_inc(s.xnT_lo, 1)
                if mt is not None:
                    pt_lo(mt, 3, par)
                if b3 is not None:
                    dve.wait_ge(s.rk_ps, b3 + 1)
                    dve.wait_ge(s.xnT_hi, upto(i + 2))
                    dve.tensor_tensor(ohr[:], oh[:], misc[:, D:D + E].unsqueeze(1).to_broadcast([P, 2, E]), ALU.mult).then_inc(s.ohr_d, 1)
                if b3 is not None:
                    dve.wait_ge(s.ohr_d, b3 + 1)
                    wait(dve, S[f"scat{p1}"], per_tile(b3, p1, 32))
                    with nc.allow_low_precision(reason="whole numbers below 2^24"):
                        dve.tensor_reduce(pos[:, p1, :], ohr[:], AX.X, ALU.add).then_inc(s.pos_d, 1)
                if sc is not None:
                    maxima(sc, 3)
                if f1 is not None:
                    dve.wait_ge(s.rstd1, f1 + 1)
                    wait(dve, s.xnT_ps, f1)
                    dve.tensor_scalar(xn, xa[:, p1, :], mv1[:, 0:1], rs1[:, 1:2], ALU.subtract, ALU.mult).then_inc(s.xn_done, 1)
                if sc is not None:
                    exp_bias(sc, 3)
                if mt is not None:
                    pt_lo(mt, 4, par)
                if f2 is not None:
                    dve.wait_ge(s.q_hi, f2 + 1)
                    dve.scalar_tensor_tensor(out=qs[:, par, 1, :], in0=misc, scalar=SQ / (SX * SW), in1=qs[:, par, 0, :],
                                             op0=ALU.mult, op1=ALU.subtract).then_inc(s.q_lo, 1)
                split_w_lo(i, par, 3)
                split_w_lo(i, par, 4)

            dve.wait_ge(s.z_cum, 1)
            turns(turn, dve.Fori)

            n_sched = [0]

            def then(ins):
                n_sched[0] += 1
                ins.then_inc(s.sched, 1)
                dve.wait_ge(s.sched, n_sched[0])

            dve.wait_ge(s.cnt_ps, 1)
            then(dve.tensor_copy(cnt_i[:, 0, :], misc[:, 0:E]))
            dve.tensor_scalar(cnt_f[:, 0, :], misc[:, 0:E], float(P - 1), None, ALU.add).then_inc(s.n_done, 1)
            dve.wait_ge(s.n_done, 1)
            then(dve.tensor_copy(cnt_i[:, 1, :], cnt_f[:, 0, :]))
            then(dve.tensor_single_scalar(cnt_i[:, 2, :], cnt_i[:, 1, :], 7, ALU.arith_shift_right))
            then(dve.tensor_copy(cnt_f[:, 1, :], cnt_i[:, 2, :]))
            src = 1
            for n, step in enumerate((1, 2, 4)):
                then(dve.tensor_copy(cnt_f[:, 2 + n, 0:step], cnt_f[:, src, 0:step]))
                then(dve.tensor_tensor(cnt_f[:, 2 + n, step:E], cnt_f[:, src, step:E], cnt_f[:, src, 0:E - step], ALU.add))
                src = 2 + n
            blk = c32[:, C_BLK:C_BLK + NBLK]
            before, expert, start = (sched_f[:, n, 0:NBLK] for n in range(3))
            ended = probs[:, 0:NBLK * E].rearrange("p (b e) -> p b e", e=E)
            then(dve.tensor_tensor(ended, blk.unsqueeze(2).to_broadcast([P, NBLK, E]),
                                   cnt_f[:, 4, :].unsqueeze(1).to_broadcast([P, NBLK, E]), ALU.is_ge))
            then(dve.tensor_reduce(expert, ended, AX.X, ALU.add))
            then(dve.tensor_tensor(ended, ended, cnt_f[:, 1, :].unsqueeze(1).to_broadcast([P, NBLK, E]), ALU.mult))
            then(dve.tensor_reduce(start, ended, AX.X, ALU.add))
            then(dve.tensor_tensor(before, blk, start, ALU.subtract))
            then(dve.tensor_scalar(before, before, float(P), None, ALU.mult))
            then(dve.scalar_tensor_tensor(out=start, in0=expert, scalar=float(LIST), in1=before, op0=ALU.mult, op1=ALU.add))
            then(dve.tensor_scalar(before, expert, float(E - 1), None, ALU.min))
            then(dve.tensor_copy(sched_i[0:1, 0, 0:NBLK], start[0:1, :]))
            dve.tensor_copy(sched_i[0:1, 1, 0:NBLK], before[0:1, :]).then_inc(s.sched_done, 1)
            dve.wait_ge(s.b2_in, 16)
            dve.wait_ge(s.sched_done, 1)

            def split_h(t, m, par):
                cols = slice(m * 512, (m + 1) * 512)
                dve.wait_ge(s.h_done, 2 * t + m + 1)
                wait(dve, s.y_ps_d, t - 1)
                dve.tensor_scalar(hh[par][:, 0, cols], h32[par][:, cols], S_H, None, ALU.mult).then_inc(s.hh_hi, 1)
                dve.wait_ge(s.hh_hi, 2 * t + m + 1)
                dve.scalar_tensor_tensor(out=hh[par][:, 1, cols], in0=h32[par][:, cols], scalar=S_H, in1=hh[par][:, 0, cols],
                                         op0=ALU.mult, op1=ALU.subtract).then_inc(s.hh_lo, 1)

            def extract(t, slot):
                dve.wait_ge(S[f"xt_in{slot}"], per_block(t, slot) + 16)
                wait(dve, s.y_done, t - 3)
                dve.scalar_tensor_tensor(out=wsel[:, slot, 0:1], in0=pay[slot][:, 1:2], scalar=sched_f[:, 1, ds(t, 1)],
                                         in1=pay[slot][:, 2:3], op0=ALU.is_equal, op1=ALU.mult).then_inc(s.wa_d, 1)
                wait(dve, s.added, 16 * (t - 3))
                dve.tensor_copy(row_id[:, slot:slot + 1], pay[slot][:, 0:1].bitcast(i32)).then_inc(s.wb_d, 1)
                dve.wait_ge(s.wa_d, t + 1)
                dve.tensor_tensor(wsel[:, slot, 1:2], wsel[:, slot, 0:1], pay[slot][:, 3:4], ALU.add).then_inc(s.ex_d, 1)

            def weigh(t, e, slot):
                par = slot % 2
                dve.wait_ge(s.y_ps_d, t + 1)
                wait(dve, s.added, 16 * (t - 1))
                dve.scalar_tensor_tensor(out=ysb[par][:], in0=y_ps[par][:, 0:D], scalar=1.0 / (S_H * SW), in1=b2bc[:, ds(e * D, D)],
                                         op0=ALU.mult, op1=ALU.add).then_inc(s.yb_d, 1)
                dve.wait_ge(s.yb_d, 2 * t + 1)
                dve.scalar_tensor_tensor(out=ysb[par][:], in0=y_ps[par][:, D:2 * D], scalar=1.0 / (S_H * SW), in1=ysb[par][:],
                                         op0=ALU.mult, op1=ALU.add).then_inc(s.yb_d, 1)
                dve.wait_ge(s.yb_d, 2 * t + 2)
                dve.wait_ge(s.ex_d, t + 1)
                dve.tensor_scalar(ysb[par][:], ysb[par][:], wsel[:, slot, 1:2], None, ALU.mult).then_inc(s.y_done, 1)

            def step(t, slot, e):
                ahead = not isinstance(t, int) or 0 <= t + 1 < NBLK
                if ahead:
                    split_h(t + 1, 0, 1 - slot % 2)
                if not isinstance(t, int) or t + 2 < NBLK:
                    extract(t + 2, (slot + 2) % 4)
                if not isinstance(t, int) or t >= 0:
                    weigh(t, e[0], slot)
                if ahead:
                    split_h(t + 1, 1, 1 - slot % 2)

            blocks(step, dve, -2, 0)

        @block.tensor
        def _(pe):
            def mm(out_, lhsT, rhs, start, stop, skip=False):
                return nc.tensor.matmul(out_, lhsT, rhs, start=start, stop=stop, skip_group_check=skip)

            THREE = ((0, 0), (0, 1), (1, 0))
            pe.wait_ge(s.c_in, 48)
            pe.wait_ge(s.ctx_in, 32)
            for c in range(DC):
                for b in range(B):
                    cols = slice(c * P, (c + 1) * P)
                    nc.tensor.transpose(ps[:, 2 * c + b, 0:P], ctx_main[:, b, cols], ident)
                    last = nc.tensor.transpose(ps[:, 2 * c + b, P:NK], ctx_tail[:, b, cols], ident[0:NK - P, 0:NK - P])
            last.then_inc(s.ctxT_ps, 1)
            pe.wait_ge(s.bias_in, 16 * BIASES)
            nc.tensor.transpose(o_ps[:, 0:E * FC], b1_raw, ident[0:E * FC, 0:E * FC]).then_inc(s.b1T_ps, 1)
            pe.wait_ge(s.wsplit, 11)
            for b in range(B):
                for ch in range(NC):
                    k0, h0 = ch * P % NK, ch * P // NK
                    o = (ch % (NC // 2)) * 32
                    bank = ps[:, v_bank(b, ch // (NC // 2)), :]
                    for o, w in ((o, 32),) if h0 + 1 < H else ((o, DH), (o + DH, DH)):
                        for c in range(DC):
                            for a, z in THREE:
                                mm(bank[:, o:o + w], ctxT[:, a, c, b, k0:k0 + P], wva[:, z, c, h0 * DH:h0 * DH + w],
                                   c == 0 and (a, z) == (0, 0), False)
                        for z in range(2):
                            last = mm(bank[:, o:o + w], c16[0:1, H_BV:H_BV + P],
                                      bvr[0:1, z * D + h0 * DH:z * D + h0 * DH + w], False, z == 1)
                last.then_inc(s.v_ps, 1)

            pe.wait_ge(s.wsplit, 10)
            for b in range(B):
                for g in range(G):
                    n = b * G + g
                    dst = k_bank[n % 2]
                    wait(pe, s.k_aff, n - 1)
                    for c in range(DC):
                        for a, z in THREE:
                            last = mm(dst[:, 0:NK], wka[:, a, c, g * HG:(g + 1) * HG, :].rearrange("p h d -> p (h d)"),
                                      ctxT[:, z, c, b, 0:NK], c == 0 and (a, z) == (0, 0), c == 1 and (a, z) == (1, 0))
                    last.then_inc(s.k_ps, 1)
            def transposes(i, v, par):
                pe.wait_ge(s.p_done, i * G + group_of_unit(v) + 1)
                wait(pe, s.pt_lo, i * NU + v - 1)
                for n in range(4):
                    c = 4 * v + n
                    last = nc.tensor.transpose(pt_ps[(v + par) % 2][:, n * P:(n + 1) * P], probs[:, c * P:(c + 1) * P], ident)
                last.then_inc(s.t_ps, 1)

            def scores(i, g, par):
                pe.wait_ge(s.q_lo, i + 1)
                wait(pe, s.p_done, i * G + g - 1)
                for n in range(2):
                    for a, z in THREE:
                        last = mm(score_ps[g % 2][:, n, 0:PAIR], qs[:, par, a, g * P:(g + 1) * P],
                                  kbd[:, z, par, g, n * PAIR:(n + 1) * PAIR], (a, z) == (0, 0), (a, z) == (1, 0))
                last.then_inc(s.s_ps, 1)

            def mix(i, v, par):
                pe.wait_ge(s.pt_lo, i * NU + v + 1)
                if v == 0:
                    wait(pe, s.o_norm, i)
                for n in range(4):
                    c = 4 * v + n
                    h0 = c * P // NK
                    two = (c * P + P - 1) // NK > h0 and h0 + 1 < H
                    w = 2 * DV if two else DV
                    for a, z in THREE:
                        last = mm(o_ps[:, h0 * DV:h0 * DV + w], pt[:, v, a, n * P:(n + 1) * P],
                                  vs[:, z, par, c, :, :].rearrange("p h d -> p (h d)")[:, 0:w],
                                  c == 0 and (a, z) == (0, 0), c == NC - 1 and (a, z) == (1, 0), True)
                last.then_inc(s.m_done, 1)

            def turn(i, par):
                f1, f2, sc, mt, b1, b2, b3 = stages(i)
                q = 1 - par
                if sc is not None:
                    scores(sc, 0, q)
                if mt is not None:
                    transposes(mt, 1, par)
                if b1 is not None:
                    mix(b1, NU - 1, q)
                wait(pe, s.x2_done, upto(i - 2))
                if isinstance(i, int):
                    wait(pe, s.q_lo, min(i + 2, NT))
                if b3 is not None:
                    pe.wait_ge(s.x2T_done, b3 + 1)
                    for c in range(DC):
                        for a, z in THREE:
                            last = mm(misc[:, 0:E], x2T[:, (2 * a + c) * P:(2 * a + c + 1) * P], wgs[:, z, c, :],
                                      c == 0 and (a, z) == (0, 0), c == 1 and (a, z) == (1, 0))
                    last.then_inc(s.lg_ps, 1)
                if sc is not None:
                    scores(sc, 1, q)
                if mt is not None:
                    transposes(mt, 2, par)
                if b1 is not None:
                    pe.wait_ge(s.o_norm, b1 + 1)
                    wait(pe, s.lg_d, b3 + 1 if b3 is not None else 0)
                    for c in range(DC):
                        last = nc.tensor.transpose(misc[:, c * P:(c + 1) * P], o32[:, c * P:(c + 1) * P], ident)
                    last.then_inc(s.oT_ps, 1)
                if mt is not None:
                    mix(mt, 0, par)
                if sc is not None:
                    scores(sc, 2, q)
                if mt is not None:
                    transposes(mt, 3, par)
                if mt is not None:
                    mix(mt, 1, par)
                if b3 is not None:
                    pe.wait_ge(s.sel_d, b3 + 1)
                    wait(pe, s.cum_d, b3)
                    wait(pe, s.lg_d, b3 + 1)
                if b1 is not None:
                    pe.wait_ge(s.oT_lo, b1 + 1)
                if b3 is not None:
                    mm(misc[:, D:D + E], tri16, sel[:], True, False)
                    mm(misc[:, D:D + E], one16, cum[:, q, :], False, False)
                    mm(misc[:, D:D + E], one16[0:1, :], c16[0:1, H_BASE:H_BASE + E], False, True).then_inc(s.rk_ps, 1)
                if f2 is not None:
                    pe.wait_ge(s.xn_done, f2 + 1)
                    for c in range(DC):
                        last = nc.tensor.transpose(misc[:, c * P:(c + 1) * P], xn[:, c * P:(c + 1) * P], ident)
                    last.then_inc(s.xnT_ps, 1)
                if sc is not None:
                    scores(sc, 3, q)
                if mt is not None:
                    transposes(mt, 4, par)
                if mt is not None:
                    mix(mt, 2, par)
                if f2 is not None:
                    pe.wait_ge(s.xnT_lo, f2 + 1)
                    if b3 is not None:
                        pe.wait_ge(s.ohr_d, b3 + 1)
                    for g in range(G):
                        for c in range(DC):
                            for a, z in THREE:
                                mm(misc[:, g * P:(g + 1) * P],
                                   wqa[:, a, c, g * HG:(g + 1) * HG, :].rearrange("p h d -> p (h d)"),
                                   xnT[:, z, c * P:(c + 1) * P], c == 0 and (a, z) == (0, 0), False)
                        last = mm(misc[:, g * P:(g + 1) * P], c16[0:1, H_ROW:H_ROW + P], c16[0:1, H_BV:H_BV + P], False, True)
                    last.then_inc(s.q_ps, 1)
                if sc is not None:
                    transposes(sc, 0, q)
                if mt is not None:
                    mix(mt, 3, par)
                if b3 is not None:
                    wait(pe, s.ohr_d, b3 + 1)
                if b1 is not None or b2 is not None:
                    wait(pe, s.q_lo, upto(i + 2))
                if b2 is not None:
                    pe.wait_ge(s.xs_lo, b2 + 1)
                    for n in range(4):
                        last = nc.tensor.transpose(misc16[:, 2 * D + n * P:2 * D + (n + 1) * P], rows[:, par, n * P:(n + 1) * P], ident16)
                    last.then_inc(s.x2T_ps, 1)
                if b1 is not None:
                    pe.wait_ge(s.oT_lo, b1 + 1)
                    for c in range(DC):
                        for a, z in THREE:
                            last = mm(misc[:, 0:D], oT[:, a, c * P:(c + 1) * P], wos[:, z, c, :],
                                      c == 0 and (a, z) == (0, 0), c == 1 and (a, z) == (1, 0))
                    last.then_inc(s.pr_ps, 1)

            pe.wait_ge(s.wsplit, 15)
            pe.wait_ge(s.k_lo, B * G)
            pe.wait_ge(s.v_done, 2 * B)
            pe.wait_ge(s.b1T_done, 1)
            pe.wait_ge(s.z_cum, 1)
            turns(turn, pe.Fori)
            pe.wait_ge(s.cum_d, NT)
            mm(misc[:, 0:E], one16, cum[:, 0, :], True, True).then_inc(s.cnt_ps, 1)

            pe.wait_ge(s.sched_done, 1)

            def turn_rows(t, slot):
                pe.wait_ge(S[f"xt_in{slot}"], per_block(t, slot) + 16)
                wait(pe, s.xT_done, t - 1)
                for n in range(4):
                    last = nc.tensor.transpose(xT_ps[slot % 2][:, n * P:(n + 1) * P], xt[slot][:, n * P:(n + 1) * P], ident16)
                last.then_inc(s.xT_ps_d, 1)

            def up(t, f, w1e, par):
                m = f // 4
                if f == 0:
                    pe.wait_ge(s.xT_done, t + 1)
                    wait(pe, s.h_done, 2 * (t - 1))
                for c in range(DC):
                    for a, z in THREE:
                        last = mm(h_ps[par][m][:, (f % 4) * P:(f % 4 + 1) * P], w1e[:, a, c * F + f * P:c * F + (f + 1) * P],
                                  xT[par][:, (2 * z + c) * P:(2 * z + c + 1) * P],
                                  c == 0 and (a, z) == (0, 0), c == 1 and (a, z) == (1, 0))
                if f % 4 == 3:
                    last.then_inc(s.h_ps_d, 1)

            def down(t, c, w2e, par):
                if c == 0:
                    wait(pe, s.yb_d, 2 * (t - 1))
                if c % 4 == 0:
                    pe.wait_ge(s.hh_lo, 2 * t + c // 4 + 1)
                mm(y_ps[par], hh[par][:, 0, c * P:(c + 1) * P], w2e[:, 2 * c * D:2 * (c + 1) * D], c == 0, False)
                last = mm(y_ps[par][:, 0:D], hh[par][:, 1, c * P:(c + 1) * P], w2e[:, 2 * c * D:(2 * c + 1) * D], False, c == FC - 1)
                if c == FC - 1:
                    last.then_inc(s.y_ps_d, 1)

            pe.wait_ge(s.w_lo0, UNITS // 2)
            pe.wait_ge(s.w_lo1, UNITS // 2)
            def step(t, slot, e):
                if not isinstance(t, int) or t + 2 < NBLK:
                    turn_rows(t + 2, (slot + 2) % 4)
                ahead = not isinstance(t, int) or 0 <= t + 1 < NBLK
                here = not isinstance(t, int) or t >= 0
                if ahead:
                    w1e = wts[:, ds(e[1], 1), 0:2, :].rearrange("p o a k -> p (o a) k")
                if here:
                    w2e = wts[:, ds(e[0], 1), 2:4, :].rearrange("p o a k -> p (o a k)")
                for f in range(FC):
                    if ahead:
                        up(t + 1, f, w1e, 1 - slot % 2)
                    if here:
                        down(t, f, w2e, slot % 2)

            blocks(step, pe, -2, 1)


_NAMES = ["x", "ctx_1024", "L0_xattn_Wq", "L0_xattn_bq", "L0_xattn_Wkv", "L0_xattn_bkv", "L0_xattn_Wo", "L0_xattn_bo",
          "L0_ffn_Wg", "L0_ffn_bg", "L0_ffn_W1", "L0_ffn_b1", "L0_ffn_W2", "L0_ffn_b2"]


def kernel(**inputs):
    import concourse.bacc as bacc
    from concourse.bass_utils import run_bass_kernel_spmd

    nc = bacc.Bacc("TRN2", target_bir_lowering=False, num_devices=1)
    arrays, args = {}, []
    c32, c16, ids = constants()
    for name, a in [(n, np.ascontiguousarray(inputs[n])) for n in _NAMES] + [("c32", c32), ("c16", c16), ("ids", ids)]:
        arrays[f"in_{name}"] = a
        args.append(nc.dram_tensor(f"in_{name}", a.shape, mybir.dt.from_np(a.dtype), kind="ExternalInput").ap())
    args.append(nc.dram_tensor("out_0", (B, NQ, D), mybir.dt.float32, kind="ExternalOutput").ap())
    program(nc, *args)
    result = run_bass_kernel_spmd(nc, [arrays], core_ids=[0])
    return result.results[0]["out_0"]
```

```python
import math
from contextlib import ExitStack

import numpy as np

import concourse.bass as bass
from concourse import mybir

P = 128
B, NQ, NK, D = 2, 1024, 154, 256
H, DH = 16, 16
E, F = 8, 1024
NT = B * NQ // P
DC = D // P
HG = 4
G = H // HG
GK = HG * NK
PAIR = 2 * NK
FLAT = H * NK
NC = -(-FLAT // P)
NU = NC // 4
DV = DH + 1
FC = F // P
LIST = B * NQ + P
NBLK = (2 * B * NQ - E) // P + E
SPARE = NBLK - 2 * B * NQ // P
XROWS = E * LIST + SPARE * P
ROW = 2 * D + 8
BIASES = 2 + HG + 4
EARLY = 4
UNITS = E * 4
UNIT_PAIRS = [(0, 0), (0, 1), (1, 0), (1, 1), (2, 0), (2, 1), (3, 1), (4, 1),
              (3, 0), (4, 0), (5, 0), (5, 1), (6, 0), (6, 1), (7, 0), (7, 1)]
EPS = 1e-5
KINK = NQ - NK

SX, SW = 2.0**8, 2.0**8
SCALE = 1 / math.sqrt(DH)
SQ, SK = 2.0**6 * SCALE, 2.0**8
SCTX = 2.0**6
S_SCORE = 2.0**14
S_ROW = 2.0**6
S_P, S_V, S_H = 2.0**8, 2.0**8, 2.0**6
SLOPES = [2.0 ** (-8.0 * (h + 1) / H) for h in range(H)]

C_ID, C_MASK = 0, P
C_SLOPE = C_MASK + 2 * NC
C_IOTA = C_SLOPE + G
C_BLK = C_IOTA + E
C_HALF = C_BLK + NBLK
C_MINUS = C_HALF + 1
C_SW = C_MINUS + 1
C_ROW = C_SW + 1
C_KPOS = C_ROW + HG
C_LE = C_KPOS + NK
C_END = C_LE + E * E
H_ID, H_TRI, H_ONE = 0, P, 2 * P
H_ROW, H_BV, H_BASE, H_END = 3 * P, 4 * P, 5 * P, 5 * P + E
K_END = 6 * P + 8 * NK


def group_of_unit(v):
    return (min(4 * P * (v + 1), FLAT) - 1) // GK


def constants():
    c = np.zeros((P, C_END), np.float32)
    c[:, C_ID:C_ID + P] = np.eye(P)
    k = np.arange(NK)
    for ch in range(NC):
        f = ch * P + np.arange(P)
        h = f // NK
        first = ch * P // NK
        c[:, C_MASK + 2 * ch] = (h == first) & (f < FLAT)
        c[:, C_MASK + 2 * ch + 1] = (h == first + 1) & (f < FLAT)
    for j in range(HG):
        for g in range(G):
            c[32 * j + DH, C_SLOPE + g] = -SLOPES[HG * g + j] * S_ROW
        c[32 * j + DH, C_ROW + j] = 1.0
    c[:, C_KPOS:C_KPOS + NK] = k
    c[:, C_IOTA:C_IOTA + E] = np.arange(E)
    c[:, C_LE:C_LE + E * E] = np.tril(np.ones((E, E))).reshape(-1)
    c[:, C_BLK:C_BLK + NBLK] = np.arange(NBLK)
    c[:, C_HALF] = -0.5
    c[:, C_MINUS] = -1.0
    c[:, C_SW] = SW
    h = np.zeros((P, H_END), np.float16)
    h[:, H_ID:H_ID + P] = np.eye(P)
    h[:, H_TRI:H_TRI + P] = np.triu(np.ones((P, P)), 1)
    h[:, H_ONE:H_ONE + P] = 1.0
    h[0, H_BV:H_BV + P] = 2.0**7
    h[0, H_BASE:H_BASE + E] = np.arange(E) * LIST
    for j in range(HG):
        h[0, H_ROW + 32 * j + DH] = S_SCORE / S_ROW * (SX * SW / SQ) / 2.0**7
    kink = np.zeros((P, K_END), np.float16)
    root = np.float16(math.sqrt(2.0))
    for n, v in enumerate((float(root), math.sqrt(2.0) - float(root), 1.0)):
        for m in range(2):
            kink[:, (2 * n + m) * P:(2 * n + m + 1) * P] = np.eye(P) * v * 2.0 ** (10 - 4 * m)
    for n in range(2):
        u = np.maximum((NQ // P - 2 + n) * P + np.arange(P) - KINK, 0)
        for m in range(4):
            o = 6 * P + (4 * n + m) * NK
            kink[:, o:o + NK] = np.minimum(k[None, :], u[:, None]) * 2.0 ** (4 - m)
    ids = np.zeros((P, NT + 1), np.int32)
    for i in range(NT):
        ids[:, i] = (i % B) * NQ + (i // B) * P + np.arange(P)
    ids[:, NT] = 2 * B * NQ + np.arange(P)
    return c, h, kink, ids


def program(nc, x, ctx_in, wq, bq, wkv, bkv, wo, bo, wg, bg, w1, b1, w2, b2, c32_in, c16_in, kink_in, ids_in, out):
    f32, f16, i32, u32 = mybir.dt.float32, mybir.dt.float16, mybir.dt.int32, mybir.dt.uint32
    ALU = mybir.AluOpType
    ACT = mybir.ActivationFunctionType
    AX = mybir.AxisListType
    ds = bass.ds
    xlist = nc.dram_tensor("xlist", [XROWS, ROW // 2], i32, kind="Internal").ap()
    out_rows = out.rearrange("b n d -> (b n) d")
    x_rows = x.rearrange("b n d -> (b n) d")

    with ExitStack() as ctx:
        def sb(name, shape, dt):
            return ctx.enter_context(nc.sbuf_tensor(name, shape, dt))

        def sem(name):
            return ctx.enter_context(nc.semaphore(name))

        c32 = sb("c32", [P, C_END], f32)
        c16 = sb("c16", [P, H_END], f16)
        ids = sb("ids", [P, NT + 1], i32)
        kinks = sb("kinks", [P, K_END], f16)
        wts = sb("wts", [P, E, 4, 2048], f16)
        stage = sb("stage", [P, 2, 1024], f32)
        b1T = sb("b1T", [P, E * FC], f32)
        pad_rows = sb("pad_rows", [P, ROW], f16)
        sched_f = sb("sched_f", [P, 2, NBLK + 1], f32)
        sched_i = sb("sched_i", [1, 2, NBLK + 1], i32)
        cnt_f = sb("cnt_f", [P, 4, E], f32)
        cnt_i = sb("cnt_i", [P, 3, E], i32)
        ident = c32[:, C_ID:C_ID + P]
        ident16 = c16[:, H_ID:H_ID + P]
        tri16 = c16[:, H_TRI:H_TRI + P]
        one16 = c16[:, H_ONE:H_ONE + P]

        kbd = sb("kbd", [P, 2, B, G, GK], f16)
        after_k = kbd[:].rearrange("p a b g k -> p (a b g k)").bitcast(f32)
        b2bc = after_k[:, 0:E * D]
        block_rows = [after_k[:, E * D + n * ROW // 2:E * D + (n + 1) * ROW // 2] for n in range(4)]
        xt = [b.bitcast(f16)[:, 0:2 * D] for b in block_rows]
        pay = [b[:, D:ROW // 2] for b in block_rows]
        probs = sb("probs", [P, NC * P], f32)
        h32 = [probs[:, n * F:(n + 1) * F] for n in range(2)]
        pt = sb("pt", [P, NU, 2, 512], f16)
        hh = [pt[:].rearrange("p u s k -> p (u s k)")[:, n * 2 * F:(n + 1) * 2 * F].rearrange("p (s k) -> p s k", s=2)
              for n in range(2)]
        qs = sb("qs", [P, 2, 2, G * P], f16)
        xa = sb("xa", [P, 2, D], f32)
        xb = sb("xb", [P, 2, D], f32)
        wos = sb("wos", [P, 2, DC, D], f16)
        wgs = sb("wgs", [P, 2, DC, E], f16)
        kbias = sb("kbias", [P, G], f32)
        fold = sb("fold", [P, G], f32)
        bo_bc = sb("bo_bc", [P, D], f32)
        bg_bc = sb("bg_bc", [P, E], f32)
        o32 = sb("o32", [P, D], f32)
        xn2 = sb("xn2", [P, D], f32)
        rows = sb("rows", [P, 2, ROW], f16)
        oT = sb("oT", [P, 2, D], f16)
        x2T = sb("x2T", [P, 4 * P], f16)
        small = sb("small", [P, 8], f32)
        mx = sb("mx", [P, G, HG], f32)
        nb = sb("nb", [P, G, HG], f32)
        rec = sb("rec", [P, H], f32)
        lg = sb("lg", [P, E], f32)
        m8 = sb("m8", [P, E], f32)
        e8 = sb("e8", [P, E], f32)
        mi = sb("mi", [P, E], u32)
        oh = sb("oh", [P, 2, E], f32)
        ohr = sb("ohr", [P, 2, E], f32)
        pos = sb("pos", [P, 2, 2], i32)
        sel = sb("sel", [P, E], f16)
        cum = sb("cum", [P, 2, E], f16)
        st1, mv1, rs1 = sb("st1", [P, 6], f32), sb("mv1", [P, 2], f32), sb("rs1", [P, 2], f32)
        st2, mv2, rs2 = sb("st2", [P, 6], f32), sb("mv2", [P, 2], f32), sb("rs2", [P, 2], f32)
        xT = [qs[:, n, 0, :] for n in range(2)]
        ysb = [o32, xn2]
        wsel = sb("wsel", [P, 4, 2], f32)
        row_id = sb("row_id", [P, 4], i32)

        at = [0, 0]

        def borrow(e, words16):
            n = e - (E - 2)
            at[n] += words16
            assert at[n] <= 8192
            return wts[:, e, :, :].rearrange("p a k -> p (a k)")[:, at[n] - words16:at[n]]

        def scratch(words16):
            return borrow(E - 2, words16)

        def late(words16):
            return borrow(E - 1, words16)

        wqa = late(2 * DC * H * 32).rearrange("p (s c h d) -> p s c h d", s=2, c=DC, h=H)
        xn = late(2 * D).bitcast(f32)
        xnT = late(2 * D).rearrange("p (s d) -> p s d", s=2)
        late(1024)
        vs = late(2 * B * NC * 2 * DV).rearrange("p (s b c h d) -> p s b c h d", s=2, b=B, c=NC, h=2)

        wka = scratch(2 * DC * 512).rearrange("p (s c h d) -> p s c h d", s=2, c=DC, h=H)
        wva = scratch(2 * DC * D).rearrange("p (s c d) -> p s c d", s=2, c=DC)
        ctxT = scratch(2 * DC * B * PAIR).rearrange("p (s c b k) -> p s c b k", s=2, c=DC, b=B)
        v32 = scratch(NC * 32 * 2).bitcast(f32)
        bvr = scratch(2 * D)
        bvf = scratch(2 * D).bitcast(f32)
        raw = pt[:].rearrange("p u s k -> p (u s k)").bitcast(f32)
        wq_raw = raw[:, 0:512].rearrange("p (c n) -> p c n", c=DC)
        wkv_raw = raw[:, 512:1536].rearrange("p (c n) -> p c n", c=DC)
        wo_raw = raw[:, 1536:2048].rearrange("p (c n) -> p c n", c=DC)
        wg_raw = raw[:, 2048:2064].rearrange("p (c n) -> p c n", c=DC)
        ctx_main = probs[:, 0:512].rearrange("p (b d) -> p b d", b=B)
        ctx_tail = probs[0:NK - P, 512:1024].rearrange("p (b d) -> p b d", b=B)
        b1_raw = probs[0:E * FC, 1024:1024 + P]
        bk_bc, bq_bc, prod = (probs[:, 1152 + n * D:1152 + (n + 1) * D] for n in range(3))
        k32 = [probs[:, 1920 + n * NK:1920 + (n + 1) * NK] for n in range(3)]

        ps = ctx.enter_context(nc.psum_tensor("ps", [P, 8, 512], f32))
        score_ps = [ps[:, 2 * n:2 * n + 2, :] for n in range(2)]
        pt_ps, o_ps, misc = [ps[:, 4, :], ps[:, 7, :]], ps[:, 5, :], ps[:, 6, :]
        k_bank = [misc, ps[:, 7, :]]
        misc16 = ps[:, 6, :].bitcast(f16)
        h_ps = [[ps[:, 2 * n + m, :] for m in range(2)] for n in range(2)]
        y_ps = [ps[:, 4, :], ps[:, 5, :]]
        xT_ps = [ps[:, 6, :].bitcast(f16)[:, 0:512], ps[:, 7, :].bitcast(f16)[:, 0:512]]

        S = {n: sem(n) for n in """c_in ctx_in w_in bias_in z_bias z_pad z_cum z_kbd z_set padid x_in0 x_in1 xb_in0 xb_in1 list_init
            ctxT_ps k_ps k_aff k_hi k_lo k_row k_fold v_ps v_mask v_hi v_done b1T_ps b1T_done wsplit_hi wsplit
            w_stage0 w_stage1 w_scaled w_hi w_lo0 w_lo1 apart
            st1_d mv1_d ve1_d rstd1 xn_done xnT_ps xnT_hi xnT_lo q_ps q_hi q_lo
            s_ps kink_in mx_d nb_d p_done t_ps pt_hi pt_lo m_done rec_d o_norm oT_ps oT_hi oT_lo pr_ps xb_bo x2_done x2_out0 x2_out1
            st2_d mv2_d ve2_d rstd2 xn2_done xs_hi xs_lo x2T_ps x2T_done lg_ps lg_d m8_d mi_d nm_d e8_d oh_d sel_d
            cum_d rk_ps ohr_d pos_d gates tail_d scat0 scat1
            cnt_ps sched sched_done n_done pads b2_in
            xt_in0 xt_in1 xt_in2 xt_in3 xT_ps_d xT_done h_ps_d h_done hh_hi hh_lo y_ps_d yb_d wa_d wb_d ex_d y_done added""".split()}
        s = type("Sems", (), S)

        def wait(eng, semaphore, value):
            if not isinstance(value, int) or value > 0:
                eng.wait_ge(semaphore, value)

        def wait_alone(eng, semaphore, value):
            if not isinstance(value, int):
                eng.wait_ge(semaphore, value).then_inc(s.apart, 1)
            elif value > 0:
                eng.wait_ge(semaphore, value)

        def per_tile(i, par, each):
            return each * (i // 2) if isinstance(i, int) else each // 2 * (i - par)

        def turns(turn, loop, first=-3):
            for i in range(first, 5):
                turn(i, i % 2)
            with loop(5, 11, 2) as i:
                turn(i, 1)
                turn(i + 1, 0)
            for i in range(11, NT + 3):
                turn(i, i % 2)

        def tile(t):
            return t if not isinstance(t, int) or 0 <= t < NT else None

        def stages(i):
            return [tile(i + n) for n in (3, 2, 1, 0, -1, -2, -3)]

        def upto(t):
            return min(max(t + 1, 0), NT) if isinstance(t, int) else t + 1

        def first_row(i, par):
            return (i % B) * NQ + (i // B) * P if isinstance(i, int) else par * NQ + (i - par) * (P // B)

        def pooled(u):
            return u < EARLY + 2 or u < 16 and u % 2 == 1 or 16 <= u < 24 or u in (25, 27)

        class Unit:
            def __init__(self, u, n, place, second, twice_before, pool, scaled):
                self.u, self.n, self.place, self.second, self.twice_before, self.pool, self.scaled = \
                    u, n, place, second, twice_before, pool, scaled

        def numbered(u):
            expert, second = UNIT_PAIRS[u // 2]
            return Unit(u, u % 2, 2 * expert, second, u - u % 2, pooled(u), sum(pooled(v) for v in range(u)))

        def weight_units(i, par):
            if not isinstance(i, int):
                n = 1 - par
                return [Unit(i + 11, n, i + par, 0, i + 11 - n, True, i + 6)]
            first, count = ((EARLY + 2 + i, 1) if i in (-2, -1) else (6 + 2 * i, 2) if 0 <= i < 5 else
                            (i + 11, 1) if 5 <= i < 13 else (24 + 2 * (i - 13), 2) if 13 <= i < 17 else (0, 0))
            return [numbered(u) for u in range(first, first + count)]

        def units_at(i, par, slot):
            return weight_units(i, par)[slot - 3:slot - 2] if slot in (3, 4) else []

        def unit_place(unit, lo):
            twice, second, n = unit.place, unit.second, unit.n
            flat = wts[:].rearrange("p e a k -> p (e a k)")
            if second:
                return flat[:, ds(twice * 4096 + 4096 + n * 2048, 2048)].rearrange("p (c s d) -> p c s d", c=4, s=2)[:, :, lo, :]
            return flat[:, ds(twice * 4096 + lo * 2048 + n * 1024, 1024)].rearrange("p (c k) -> p c k", c=4)

        def staged(unit):
            return stage[:, unit.n, :].rearrange("p (c k) -> p c k", c=4)

        def v_bank(b, half):
            return 2 * half + b

        def v_parts(n):
            chunks = slice((n % 2) * (NC // 2), (n % 2 + 1) * (NC // 2))
            return (v32.rearrange("p (n c h d) -> p n c h d", n=2, h=2, d=DH)[:, n % 2],
                    lambda w: vs[:, w, n // 2, chunks, :, 0:DH])

        def per_block(t, slot):
            return 16 * (t // 4) if isinstance(t, int) else 4 * (t - slot)

        def experts(eng, t, n):
            first = max(t, 0) if isinstance(t, int) else t
            n = min(t + n, NBLK) - first if isinstance(t, int) else n
            _, values = nc.values_load_multi_w_load_instructions(sched_i[0:1, 1, ds(first, n)], engines=[eng.engine],
                                                                 min_val=0, max_val=E - 1,
                                                                 skip_runtime_bounds_check_because="the schedule holds no more than E - 1")
            return [None] * (first - t if isinstance(t, int) else 0) + list(values)

        def blocks(step, eng, first, ahead=None, size=4):
            def group(t, n, slot):
                known = None if ahead is None else experts(eng, t, n + ahead)
                for k in range(n):
                    step(t + k, (slot + k) % 4, *([] if ahead is None else [known[k:]]))

            group(first, 3 - first, first % 4)
            with eng.Fori(3, NBLK - 3 - size, size) as t:
                group(t, size, 3)
            group(NBLK - 4, 4, 3)

        def pad_lists(eng, which):
            eng.wait_ge(s.n_done, 1)
            eng.wait_ge(s.padid, 1)
            _, lengths = nc.values_load_multi_w_load_instructions(cnt_i[0:1, 0, which[0]:which[-1] + 1], engines=[eng.engine],
                                                                  min_val=0, max_val=B * NQ,
                                                                  skip_runtime_bounds_check_because="a list's length")
            for e, length in zip(which, lengths):
                eng.dma_start(xlist[ds(length + e * LIST, P), :], pad_rows[:].bitcast(i32)).then_inc(s.pads, 16)

        block = ctx.enter_context(nc.Block())

        @block.sync
        def _(sp):
            sp.dma_start(c32[:], c32_in).then_inc(s.c_in, 16)
            sp.dma_start(ctx_main, ctx_in[:, 0:P, :].rearrange("b k d -> k b d")).then_inc(s.ctx_in, 16)
            sp.dma_start(ctx_tail, ctx_in[:, P:NK, :].rearrange("b k d -> k b d")).then_inc(s.ctx_in, 16)
            sp.dma_start(c16[:], c16_in).then_inc(s.c_in, 16)
            sp.dma_start(ids[:], ids_in).then_inc(s.c_in, 16)
            sp.dma_start(wkv_raw, wkv.rearrange("(c p) n -> p c n", p=P)).then_inc(s.w_in, 16)
            sp.dma_start(wq_raw, wq.rearrange("(c p) n -> p c n", p=P)).then_inc(s.w_in, 16)
            sp.dma_start(wo_raw, wo.rearrange("(c p) n -> p c n", p=P)).then_inc(s.w_in, 16)
            sp.dma_start(wg_raw, wg.rearrange("(c p) n -> p c n", p=P)).then_inc(s.w_in, 16)
            sp.dma_start(bvf[0:1, :], bkv[D:2 * D].rearrange("(o n) -> o n", o=1)).then_inc(s.bias_in, 16)
            sp.dma_start(b1_raw, b1.rearrange("e (c p) -> (e c) p", p=P)).then_inc(s.bias_in, 16)
            sp.wait_ge(s.z_bias, 1)
            with nc.allow_non_contiguous_dma(reason="bias columns"):
                for j in range(HG):
                    part = slice(32 * j, 32 * j + DH)
                    sp.dma_start(kbias[part, :], bkv[0:D].rearrange("(g j d) -> j d g", j=HG, d=DH)[j]).then_inc(s.bias_in, 16)
            sp.dma_start(bq_bc, bq.rearrange("(o n) -> o n", o=1).to_broadcast([P, D])).then_inc(s.bias_in, 16)
            sp.dma_start(bk_bc, bkv[0:D].rearrange("(o n) -> o n", o=1).to_broadcast([P, D])).then_inc(s.bias_in, 16)
            sp.dma_start(bo_bc[:], bo.rearrange("(o n) -> o n", o=1).to_broadcast([P, D])).then_inc(s.bias_in, 16)
            sp.dma_start(bg_bc[:], bg.rearrange("(o n) -> o n", o=1).to_broadcast([P, E])).then_inc(s.bias_in, 16)

            def load_a(i, par):
                wait_alone(sp, s.xn_done, i - 1)
                sp.dma_start(xa[:, par, :], x_rows[ds(first_row(i, par), P), :]).then_inc(S[f"x_in{par}"], 16)

            def store(i, par):
                wait_alone(sp, s.x2_done, i + 1)
                sp.dma_start(out_rows[ds(first_row(i, par), P), :], xb[:, par, :]).then_inc(S[f"x2_out{par}"], 16)

            def load_b(i, par):
                wait_alone(sp, s.xn2_done, i - 1)
                wait_alone(sp, S[f"x2_out{par}"], per_tile(i, par, 16))
                sp.dma_start(xb[:, par, :], x_rows[ds(first_row(i, par), P), :]).then_inc(S[f"xb_in{par}"], 16)

            def load_second_biases():
                sp.wait_ge(s.s_ps, G * NT)
                sp.dma_start(b2bc, b2.rearrange("(o e) d -> o (e d)", o=1).to_broadcast([P, E * D])).then_inc(s.b2_in, 16)

            def load_w(unit):
                twice, second, n = unit.place, unit.second, unit.n
                wait_alone(sp, S[f"w_lo{n}"], unit.twice_before)
                if second:
                    src = w2.rearrange("e f d -> (e f) d")[ds(twice * 512 + n * 512, 512), :].rearrange("(c p) d -> p c d", p=P)
                    sp.dma_start(staged(unit), src).then_inc(S[f"w_stage{n}"], 16)
                else:
                    src = w1.rearrange("e d f -> (e d) f")[ds(twice * P + n * P, P), :]
                    sp.dma_start(stage[:, n, :], src).then_inc(S[f"w_stage{n}"], 16)

            load_a(0, 0)
            load_a(1, 1)
            for u in range(2):
                load_w(numbered(u))
            sp.wait_ge(s.padid, 1)
            for n in range(SPARE):
                sp.dma_start(xlist[E * LIST + n * P:E * LIST + (n + 1) * P, :], pad_rows[:].bitcast(i32)).then_inc(s.list_init, 16)

            def turn(i, par):
                f1, f2, sc, mt, b1, b2, b3 = stages(i)
                for u in weight_units(i, par):
                    load_w(u)
                if tile(i + 4) is not None and not (isinstance(i, int) and i == -3):
                    load_a(i + 4, par)
                if b2 is not None:
                    store(b2, par)
                if mt is not None:
                    load_b(mt, par)
                if isinstance(i, int) and i == 15:
                    load_second_biases()

            for u in range(2, EARLY):
                load_w(numbered(u))
            sp.dma_start(kinks[:], kink_in).then_inc(s.kink_in, 16)
            turns(turn, sp.Fori)
            sp.wait_ge(s.list_init, 16 * SPARE)
            pad_lists(sp, range(0, E // 2))
            sp.wait_ge(s.scat0, 16 * NT)
            sp.wait_ge(s.scat1, 16 * NT)
            sp.wait_ge(s.pads, 16 * E)
            sp.wait_ge(s.sched_done, 1)

            def load_block(t, slot):
                _, (r,) = nc.values_load_multi_w_load_instructions(sched_i[0:1, 0, ds(t, 1)], engines=[sp.engine], min_val=0, max_val=XROWS - P,
                                                                   skip_runtime_bounds_check_because="a block of a list or of the spare rows")
                wait_alone(sp, s.xT_ps_d, t - 3)
                wait_alone(sp, s.ex_d, t - 3)
                sp.dma_start(block_rows[slot].bitcast(i32), xlist[ds(r, P), :]).then_inc(S[f"xt_in{slot}"], 16)

            blocks(lambda t, slot: load_block(t + 4, slot) if not isinstance(t, int) or t + 4 < NBLK else None, sp, -4)
            sp.wait_ge(s.added, 16 * NBLK)

        @block.gpsimd
        def _(pool):
            pool.memset(kbias[:], 0.0).then_inc(s.z_bias, 1)
            pool.memset(pad_rows[:], 0.0).then_inc(s.z_pad, 1)
            pool.memset(kbd[:].bitcast(u32), 0).then_inc(s.z_kbd, 1)
            pool.memset(cum[:], 0.0).then_inc(s.z_cum, 1)
            pool.wait_ge(s.c_in, 48)
            pool.wait_ge(s.z_pad, 1)
            pool.tensor_copy(pad_rows[:, 2 * D:2 * D + 2].bitcast(i32), ids[:, NT:NT + 1]).then_inc(s.padid, 1)

            def rstd(i, rs, done, ve_sem):
                pool.wait_ge(ve_sem, i + 1)
                pool.tensor_tensor(rs[:, 1:2], rs[:, 0:1], c32[:, C_HALF:C_HALF + 1], ALU.pow).then_inc(done, 1)

            def scale_w(u):
                pool.wait_ge(S[f"w_stage{u.n}"], 8 * u.twice_before + 16)
                pool.tensor_tensor(stage[:, u.n, :], stage[:, u.n, :], c32[:, C_SW:C_SW + 1].to_broadcast([P, 1024]), ALU.mult).then_inc(s.w_scaled, 1)

            def split_w_lo(u):
                wait_alone(pool, s.w_hi, u.u + 1)
                pool.tensor_tensor(unit_place(u, 1), staged(u), unit_place(u, 0), ALU.subtract).then_inc(S[f"w_lo{u.n}"], 2)

            def weights_of(i, q):
                words = rows[:, q, 2 * D:ROW]
                z, zsum = e8[:, 1:2], small[:, 1:2]
                pool.tensor_copy(words[:, 0:2].bitcast(i32), ids[:, ds(i, 1)]).then_inc(s.tail_d, 1)
                wait_alone(pool, s.e8_d, i + 1)
                pool.tensor_scalar(small[:, 2:3], zsum, 1e-8, 1.0, ALU.mult, ALU.add).then_inc(s.gates, 1)
                pool.tensor_copy(words[:, 2:4].bitcast(f32), mi[:, 0:1]).then_inc(s.tail_d, 1)
                pool.wait_ge(s.gates, 4 * i + 1)
                pool.tensor_tensor(small[:, 3:4], small[:, 2:3], z, ALU.add).then_inc(s.gates, 1)
                pool.wait_ge(s.gates, 4 * i + 2)
                pool.tensor_tensor(small[:, 4:5], small[:, 3:4], c32[:, C_MINUS:C_MINUS + 1], ALU.pow).then_inc(s.gates, 1)
                pool.wait_ge(s.gates, 4 * i + 3)
                pool.tensor_tensor(words[:, 6:8].bitcast(f32), small[:, 4:5], z, ALU.mult).then_inc(s.gates, 1)
                pool.wait_ge(s.gates, 4 * i + 4)
                pool.tensor_tensor(words[:, 4:6].bitcast(f32), small[:, 4:5], words[:, 6:8].bitcast(f32), ALU.subtract).then_inc(s.tail_d, 1)

            def rows_lo(i, q):
                pool.wait_ge(s.xs_hi, i + 1)
                pool.tensor_tensor(rows[:, q, D:2 * D], xn2[:], rows[:, q, 0:D], ALU.subtract).then_inc(s.xs_lo, 1)

            def dispatch(i, q):
                wait_alone(pool, s.xs_lo, i + 1)
                wait_alone(pool, s.tail_d, 3 * (i + 1))
                wait_alone(pool, s.pos_d, i + 1)
                for c in range(2):
                    pool.indirect_dma_start(
                        out=xlist, out_offset=bass.IndirectOffsetOnAxis(ap=pos[:, q, c:c + 1], axis=0),
                        in_=rows[:, q, :].bitcast(i32), in_offset=None).then_inc(S[f"scat{q}"], 16)

            def turn(i, par):
                f1, f2, sc, mt, b1, b2, b3 = stages(i)
                units = [u for u in weight_units(i, par) if u.pool]
                if b2 is not None:
                    rstd(b2, rs2, s.rstd2, s.ve2_d)
                if b1 is not None:
                    pool.wait_ge(S[f"xb_in{1 - par}"], per_tile(b1, 1 - par, 16) + 16)
                    pool.tensor_tensor(xb[:, 1 - par, :], xb[:, 1 - par, :], bo_bc[:], ALU.add).then_inc(s.xb_bo, 1)
                for u in units:
                    scale_w(u)
                if f1 is not None:
                    rstd(f1, rs1, s.rstd1, s.ve1_d)
                last = isinstance(i, int) and i == NT + 1
                if last:
                    rows_lo(b2, par)
                if b3 is not None:
                    weights_of(b3, 1 - par)
                if b2 is not None and not last:
                    rows_lo(b2, par)
                if b3 is not None:
                    dispatch(b3, 1 - par)
                for u in units:
                    split_w_lo(u)

            scale_w(numbered(0))
            for u in range(1, EARLY):
                scale_w(numbered(u))
                split_w_lo(numbered(u - 1))
            turn(-3, 1)
            split_w_lo(numbered(EARLY - 1))
            pool.wait_ge(s.bias_in, 16 * BIASES)
            turns(turn, pool.Fori, -2)
            pool.wait_ge(s.x2_out0, 8 * NT)
            pool.wait_ge(s.x2_out1, 8 * NT)

            def add_block(t, slot):
                wait_alone(pool, s.y_done, t + 1)
                wait_alone(pool, s.added, 16 * t)
                pool.indirect_dma_start(
                    out=out_rows, out_offset=bass.IndirectOffsetOnAxis(ap=row_id[:, slot:slot + 1], axis=0),
                    in_=ysb[slot % 2][:], in_offset=None, bounds_check=B * NQ - 1, oob_is_err=False,
                    compute_op=ALU.add).then_inc(s.added, 16)

            blocks(add_block, pool, 0)
            pool.wait_ge(s.added, 16 * NBLK)

        @block.scalar
        def _(act):
            def split_w_hi(u):
                if u.pool:
                    act.wait_ge(s.w_scaled, u.scaled + 1)
                else:
                    act.wait_ge(S[f"w_stage{u.n}"], 8 * u.twice_before + 16)
                if isinstance(u.u, int) and u.u == UNITS - 4:
                    act.wait_ge(s.q_ps, NT)
                if isinstance(u.u, int) and u.u == UNITS - 2:
                    act.wait_ge(s.m_done, NU * NT)
                nc.scalar.activation(unit_place(u, 0), staged(u), ACT.Copy, scale=1.0 if u.pool else SW).then_inc(s.w_hi, 1)

            for u in range(2):
                split_w_hi(numbered(u))
            act.wait_ge(s.z_kbd, 1)
            act.wait_ge(s.k_fold, 2 * DC + 6)

            def k_affine(n):
                act.wait_ge(s.k_ps, n + 1)
                wait(act, s.k_lo, n - 2)
                nc.scalar.activation(k32[n % 3], k_bank[n % 2][:, 0:NK], ACT.Identity, bias=kbias[:, n % G:n % G + 1],
                                     scale=SK / (SCTX * SW)).then_inc(s.k_aff, 1)

            for n in range(2):
                k_affine(n)
            for b in range(B):
                for g in range(G):
                    n = b * G + g
                    act.wait_ge(s.k_row, n + 1)
                    for j in range(HG):
                        part = slice(32 * j, 32 * j + 32)
                        last = nc.scalar.copy(kbd[part, 0, b, g, j * NK:(j + 1) * NK], k32[n % 3][part, :])
                    last.then_inc(s.k_hi, 1)
                    if n + 2 < B * G:
                        k_affine(n + 2)
                    if n % G == G - 1:
                        split_w_hi(numbered(2 + b))
            def values_hi():
                for n in range(2 * B):
                    act.wait_ge(s.v_mask, n + 1)
                    vm, vh = v_parts(n)
                    nc.scalar.copy(vh(0), vm).then_inc(s.v_hi, 1)

            def pt_hi(i, v, par):
                act.wait_ge(s.t_ps, i * NU + v + 1)
                wait(act, s.m_done, (i - 1) * NU + v + 1)
                nc.scalar.copy(pt[:, v, 0, :], pt_ps[(v + par) % 2]).then_inc(s.pt_hi, 1)

            def exps(i, g):
                act.wait_ge(s.nb_d, i * G + g + 1)
                wait(act, s.t_ps, (i - 1) * NU + min((g + 1) * GK - 1, FLAT - 1) // 512 + 1)
                for j in range(HG):
                    last = nc.scalar.activation(probs[:, (g * HG + j) * NK:(g * HG + j + 1) * NK],
                                                score_ps[g % 2][:, j // 2, (j % 2) * NK:(j % 2 + 1) * NK],
                                                ACT.Exp, bias=nb[:, g, j:j + 1], scale=1.0 / S_SCORE)
                last.then_inc(s.p_done, 1)

            def turn(i, par):
                f1, f2, sc, mt, b1, b2, b3 = stages(i)
                for slot in range(5):
                    if mt is not None:
                        pt_hi(mt, slot, par)
                    if b3 is not None and slot == 0:
                        act.wait_ge(s.x2T_ps, b3 + 1)
                        act.wait_ge(s.x2_done, upto(i - 2))
                        nc.scalar.copy(x2T[:], misc16[:, 2 * D:4 * D]).then_inc(s.x2T_done, 1)
                    if b1 is not None and slot == 2:
                        act.wait_ge(s.oT_ps, b1 + 1)
                        wait(act, s.pr_ps, b1)
                        nc.scalar.copy(oT[:, 0, :], misc[:, 0:D]).then_inc(s.oT_hi, 1)
                    if f2 is not None and slot == 3:
                        act.wait_ge(s.xnT_ps, f2 + 1)
                        wait(act, s.q_ps, f2)
                        nc.scalar.copy(xnT[:, 0, :], misc[:, 0:D]).then_inc(s.xnT_hi, 1)
                    if isinstance(i, int) and i == -2 and slot == 4:
                        values_hi()
                    early = isinstance(i, int) and i < 0
                    if slot == 4 and not early:
                        for u in units_at(i, par, 3):
                            split_w_hi(u)
                    if f2 is not None and slot == 4:
                        act.wait_ge(s.q_ps, f2 + 1)
                        nc.scalar.activation(qs[:, par, 0, :], misc, ACT.Copy, scale=SQ / (SX * SW)).then_inc(s.q_hi, 1)
                    if sc is not None and slot > 0:
                        exps(sc, slot - 1)
                    if b3 is not None and slot == 2:
                        act.wait_ge(s.nm_d, b3 + 1)
                        wait(act, s.tail_d, 3 * b3)
                        nc.scalar.activation(e8[:], m8[:], ACT.Exp, bias=small[:, 0:1], accum_out=small[:, 1:2]).then_inc(s.e8_d, 1)
                    if b2 is not None and slot == 3:
                        act.wait_ge(s.xn2_done, b2 + 1)
                        wait(act, S[f"scat{par}"], per_tile(b2, par, 32))
                        nc.scalar.copy(rows[:, par, 0:D], xn2[:]).then_inc(s.xs_hi, 1)
                    if slot == 4:
                        for u in units_at(i, par, 4) + (units_at(i, par, 3) if early else []):
                            split_w_hi(u)

            turns(turn, act.Fori)
            pad_lists(act, range(E // 2, E))
            nc.scalar.activation(nb[:, 0, 0:1], c32[:, C_HALF:C_HALF + 1], ACT.Gelu_apprx_tanh)

            act.wait_ge(s.sched_done, 2)
            act.wait_ge(s.b1T_done, 1)
            act.wait_ge(s.o_norm, NT)

            def copy_rows(t, par):
                act.wait_ge(s.xT_ps_d, t + 1)
                wait(act, s.h_ps_d, 2 * (t - 1))
                nc.scalar.copy(xT[par], xT_ps[par]).then_inc(s.xT_done, 1)

            def gelu_block(t, e, par):
                for m in range(2):
                    act.wait_ge(s.h_ps_d, 2 * t + m + 1)
                    wait(act, s.hh_lo, 2 * (t - 1))
                    for f in range(4):
                        c = 4 * m + f
                        last = nc.scalar.activation(h32[par][:, c * P:(c + 1) * P], h_ps[par][m][:, f * P:(f + 1) * P],
                                                    ACT.Gelu_apprx_tanh, bias=b1T[:, ds(e * FC + c, 1)], scale=1.0 / (SX * SW))
                    last.then_inc(s.h_done, 1)

            def step(t, slot, e):
                if not isinstance(t, int) or t + 2 < NBLK:
                    copy_rows(t + 2, slot % 2)
                if not isinstance(t, int) or 0 <= t + 1 < NBLK:
                    gelu_block(t + 1, e[1], 1 - slot % 2)

            blocks(step, act, -2, 1)

        @block.vector
        def _(dve):
            def split(dst, src, scale, inc=None):
                dve.tensor_scalar(dst(0), src, scale, None, ALU.mult).then_inc(s.wsplit_hi, 1)
                count[0] += 1
                dve.wait_ge(s.wsplit_hi, count[0])
                dve.scalar_tensor_tensor(out=dst(1), in0=src, scalar=scale, in1=dst(0), op0=ALU.mult,
                                         op1=ALU.subtract).then_inc(s.wsplit, 1)

            count = [0]
            dve.memset(wka.bitcast(u32), 0).then_inc(s.z_set, 1)
            dve.memset(wqa.bitcast(u32), 0).then_inc(s.z_set, 1)
            dve.memset(probs[:, FLAT:NC * P], 0.0).then_inc(s.z_set, 1)
            dve.wait_ge(s.z_set, 3)
            dve.wait_ge(s.w_in, 64)
            for c in range(DC):
                split(lambda w: wka[:, w, c, :, 0:DH], wkv_raw[:, c, 0:D].rearrange("p (h d) -> p h d", h=H), SW)
            for c in range(DC):
                split(lambda w: wva[:, w, c, :], wkv_raw[:, c, D:2 * D], SW)
            dve.wait_ge(s.ctxT_ps, 1)
            for c in range(DC):
                for b in range(B):
                    src = ps[:, 2 * c + b, 0:NK].unsqueeze(1).to_broadcast([P, 2, NK])
                    split(lambda w: ctxT[:, w, c, b, :].rearrange("p (r k) -> p r k", r=2), src, SCTX)
            dve.wait_ge(s.bias_in, 16 * BIASES)
            for n in range(DC + 1):
                src = wkv_raw[:, n, 0:D] if n < DC else bk_bc
                dve.tensor_tensor(prod, src, bq_bc, ALU.mult).then_inc(s.k_fold, 1)
                dve.wait_ge(s.k_fold, 2 * n + 1)
                dve.tensor_reduce(rec[:], prod.rearrange("p (h d) -> p h d", h=H), AX.X, ALU.add).then_inc(s.k_fold, 1)
                dve.wait_ge(s.k_fold, 2 * n + 2)
                if n < DC:
                    split(lambda w: wka[:, w, n, :, DH], rec[:], S_ROW * SCALE * SW / SK)
                    dve.wait_ge(s.wsplit, count[0])
            dve.tensor_tensor(prod[:, 0:H].rearrange("p (g j) -> p g j", g=G), rec[:].rearrange("p (g j) -> p g j", g=G),
                              c32[:, C_ROW:C_ROW + HG].unsqueeze(1).to_broadcast([P, G, HG]), ALU.mult).then_inc(s.k_fold, 1)
            dve.wait_ge(s.k_fold, 2 * DC + 3)
            dve.tensor_reduce(fold[:], prod[:, 0:H].rearrange("p (g j) -> p g j", g=G), AX.X, ALU.add).then_inc(s.k_fold, 1)
            dve.wait_ge(s.z_bias, 1)
            dve.tensor_scalar(kbias[:], kbias[:], SK, None, ALU.mult).then_inc(s.k_fold, 1)
            dve.wait_ge(s.k_fold, 2 * DC + 5)
            dve.scalar_tensor_tensor(out=kbias[:], in0=fold[:], scalar=S_ROW * SCALE, in1=kbias[:], op0=ALU.mult,
                                     op1=ALU.add).then_inc(s.k_fold, 1)
            split(lambda w: bvr[0:1, w * D:(w + 1) * D], bvf[0:1, :], 2.0**7)
            for c in range(DC):
                split(lambda w: wqa[:, w, c, :, 0:DH], wq_raw[:, c, :].rearrange("p (h d) -> p h d", h=H), SW)
            split(lambda w: wos[:, w, :, :], wo_raw, SW)
            split(lambda w: wgs[:, w, :, :], wg_raw, SW)
            dve.wait_ge(s.b1T_ps, 1)
            dve.tensor_copy(b1T[:], o_ps[:, 0:E * FC]).then_inc(s.b1T_done, 1)

            def k_slope(n):
                g = n % G
                dve.wait_ge(s.k_aff, n + 1)
                dve.scalar_tensor_tensor(out=k32[n % 3], in0=c32[:, C_KPOS:C_KPOS + NK], scalar=c32[:, C_SLOPE + g:C_SLOPE + g + 1],
                                         in1=k32[n % 3], op0=ALU.mult, op1=ALU.add).then_inc(s.k_row, 1)

            def k_low(n):
                b, g = n // G, n % G
                dve.wait_ge(s.k_hi, n + 1)
                for j in range(HG):
                    part, cols = slice(32 * j, 32 * j + 32), slice(j * NK, (j + 1) * NK)
                    last = dve.tensor_tensor(kbd[part, 1, b, g, cols], k32[n % 3][part, :], kbd[part, 0, b, g, cols], ALU.subtract)
                last.then_inc(s.k_lo, 1)

            for n in range(2):
                k_slope(n)
            for n in range(B * G):
                k_low(n)
                if n + 2 < B * G:
                    k_slope(n + 2)
            def split_values():
                mask = c32[:, C_MASK:C_MASK + 2 * NC].rearrange("p (c m) -> p c m", m=2)
                dve.tensor_copy(vs[:, 0, :, :, :, DH], mask.unsqueeze(1).to_broadcast([P, B, NC, 2]))
                dve.memset(vs[:, 1, :, :, :, DH], 0.0)
                def v_low(n):
                    vm, place = v_parts(n)
                    dve.wait_ge(s.v_hi, n + 1)
                    dve.tensor_tensor(place(1), vm, place(0), ALU.subtract).then_inc(s.v_done, 1)

                for n in range(2 * B):
                    chunks = slice((n % 2) * (NC // 2) * 2, (n % 2 + 1) * (NC // 2) * 2)
                    flat = lambda v: v.rearrange("p (k d) -> p k d", d=DH)
                    dve.wait_ge(s.v_ps, n // 2 + 1)
                    wait(dve, s.v_done, n - 1)
                    dve.scalar_tensor_tensor(out=flat(v32)[:, chunks], in0=flat(ps[:, v_bank(n // 2, n % 2), 0:(NC // 2) * 32]),
                                             scalar=S_V / (SCTX * SW),
                                             in1=c32[:, C_MASK:C_MASK + 2 * NC][:, chunks].unsqueeze(2).to_broadcast([P, NC, DH]),
                                             op0=ALU.mult, op1=ALU.mult).then_inc(s.v_mask, 1)
                    if n > 0:
                        v_low(n - 1)
                v_low(2 * B - 1)

            def pt_lo(i, v, par):
                dve.wait_ge(s.pt_hi, i * NU + v + 1)
                dve.tensor_tensor(pt[:, v, 1, :], pt_ps[(v + par) % 2], pt[:, v, 0, :], ALU.subtract).then_inc(s.pt_lo, 1)

            def split_w_lo(i, par, slot):
                for u in units_at(i, par, slot):
                    if not u.pool:
                        dve.wait_ge(s.w_hi, u.u + 1)
                        dve.scalar_tensor_tensor(out=unit_place(u, 1), in0=staged(u), scalar=SW, in1=unit_place(u, 0),
                                                 op0=ALU.mult, op1=ALU.subtract).then_inc(S[f"w_lo{u.n}"], 2)

            def maxima(i, g):
                two_banks = score_ps[g % 2]
                dve.wait_ge(s.s_ps, i * G + g + 1)
                dve.tensor_reduce(mx[:, g, :], two_banks[:, :, 0:PAIR].rearrange("p a (j k) -> p a j k", j=2), AX.X, ALU.max).then_inc(s.mx_d, 1)

            def exp_bias(i, g):
                dve.wait_ge(s.mx_d, i * G + g + 1)
                dve.tensor_scalar(nb[:, g, :], mx[:, g, :], -1.0 / S_SCORE, math.log(S_P), ALU.mult, ALU.add).then_inc(s.nb_d, 1)

            def turn(i, par):
                f1, f2, sc, mt, b1, b2, b3 = stages(i)
                p1, p2 = 1 - par, par
                if b2 is not None:
                    dve.wait_ge(s.pr_ps, b2 + 1)
                    dve.wait_ge(s.xb_bo, b2 + 1)
                    dve.scalar_tensor_tensor(out=xb[:, p2, :], in0=misc[:, 0:D], scalar=1.0 / (S_V * SW), in1=xb[:, p2, :],
                                             op0=ALU.mult, op1=ALU.add).then_inc(s.x2_done, 1)
                if mt is not None:
                    pt_lo(mt, 0, par)
                if sc is not None:
                    maxima(sc, 0)
                if sc is not None:
                    exp_bias(sc, 0)
                if b3 is not None:
                    dve.wait_ge(s.lg_ps, b3 + 1)
                    dve.scalar_tensor_tensor(out=lg[:], in0=misc[:, 0:E], scalar=1.0 / (SX * SW), in1=bg_bc[:], op0=ALU.mult,
                                             op1=ALU.add).then_inc(s.lg_d, 1)
                if b3 is not None:
                    wait_alone(dve, s.lg_d, b3 + 1)
                    wait_alone(dve, s.e8_d, b3)
                    dve.max(m8[:], lg[:]).then_inc(s.m8_d, 1)
                if b2 is not None:
                    dve.wait_ge(s.x2_done, b2 + 1)
                    dve.bn_stats(st2[:], xb[:, p2, :]).then_inc(s.st2_d, 1)
                if b3 is not None:
                    wait_alone(dve, s.m8_d, b3 + 1)
                    wait_alone(dve, s.tail_d, 3 * b3)
                    dve.max_index(mi[:], m8[:], lg[:]).then_inc(s.mi_d, 1)
                    dve.tensor_scalar(small[:, 0:1], m8[:, 0:1], -1.0, None, ALU.mult).then_inc(s.nm_d, 1)
                if mt is not None:
                    pt_lo(mt, 1, par)
                if b2 is not None:
                    wait_alone(dve, s.st2_d, b2 + 1)
                    dve.bn_aggr(mv2[:], st2[:]).then_inc(s.mv2_d, 1)
                if sc is not None:
                    maxima(sc, 1)
                if b3 is not None:
                    dve.wait_ge(s.mi_d, b3 + 1)
                    dve.tensor_tensor(oh[:], c32[:, C_IOTA:C_IOTA + E].unsqueeze(1).to_broadcast([P, 2, E]),
                                      mi[:, 0:2].unsqueeze(2).to_broadcast([P, 2, E]), ALU.is_equal).then_inc(s.oh_d, 1)
                if sc is not None:
                    exp_bias(sc, 1)
                if b2 is not None:
                    dve.wait_ge(s.mv2_d, b2 + 1)
                    dve.tensor_scalar(rs2[:, 0:1], mv2[:, 1:2], EPS, 1.0 / (SX * SX), ALU.add, ALU.mult).then_inc(s.ve2_d, 1)
                if b3 is not None:
                    dve.wait_ge(s.oh_d, b3 + 1)
                    wait(dve, s.rk_ps, b3)
                    dve.tensor_tensor(sel[:], oh[:, 0, :], oh[:, 1, :], ALU.add).then_inc(s.sel_d, 1)
                if b1 is not None:
                    dve.wait_ge(s.oT_hi, b1 + 1)
                    dve.tensor_tensor(oT[:, 1, :], misc[:, 0:D], oT[:, 0, :], ALU.subtract).then_inc(s.oT_lo, 1)
                if mt is not None:
                    pt_lo(mt, 2, par)
                if b3 is not None:
                    dve.wait_ge(s.sel_d, b3 + 1)
                    dve.tensor_tensor(cum[:, p2, :], cum[:, p1, :], sel[:], ALU.add).then_inc(s.cum_d, 1)
                if sc is not None:
                    maxima(sc, 2)
                if f1 is not None:
                    dve.wait_ge(S[f"x_in{p1}"], per_tile(f1, p1, 16) + 16)
                    dve.bn_stats(st1[:], xa[:, p1, :]).then_inc(s.st1_d, 1)
                if sc is not None:
                    exp_bias(sc, 2)
                if f2 is not None:
                    dve.wait_ge(s.xnT_hi, f2 + 1)
                    dve.tensor_tensor(xnT[:, 1, :], misc[:, 0:D], xnT[:, 0, :], ALU.subtract).then_inc(s.xnT_lo, 1)
                if b3 is not None:
                    dve.wait_ge(s.rk_ps, b3 + 1)
                    dve.wait_ge(s.xnT_hi, upto(i + 2))
                    dve.tensor_tensor(ohr[:], oh[:], misc[:, D:D + E].unsqueeze(1).to_broadcast([P, 2, E]), ALU.mult).then_inc(s.ohr_d, 1)
                if b2 is not None:
                    dve.wait_ge(s.rstd2, b2 + 1)
                    wait(dve, s.xs_lo, b2)
                    dve.tensor_scalar(xn2[:], xb[:, p2, :], mv2[:, 0:1], rs2[:, 1:2], ALU.subtract, ALU.mult).then_inc(s.xn2_done, 1)
                if f1 is not None:
                    wait_alone(dve, s.st1_d, f1 + 1)
                    dve.bn_aggr(mv1[:], st1[:]).then_inc(s.mv1_d, 1)
                if f1 is not None:
                    dve.wait_ge(s.mv1_d, f1 + 1)
                    dve.tensor_scalar(rs1[:, 0:1], mv1[:, 1:2], EPS, 1.0 / (SX * SX), ALU.add, ALU.mult).then_inc(s.ve1_d, 1)
                if mt is not None:
                    pt_lo(mt, 3, par)
                if b3 is not None:
                    dve.wait_ge(s.ohr_d, b3 + 1)
                    wait(dve, S[f"scat{p1}"], per_tile(b3, p1, 32))
                    with nc.allow_low_precision(reason="whole numbers below 2^24"):
                        dve.tensor_reduce(pos[:, p1, :], ohr[:], AX.X, ALU.add).then_inc(s.pos_d, 1)
                if sc is not None:
                    maxima(sc, 3)
                if isinstance(i, int) and i == -2:
                    split_values()
                if f1 is not None:
                    dve.wait_ge(s.rstd1, f1 + 1)
                    wait(dve, s.xnT_ps, f1)
                    dve.tensor_scalar(xn, xa[:, p1, :], mv1[:, 0:1], rs1[:, 1:2], ALU.subtract, ALU.mult).then_inc(s.xn_done, 1)
                if sc is not None:
                    exp_bias(sc, 3)
                if mt is not None:
                    pt_lo(mt, 4, par)
                if f2 is not None:
                    dve.wait_ge(s.q_hi, f2 + 1)
                    dve.scalar_tensor_tensor(out=qs[:, par, 1, :], in0=misc, scalar=SQ / (SX * SW), in1=qs[:, par, 0, :],
                                             op0=ALU.mult, op1=ALU.subtract).then_inc(s.q_lo, 1)
                if mt is not None:
                    dve.wait_ge(s.m_done, NU * (mt + 1))
                    ov = o_ps[:, 0:H * DV].rearrange("p (h d) -> p h d", h=H)
                    dve.reciprocal(rec[:], ov[:, :, DH]).then_inc(s.rec_d, 1)
                    dve.wait_ge(s.rec_d, mt + 1)
                    wait(dve, s.oT_ps, mt)
                    dve.tensor_tensor(o32[:].rearrange("p (h d) -> p h d", h=H), ov[:, :, 0:DH],
                                      rec[:].unsqueeze(2).to_broadcast([P, H, DH]), ALU.mult).then_inc(s.o_norm, 1)
                split_w_lo(i, par, 3)
                split_w_lo(i, par, 4)

            dve.wait_ge(s.z_cum, 1)
            turns(turn, dve.Fori)

            n_sched = [0]

            def then(ins):
                n_sched[0] += 1
                ins.then_inc(s.sched, 1)
                dve.wait_ge(s.sched, n_sched[0])

            dve.wait_ge(s.cnt_ps, 1)
            then(dve.tensor_copy(cnt_i[:, 0, :], misc[:, 0:E]))
            dve.tensor_scalar(cnt_f[:, 0, :], misc[:, 0:E], float(P - 1), None, ALU.add).then_inc(s.n_done, 1)
            dve.wait_ge(s.n_done, 1)
            then(dve.tensor_copy(cnt_i[:, 1, :], cnt_f[:, 0, :]))
            then(dve.tensor_single_scalar(cnt_i[:, 2, :], cnt_i[:, 1, :], 7, ALU.arith_shift_right))
            then(dve.tensor_copy(cnt_f[:, 1, :], cnt_i[:, 2, :]))
            sums = probs[:, 0:E * E].rearrange("p (e f) -> p e f", e=E)
            then(dve.tensor_tensor(sums, c32[:, C_LE:C_LE + E * E].rearrange("p (e f) -> p e f", e=E),
                                   cnt_f[:, 1, :].unsqueeze(1).to_broadcast([P, E, E]), ALU.mult))
            then(dve.tensor_reduce(cnt_f[:, 2, :], sums, AX.X, ALU.add))
            then(dve.tensor_scalar(cnt_f[:, 3, :], cnt_f[:, 1, :], -float(P), float(LIST), ALU.mult, ALU.add))
            blk = c32[:, C_BLK:C_BLK + NBLK]
            expert, gained = sched_f[:, 1, 0:NBLK], sched_f[:, 0, 0:NBLK]
            ended, gains = (probs[:, (n + 1) * 512:(n + 1) * 512 + NBLK * E].rearrange("p (b e) -> p b e", e=E) for n in range(2))
            then(dve.tensor_tensor(ended, blk.unsqueeze(2).to_broadcast([P, NBLK, E]),
                                   cnt_f[:, 2, :].unsqueeze(1).to_broadcast([P, NBLK, E]), ALU.is_ge))
            then(dve.tensor_tensor(gains, ended, cnt_f[:, 3, :].unsqueeze(1).to_broadcast([P, NBLK, E]), ALU.mult))
            then(dve.tensor_reduce(gained, gains, AX.X, ALU.add))
            dve.scalar_tensor_tensor(out=sched_i[0:1, 0, 0:NBLK], in0=blk[0:1, :], scalar=float(P), in1=gained[0:1, :],
                                     op0=ALU.mult, op1=ALU.add).then_inc(s.sched_done, 1)
            then(dve.tensor_reduce(expert, ended, AX.X, ALU.add))
            then(dve.tensor_scalar(expert, expert, float(E - 1), None, ALU.min))
            dve.tensor_copy(sched_i[0:1, 1, 0:NBLK], expert[0:1, :]).then_inc(s.sched_done, 1)
            dve.wait_ge(s.b2_in, 16)
            dve.wait_ge(s.sched_done, 2)

            def split_h(t, m, par):
                cols = slice(m * 512, (m + 1) * 512)
                dve.wait_ge(s.h_done, 2 * t + m + 1)
                wait(dve, s.y_ps_d, t - 1)
                dve.tensor_scalar(hh[par][:, 0, cols], h32[par][:, cols], S_H, None, ALU.mult).then_inc(s.hh_hi, 1)
                dve.wait_ge(s.hh_hi, 2 * t + m + 1)
                dve.scalar_tensor_tensor(out=hh[par][:, 1, cols], in0=h32[par][:, cols], scalar=S_H, in1=hh[par][:, 0, cols],
                                         op0=ALU.mult, op1=ALU.subtract).then_inc(s.hh_lo, 1)

            def extract(t, slot):
                dve.wait_ge(S[f"xt_in{slot}"], per_block(t, slot) + 16)
                wait(dve, s.y_done, t - 3)
                dve.scalar_tensor_tensor(out=wsel[:, slot, 0:1], in0=pay[slot][:, 1:2], scalar=sched_f[:, 1, ds(t, 1)],
                                         in1=pay[slot][:, 2:3], op0=ALU.is_equal, op1=ALU.mult).then_inc(s.wa_d, 1)
                wait(dve, s.added, 16 * (t - 3))
                dve.tensor_copy(row_id[:, slot:slot + 1], pay[slot][:, 0:1].bitcast(i32)).then_inc(s.wb_d, 1)
                dve.wait_ge(s.wa_d, t + 1)
                dve.tensor_tensor(wsel[:, slot, 1:2], wsel[:, slot, 0:1], pay[slot][:, 3:4], ALU.add).then_inc(s.ex_d, 1)

            def weigh(t, e, slot):
                par = slot % 2
                dve.wait_ge(s.y_ps_d, t + 1)
                wait(dve, s.added, 16 * (t - 1))
                dve.scalar_tensor_tensor(out=ysb[par][:], in0=y_ps[par][:, 0:D], scalar=1.0 / (S_H * SW), in1=b2bc[:, ds(e * D, D)],
                                         op0=ALU.mult, op1=ALU.add).then_inc(s.yb_d, 1)
                dve.wait_ge(s.yb_d, 2 * t + 1)
                dve.scalar_tensor_tensor(out=ysb[par][:], in0=y_ps[par][:, D:2 * D], scalar=1.0 / (S_H * SW), in1=ysb[par][:],
                                         op0=ALU.mult, op1=ALU.add).then_inc(s.yb_d, 1)
                dve.wait_ge(s.yb_d, 2 * t + 2)
                dve.wait_ge(s.ex_d, t + 1)
                dve.tensor_scalar(ysb[par][:], ysb[par][:], wsel[:, slot, 1:2], None, ALU.mult).then_inc(s.y_done, 1)

            def step(t, slot, e):
                ahead = not isinstance(t, int) or 0 <= t + 1 < NBLK
                if ahead:
                    split_h(t + 1, 0, 1 - slot % 2)
                if not isinstance(t, int) or t + 2 < NBLK:
                    extract(t + 2, (slot + 2) % 4)
                if not isinstance(t, int) or t >= 0:
                    weigh(t, e[0], slot)
                if ahead:
                    split_h(t + 1, 1, 1 - slot % 2)

            blocks(step, dve, -2, 0)

        @block.tensor
        def _(pe):
            def mm(out_, lhsT, rhs, start, stop, skip=False):
                return nc.tensor.matmul(out_, lhsT, rhs, start=start, stop=stop, skip_group_check=skip)

            THREE = ((0, 0), (0, 1), (1, 0))
            pe.wait_ge(s.c_in, 48)
            pe.wait_ge(s.ctx_in, 32)
            for c in range(DC):
                for b in range(B):
                    cols = slice(c * P, (c + 1) * P)
                    nc.tensor.transpose(ps[:, 2 * c + b, 0:P], ctx_main[:, b, cols], ident)
                    last = nc.tensor.transpose(ps[:, 2 * c + b, P:NK], ctx_tail[:, b, cols], ident[0:NK - P, 0:NK - P])
            last.then_inc(s.ctxT_ps, 1)
            pe.wait_ge(s.bias_in, 16 * BIASES)
            nc.tensor.transpose(o_ps[:, 0:E * FC], b1_raw, ident[0:E * FC, 0:E * FC]).then_inc(s.b1T_ps, 1)
            def values(b):
                for ch in range(NC):
                    k0, h0 = ch * P % NK, ch * P // NK
                    o = (ch % (NC // 2)) * 32
                    bank = ps[:, v_bank(b, ch // (NC // 2)), :]
                    for o, w in ((o, 32),) if h0 + 1 < H else ((o, DH), (o + DH, DH)):
                        for c in range(DC):
                            for a, z in THREE:
                                mm(bank[:, o:o + w], ctxT[:, a, c, b, k0:k0 + P], wva[:, z, c, h0 * DH:h0 * DH + w],
                                   c == 0 and (a, z) == (0, 0), False)
                        for z in range(2):
                            last = mm(bank[:, o:o + w], c16[0:1, H_BV:H_BV + P],
                                      bvr[0:1, z * D + h0 * DH:z * D + h0 * DH + w], False, z == 1)
                last.then_inc(s.v_ps, 1)

            def keys(n):
                b, g = n // G, n % G
                dst = k_bank[n % 2]
                wait(pe, s.k_aff, n - 1)
                for c in range(DC):
                    for a, z in THREE:
                        last = mm(dst[:, 0:NK], wka[:, a, c, g * HG:(g + 1) * HG, :].rearrange("p h d -> p (h d)"),
                                  ctxT[:, z, c, b, 0:NK], c == 0 and (a, z) == (0, 0), c == 1 and (a, z) == (1, 0))
                last.then_inc(s.k_ps, 1)

            pe.wait_ge(s.wsplit, 10)
            for n in range(2):
                keys(n)
            pe.wait_ge(s.wsplit, 11)
            values(0)
            for n in range(2, B * G):
                keys(n)
            values(1)

            def transposes(i, v, par):
                pe.wait_ge(s.p_done, i * G + group_of_unit(v) + 1)
                wait(pe, s.pt_lo, i * NU + v - 1)
                for n in range(4):
                    c = 4 * v + n
                    last = nc.tensor.transpose(pt_ps[(v + par) % 2][:, n * P:(n + 1) * P], probs[:, c * P:(c + 1) * P], ident)
                last.then_inc(s.t_ps, 1)

            def scores(i, g, par):
                pe.wait_ge(s.q_lo, i + 1)
                wait(pe, s.p_done, i * G + g - 1)
                late = isinstance(i, int) and i >= NT - 4
                tail = i // 2 - (NT // 2 - 2) if late else 0
                if late:
                    pe.wait_ge(s.kink_in, 16)
                for n in range(2):
                    for a, z in THREE:
                        last = mm(score_ps[g % 2][:, n, 0:PAIR], qs[:, par, a, g * P:(g + 1) * P],
                                  kbd[:, z, par, g, n * PAIR:(n + 1) * PAIR], (a, z) == (0, 0), (a, z) == (1, 0))
                        if late and (a, z) == (0, 0):
                            j = 2 * g + n
                            key = kinks[:, 6 * P + (4 * tail + j % 4) * NK:6 * P + (4 * tail + j % 4 + 1) * NK]
                            for k, head in ((0, 0), (1, 0), (2, 1)):
                                diagonal = kinks[:, (2 * k + j // 4) * P:(2 * k + j // 4 + 1) * P]
                                mm(score_ps[g % 2][:, n, head * NK:(head + 1) * NK], diagonal, key, False, False, True)
                last.then_inc(s.s_ps, 1)

            def mix(i, v, par):
                pe.wait_ge(s.pt_lo, i * NU + v + 1)
                if v == 0:
                    wait(pe, s.o_norm, i)
                for n in range(4):
                    c = 4 * v + n
                    h0 = c * P // NK
                    two = (c * P + P - 1) // NK > h0 and h0 + 1 < H
                    w = 2 * DV if two else DV
                    for a, z in THREE:
                        last = mm(o_ps[:, h0 * DV:h0 * DV + w], pt[:, v, a, n * P:(n + 1) * P],
                                  vs[:, z, par, c, :, :].rearrange("p h d -> p (h d)")[:, 0:w],
                                  c == 0 and (a, z) == (0, 0), c == NC - 1 and (a, z) == (1, 0), True)
                last.then_inc(s.m_done, 1)

            def turn(i, par):
                f1, f2, sc, mt, b1, b2, b3 = stages(i)
                q = 1 - par
                if sc is not None:
                    scores(sc, 0, q)
                if mt is not None:
                    transposes(mt, 1, par)
                wait(pe, s.x2_done, upto(i - 2))
                if isinstance(i, int):
                    wait(pe, s.q_lo, min(i + 2, NT))
                if b3 is not None:
                    pe.wait_ge(s.x2T_done, b3 + 1)
                    for c in range(DC):
                        for a, z in THREE:
                            last = mm(misc[:, 0:E], x2T[:, (2 * a + c) * P:(2 * a + c + 1) * P], wgs[:, z, c, :],
                                      c == 0 and (a, z) == (0, 0), c == 1 and (a, z) == (1, 0))
                    last.then_inc(s.lg_ps, 1)
                if sc is not None:
                    scores(sc, 1, q)
                if mt is not None:
                    transposes(mt, 2, par)
                if b1 is not None:
                    pe.wait_ge(s.o_norm, b1 + 1)
                    wait(pe, s.lg_d, b3 + 1 if b3 is not None else 0)
                    for c in range(DC):
                        last = nc.tensor.transpose(misc[:, c * P:(c + 1) * P], o32[:, c * P:(c + 1) * P], ident)
                    last.then_inc(s.oT_ps, 1)
                if mt is not None:
                    mix(mt, 0, par)
                if sc is not None:
                    scores(sc, 2, q)
                if mt is not None:
                    transposes(mt, 3, par)
                if mt is not None:
                    mix(mt, 1, par)
                if b3 is not None:
                    pe.wait_ge(s.sel_d, b3 + 1)
                    wait(pe, s.cum_d, b3)
                    wait(pe, s.lg_d, b3 + 1)
                if b1 is not None:
                    pe.wait_ge(s.oT_lo, b1 + 1)
                if b3 is not None:
                    mm(misc[:, D:D + E], tri16, sel[:], True, False)
                    mm(misc[:, D:D + E], one16, cum[:, q, :], False, False)
                    mm(misc[:, D:D + E], one16[0:1, :], c16[0:1, H_BASE:H_BASE + E], False, True).then_inc(s.rk_ps, 1)
                if f2 is not None:
                    pe.wait_ge(s.xn_done, f2 + 1)
                    for c in range(DC):
                        last = nc.tensor.transpose(misc[:, c * P:(c + 1) * P], xn[:, c * P:(c + 1) * P], ident)
                    last.then_inc(s.xnT_ps, 1)
                if sc is not None:
                    scores(sc, 3, q)
                if mt is not None:
                    transposes(mt, 4, par)
                if mt is not None:
                    mix(mt, 2, par)
                if f2 is not None:
                    pe.wait_ge(s.xnT_lo, f2 + 1)
                    if b3 is not None:
                        pe.wait_ge(s.ohr_d, b3 + 1)
                    for g in range(G):
                        for c in range(DC):
                            for a, z in THREE:
                                mm(misc[:, g * P:(g + 1) * P],
                                   wqa[:, a, c, g * HG:(g + 1) * HG, :].rearrange("p h d -> p (h d)"),
                                   xnT[:, z, c * P:(c + 1) * P], c == 0 and (a, z) == (0, 0), False)
                        last = mm(misc[:, g * P:(g + 1) * P], c16[0:1, H_ROW:H_ROW + P], c16[0:1, H_BV:H_BV + P], False, True)
                    last.then_inc(s.q_ps, 1)
                if sc is not None:
                    transposes(sc, 0, q)
                if mt is not None:
                    mix(mt, 3, par)
                    mix(mt, 4, par)
                if b3 is not None:
                    wait(pe, s.ohr_d, b3 + 1)
                if b1 is not None or b2 is not None:
                    wait(pe, s.q_lo, upto(i + 2))
                if b2 is not None:
                    pe.wait_ge(s.xs_lo, b2 + 1)
                    for n in range(4):
                        last = nc.tensor.transpose(misc16[:, 2 * D + n * P:2 * D + (n + 1) * P], rows[:, par, n * P:(n + 1) * P], ident16)
                    last.then_inc(s.x2T_ps, 1)
                if b1 is not None:
                    pe.wait_ge(s.oT_lo, b1 + 1)
                    for c in range(DC):
                        for a, z in THREE:
                            last = mm(misc[:, 0:D], oT[:, a, c * P:(c + 1) * P], wos[:, z, c, :],
                                      c == 0 and (a, z) == (0, 0), c == 1 and (a, z) == (1, 0))
                    last.then_inc(s.pr_ps, 1)

            pe.wait_ge(s.wsplit, 15)
            pe.wait_ge(s.b1T_done, 1)
            pe.wait_ge(s.k_aff, B * G)
            turn(-2, 0)
            pe.wait_ge(s.k_lo, B * G)
            pe.wait_ge(s.v_done, 2 * B)
            pe.wait_ge(s.z_cum, 1)
            turns(turn, pe.Fori, -1)
            pe.wait_ge(s.cum_d, NT)
            mm(misc[:, 0:E], one16, cum[:, 0, :], True, True).then_inc(s.cnt_ps, 1)

            pe.wait_ge(s.sched_done, 2)

            def turn_rows(t, slot):
                pe.wait_ge(S[f"xt_in{slot}"], per_block(t, slot) + 16)
                wait(pe, s.xT_done, t - 1)
                for n in range(4):
                    last = nc.tensor.transpose(xT_ps[slot % 2][:, n * P:(n + 1) * P], xt[slot][:, n * P:(n + 1) * P], ident16)
                last.then_inc(s.xT_ps_d, 1)

            def up(t, f, w1e, par):
                m = f // 4
                if f == 0:
                    pe.wait_ge(s.xT_done, t + 1)
                    wait(pe, s.h_done, 2 * (t - 1))
                for c in range(DC):
                    for a, z in THREE:
                        last = mm(h_ps[par][m][:, (f % 4) * P:(f % 4 + 1) * P], w1e[:, a, c * F + f * P:c * F + (f + 1) * P],
                                  xT[par][:, (2 * z + c) * P:(2 * z + c + 1) * P],
                                  c == 0 and (a, z) == (0, 0), c == 1 and (a, z) == (1, 0))
                if f % 4 == 3:
                    last.then_inc(s.h_ps_d, 1)

            def down(t, c, w2e, par):
                if c == 0:
                    wait(pe, s.yb_d, 2 * (t - 1))
                if c % 4 == 0:
                    pe.wait_ge(s.hh_lo, 2 * t + c // 4 + 1)
                mm(y_ps[par], hh[par][:, 0, c * P:(c + 1) * P], w2e[:, 2 * c * D:2 * (c + 1) * D], c == 0, False)
                last = mm(y_ps[par][:, 0:D], hh[par][:, 1, c * P:(c + 1) * P], w2e[:, 2 * c * D:(2 * c + 1) * D], False, c == FC - 1)
                if c == FC - 1:
                    last.then_inc(s.y_ps_d, 1)

            pe.wait_ge(s.w_lo0, UNITS)
            pe.wait_ge(s.w_lo1, UNITS)
            def step(t, slot, e):
                if not isinstance(t, int) or t + 2 < NBLK:
                    turn_rows(t + 2, (slot + 2) % 4)
                ahead = not isinstance(t, int) or 0 <= t + 1 < NBLK
                here = not isinstance(t, int) or t >= 0
                if ahead:
                    w1e = wts[:, ds(e[1], 1), 0:2, :].rearrange("p o a k -> p (o a) k")
                if here:
                    w2e = wts[:, ds(e[0], 1), 2:4, :].rearrange("p o a k -> p (o a k)")
                for f in range(FC):
                    if ahead:
                        up(t + 1, f, w1e, 1 - slot % 2)
                    if here:
                        down(t, f, w2e, slot % 2)

            blocks(step, pe, -2, 1, 8)


_NAMES = ["x", "ctx_1024", "L0_xattn_Wq", "L0_xattn_bq", "L0_xattn_Wkv", "L0_xattn_bkv", "L0_xattn_Wo", "L0_xattn_bo",
          "L0_ffn_Wg", "L0_ffn_bg", "L0_ffn_W1", "L0_ffn_b1", "L0_ffn_W2", "L0_ffn_b2"]


def kernel(**inputs):
    import concourse.bacc as bacc
    from concourse.bass_utils import run_bass_kernel_spmd

    nc = bacc.Bacc("TRN2", target_bir_lowering=False, num_devices=1)
    arrays, args = {}, []
    c32, c16, kink, ids = constants()
    for name, a in [(n, np.ascontiguousarray(inputs[n])) for n in _NAMES] + [("c32", c32), ("c16", c16), ("kink", kink), ("ids", ids)]:
        arrays[f"in_{name}"] = a
        args.append(nc.dram_tensor(f"in_{name}", a.shape, mybir.dt.from_np(a.dtype), kind="ExternalInput").ap())
    args.append(nc.dram_tensor("out_0", (B, NQ, D), mybir.dt.float32, kind="ExternalOutput").ap())
    program(nc, *args)
    result = run_bass_kernel_spmd(nc, [arrays], core_ids=[0])
    return result.results[0]["out_0"]
```
